# Optimizing a Trainium2 kernel written in Bass

```python
import numpy as np
import jax
import jax.numpy as jnp

def _softmax(x, axis=-1):
    return jax.nn.softmax(x, axis=axis)

def _gelu(x):
    return jax.nn.gelu(x, approximate=True)

def _silu(x):
    return jax.nn.silu(x)

def _sigmoid(x):
    return jax.nn.sigmoid(x)

def _layernorm(x, axis=-1, eps=1e-05):
    m = jnp.mean(x, axis=axis, keepdims=True)
    v = jnp.var(x, axis=axis, keepdims=True)
    return (x - m) / jnp.sqrt(v + eps)

def _scatter_add(tgt, idx, src, axis=0):
    return tgt.at[idx].add(src)

def _segment_sum(src, seg, n):
    return jax.ops.segment_sum(src, seg, n)
kernel_name = 'mk_prb_d1_jaxref_r4_01472f'

def setup_inputs(seed: int=0):
    np.random.seed(seed)
    _w = jnp.asarray

    def _L0_attn_setup():
        import jax, jax.numpy as jnp
        import numpy as np
        import math
        HEADS = 16
        SEG = 64
        DIL = 4
        BLOCK_M = 64

        def _hilbert_points(level, x=0, y=0, xi=1, xj=0, yi=0, yj=1):
            if level <= 0:
                yield (x, y)
            else:
                for pt in _hilbert_points(level - 1, x, y, yi // 2, yj // 2, xi // 2, xj // 2):
                    yield pt
                for pt in _hilbert_points(level - 1, x + xi // 2, y + xj // 2, xi // 2, xj // 2, yi // 2, yj // 2):
                    yield pt
                for pt in _hilbert_points(level - 1, x + xi // 2 + yi // 2, y + xj // 2 + yj // 2, xi // 2, xj // 2, yi // 2, yj // 2):
                    yield pt
                for pt in _hilbert_points(level - 1, x + xi // 2 + yi, y + xj // 2 + yj, -yi // 2, -yj // 2, -xi // 2, -xj // 2):
                    yield pt

        def create_hilbert_mapping(seq_len):
            grid = 2 ** int(math.ceil(math.log2(math.sqrt(seq_len))))
            pts = list(_hilbert_points(int(math.log2(grid)), 0, 0, grid, 0, 0, grid))
            m = np.zeros(seq_len, dtype=np.int32)
            for hidx, (x, y) in enumerate(pts[:seq_len]):
                lin = y * grid + x
                if lin < seq_len:
                    m[lin] = hidx
            return jnp.asarray(m)

        def _hilbert_attention(x, Wqkv, bqkv, Wproj, bproj, mapping):
            B, M, dim = x.shape
            H = HEADS
            D = dim // H
            scale = D ** (-0.5)
            qkv = (x @ Wqkv + bqkv).reshape(B, M, 3, H, D)
            qkv = jnp.transpose(qkv, (2, 0, 3, 1, 4))
            q, k, v = (qkv[0], qkv[1], qkv[2])
            nb = M // BLOCK_M
            rm = jnp.arange(M).reshape(nb, BLOCK_M)
            mrm = mapping[rm].astype(jnp.int32)
            seg_idx = mrm // SEG
            offs = jnp.arange(0, SEG, DIL)
            key_pos = seg_idx[:, :, None] * SEG + offs[None, None, :]
            mask_k = key_pos < M
            kp0 = key_pos[:, 0, :]
            mask0 = mask_k[:, 0, :]
            idx0 = jnp.where(mask0, mapping[jnp.clip(kp0, 0, M - 1)], 0)
            Ksel = k[:, :, idx0, :] * mask0[None, None, :, :, None]
            Vsel = v[:, :, idx0, :] * mask0[None, None, :, :, None]
            qm = q[:, :, mrm, :] * scale
            scores = jnp.einsum('bhnmd,bhnsd->bhnms', qm, Ksel)
            scores = jnp.where(mask_k[None, None], scores, -1000000000.0)
            sexp = jnp.exp(scores - jnp.max(scores, axis=3, keepdims=True))
            acc = jnp.einsum('bhnms,bhnsd->bhnmd', sexp, Vsel)
            lsum = 1e-06 + jnp.sum(sexp, axis=-1)
            out = acc / lsum[..., None]
            out = out.reshape(B, H, M, D).transpose(0, 2, 1, 3).reshape(B, M, dim)
            return out @ Wproj + bproj
        key = jax.random.key(seed)
        ks = jax.random.split(key, 5)
        B, M, dim = (2, 1024, 256)
        s = 1.0 / math.sqrt(dim)
        return {'x': jax.random.normal(ks[0], (B, M, dim), jnp.float32), 'Wqkv': jax.random.normal(ks[1], (dim, 3 * dim), jnp.float32) * s, 'bqkv': jax.random.normal(ks[2], (3 * dim,), jnp.float32) * 0.01, 'Wproj': jax.random.normal(ks[3], (dim, dim), jnp.float32) * s, 'bproj': jax.random.normal(ks[4], (dim,), jnp.float32) * 0.01, 'mapping': create_hilbert_mapping(M)}
    _L0_attn_in = _L0_attn_setup()

    def _L0_ffn_setup():
        import jax, jax.numpy as jnp
        import numpy as np
        B, S, D, H, E = (4, 512, 256, 512, 8)
        key = jax.random.key(seed)
        ks = jax.random.split(key, 8)
        scale = 0.02
        return {'x': jax.random.normal(ks[0], (B, S, D), dtype=jnp.float32), 'Wr': jax.random.normal(ks[1], (D, E), dtype=jnp.float32) * scale, 'br': jnp.zeros((E,), dtype=jnp.float32), 'W1': jax.random.normal(ks[2], (E, D, H), dtype=jnp.float32) * scale, 'b1': jnp.zeros((E, H), dtype=jnp.float32), 'W2': jax.random.normal(ks[3], (E, H, D), dtype=jnp.float32) * scale, 'b2': jnp.zeros((E, D), dtype=jnp.float32)}
    _L0_ffn_in = _L0_ffn_setup()
    _d = {'L0_attn_x': _L0_attn_in['x'], 'L0_attn_Wqkv': _L0_attn_in['Wqkv'], 'L0_attn_bqkv': _L0_attn_in['bqkv'], 'L0_attn_Wproj': _L0_attn_in['Wproj'], 'L0_attn_bproj': _L0_attn_in['bproj'], 'L0_attn_mapping': _L0_attn_in['mapping'], 'L0_ffn_Wr': _L0_ffn_in['Wr'], 'L0_ffn_br': _L0_ffn_in['br'], 'L0_ffn_W1': _L0_ffn_in['W1'], 'L0_ffn_b1': _L0_ffn_in['b1'], 'L0_ffn_W2': _L0_ffn_in['W2'], 'L0_ffn_b2': _L0_ffn_in['b2']}
    _x0 = _d['L0_attn_x']
    _d['L0_attn_x'] = jax.random.normal(jax.random.fold_in(jax.random.key(seed), 1), (1, 4096, 256), dtype=_x0.dtype)
    del _x0
    return _d

def reference(L0_attn_x, L0_attn_Wqkv, L0_attn_bqkv, L0_attn_Wproj, L0_attn_bproj, L0_attn_mapping, L0_ffn_Wr, L0_ffn_br, L0_ffn_W1, L0_ffn_b1, L0_ffn_W2, L0_ffn_b2):

    def _L0_attn_ref(x, Wqkv, bqkv, Wproj, bproj, mapping):
        import jax, jax.numpy as jnp
        import numpy as np
        import math
        HEADS = 16
        SEG = 64
        DIL = 4
        BLOCK_M = 64

        def _hilbert_points(level, x=0, y=0, xi=1, xj=0, yi=0, yj=1):
            if level <= 0:
                yield (x, y)
            else:
                for pt in _hilbert_points(level - 1, x, y, yi // 2, yj // 2, xi // 2, xj // 2):
                    yield pt
                for pt in _hilbert_points(level - 1, x + xi // 2, y + xj // 2, xi // 2, xj // 2, yi // 2, yj // 2):
                    yield pt
                for pt in _hilbert_points(level - 1, x + xi // 2 + yi // 2, y + xj // 2 + yj // 2, xi // 2, xj // 2, yi // 2, yj // 2):
                    yield pt
                for pt in _hilbert_points(level - 1, x + xi // 2 + yi, y + xj // 2 + yj, -yi // 2, -yj // 2, -xi // 2, -xj // 2):
                    yield pt

        def create_hilbert_mapping(seq_len):
            grid = 2 ** int(math.ceil(math.log2(math.sqrt(seq_len))))
            pts = list(_hilbert_points(int(math.log2(grid)), 0, 0, grid, 0, 0, grid))
            m = np.zeros(seq_len, dtype=np.int32)
            for hidx, (x, y) in enumerate(pts[:seq_len]):
                lin = y * grid + x
                if lin < seq_len:
                    m[lin] = hidx
            return jnp.asarray(m)

        def _hilbert_attention(x, Wqkv, bqkv, Wproj, bproj, mapping):
            B, M, dim = x.shape
            H = HEADS
            D = dim // H
            scale = D ** (-0.5)
            qkv = (x @ Wqkv + bqkv).reshape(B, M, 3, H, D)
            qkv = jnp.transpose(qkv, (2, 0, 3, 1, 4))
            q, k, v = (qkv[0], qkv[1], qkv[2])
            nb = M // BLOCK_M
            rm = jnp.arange(M).reshape(nb, BLOCK_M)
            mrm = mapping[rm].astype(jnp.int32)
            seg_idx = mrm // SEG
            offs = jnp.arange(0, SEG, DIL)
            key_pos = seg_idx[:, :, None] * SEG + offs[None, None, :]
            mask_k = key_pos < M
            kp0 = key_pos[:, 0, :]
            mask0 = mask_k[:, 0, :]
            idx0 = jnp.where(mask0, mapping[jnp.clip(kp0, 0, M - 1)], 0)
            Ksel = k[:, :, idx0, :] * mask0[None, None, :, :, None]
            Vsel = v[:, :, idx0, :] * mask0[None, None, :, :, None]
            qm = q[:, :, mrm, :] * scale
            scores = jnp.einsum('bhnmd,bhnsd->bhnms', qm, Ksel)
            scores = jnp.where(mask_k[None, None], scores, -1000000000.0)
            sexp = jnp.exp(scores - jnp.max(scores, axis=3, keepdims=True))
            acc = jnp.einsum('bhnms,bhnsd->bhnmd', sexp, Vsel)
            lsum = 1e-06 + jnp.sum(sexp, axis=-1)
            out = acc / lsum[..., None]
            out = out.reshape(B, H, M, D).transpose(0, 2, 1, 3).reshape(B, M, dim)
            return out @ Wproj + bproj
        return _hilbert_attention(x, Wqkv, bqkv, Wproj, bproj, mapping)

    def _L0_ffn_ref(x, Wr, br, W1, b1, W2, b2):
        import jax, jax.numpy as jnp
        import numpy as np
        B, S, D, H, E = (4, 512, 256, 512, 8)
        d = x.shape[-1]
        tokens = x.reshape(-1, d)
        logits = tokens @ Wr + br
        probs = jax.nn.softmax(logits, axis=-1)
        expert = jnp.argmax(probs, axis=-1)
        max_prob = jnp.take_along_axis(probs, expert[:, None], axis=-1)
        h = jax.nn.relu(jnp.einsum('td,edh->teh', tokens, W1) + b1[None])
        y = jnp.einsum('teh,ehd->ted', h, W2) + b2[None]
        out = jnp.take_along_axis(y, expert[:, None, None], axis=1)[:, 0, :]
        return (out * max_prob).reshape(x.shape)
    x = L0_attn_x
    xn = _layernorm(x, axis=-1)
    x = x + _L0_attn_ref(xn, L0_attn_Wqkv, L0_attn_bqkv, L0_attn_Wproj, L0_attn_bproj, L0_attn_mapping) + _L0_ffn_ref(xn, L0_ffn_Wr, L0_ffn_br, L0_ffn_W1, L0_ffn_b1, L0_ffn_W2, L0_ffn_b2)
    return x

_drawn_inputs = setup_inputs


def setup_inputs(seed=0):
    import zlib

    import numpy as np

    out = dict(_drawn_inputs(seed))
    spreads = {'L0_ffn_br': (0.0, 0.359), 'L0_ffn_b1': (0.0, 0.8), 'L0_ffn_b2': (0.0, 0.415)}
    factors = {'L0_attn_bqkv': 5.065, 'L0_attn_bproj': 6.145, 'L0_ffn_W1': 3.397, 'L0_ffn_W2': 2.758}
    for name, (base, spread) in spreads.items():
        noise = np.random.default_rng([zlib.crc32(name.encode()), seed]).standard_normal(out[name].shape)
        drawn = base * np.exp(spread * noise) if base else spread * noise
        out[name] = jnp.asarray(drawn.astype(out[name].dtype))
    for name, factor in factors.items():
        out[name] = (out[name] * factor).astype(out[name].dtype)
    return out
```

```python
from contextlib import ExitStack

import concourse.bass as bass
from concourse import mybir

F32 = mybir.dt.float32
I32 = mybir.dt.int32
ALU = mybir.AluOpType
ACT = mybir.ActivationFunctionType
AX = mybir.AxisListType

P = 128
M, D = 4096, 256
SEQ = 1024
HEADS, HD = 16, 16
BLOCK, KEYS = 64, 16
SEG, DIL = 64, 4
SCALE = HD ** -0.5
NEXP, HID = 8, 512
LN_EPS, SUM_EPS = 1e-5, 1e-6

KD = D // P
KH = HID // P
NT = M // P
GT = 8
NG = NT // GT
NQT = SEQ // P
NKB = SEQ // BLOCK + 1
NKEY = NKB * KEYS
NKT = 3
LASTK = NKEY - 2 * P
NGT = NQT + NKT
HH = P // HD
VW = P + HH
MASKED = -1e9 / SCALE
NET = M // P + NEXP - 1
REG = M + P
XW = D + 2
SLOTS = 3


class Chain:

    def __init__(self, eng, sem):
        self.eng, self.sem, self.n = eng, sem, 0

    def then(self, ins):
        self.n = self.n + 1
        ins.then_inc(self.sem, 1)
        self.eng.wait_ge(self.sem, self.n)


def build(nc, x, wqkv, bqkv, wproj, bproj, mapping, wr, br, w1, b1, w2, b2, out):
    sent = nc.dram_tensor("sent_rows", (NEXP * REG + P, XW), F32, kind="Internal").ap()
    vals = nc.dram_tensor("value_rows", (NKEY, D), F32, kind="Internal").ap()
    zrows = nc.dram_tensor("residual_rows", (M, D), F32, kind="Internal").ap()
    x2 = x.rearrange("b m d -> (b m) d")
    out2 = out.rearrange("b m d -> (b m) d")

    with ExitStack() as ctx:
        ctx.enter_context(nc.allow_non_contiguous_dma(reason="short columns of the mapping and of biases"))

        def sb(name, shape, dt=F32):
            return ctx.enter_context(nc.sbuf_tensor(name, shape, dt))

        def sem(name):
            return ctx.enter_context(nc.semaphore(name))

        ident = sb("ident", [P, P])
        ones = sb("ones", [P, P])
        before = sb("before", [P, P])
        headmask = sb("headmask", [P, HH])
        headlow = sb("headlow", [P, HH])
        first_of = sb("first_of", [P, NEXP])
        restart = sb("restart", [P, NEXP, GT])
        minus_half = sb("minus_half", [P, NGT])
        region0 = sb("region0", [P, NEXP])
        key_step = sb("key_step", [P, 1], I32)
        part_i = sb("part_i", [P, 1], I32)
        first_i = sb("first_i", [P, NEXP], I32)
        region_i = sb("region_i", [P, NEXP], I32)
        code_i = sb("code_i", [P, NT], I32)
        tile_i = sb("tile_i", [P, NET], I32)
        code = sb("code", [P, NT])
        tile_no = sb("tile_no", [P, NET])
        wqkv_sb = sb("wqkv_sb", [P, KD, 3 * D])
        wproj_sb = sb("wproj_sb", [P, KD, D])
        wr_sb = sb("wr_sb", [P, KD, NEXP])
        w1_sb = sb("w1_sb", [P, NEXP, KD, HID])
        w2_sb = sb("w2_sb", [P, NEXP, KH, D])
        b1_bc = sb("b1_bc", [P, NEXP, HID])
        b2_bc = sb("b2_bc", [P, NEXP, D])
        bqk_col = sb("bqk_col", [P, 2 * KD])
        bv_bc = sb("bv_bc", [P, D])
        bproj_bc = sb("bproj_bc", [P, D])
        br_bc = sb("br_bc", [P, NEXP])

        x_sb = sb("x_sb", [P, NT, D])
        staging = sb("staging", [P, 2, GT * XW])
        xrow = [staging[:, i, :].rearrange("p (t w) -> p t w", t=GT) for i in range(2)]
        xT = sb("xT", [P, 2, KD, 4 * P])
        logT = sb("logT", [NEXP, 2, 4 * P])
        stats = sb("stats", [P, NGT, 6])
        mv = sb("mv", [P, NGT, 2])
        guess = sb("guess", [P, NGT])
        varp = sb("varp", [P, NGT])
        nt1 = sb("nt1", [P, NGT])
        nt2 = sb("nt2", [P, NGT])
        rstd = sb("rstd", [P, NGT])
        lg = sb("lg", [P, GT, NEXP])
        lgm = sb("lgm", [P, GT])
        lgd = sb("lgd", [P, GT, NEXP])
        lge = sb("lge", [P, GT, NEXP])
        lsum = sb("lsum", [P, GT])
        eqw = sb("eqw", [P, GT, NEXP])
        eqm = sb("eqm", [P, GT])
        onehot = sb("onehot", [P, NEXP, GT])
        rank = sb("rank", [P, NEXP, GT])
        cnt = sb("cnt", [P, NEXP])
        carry = sb("carry", [P, NEXP])
        offs = sb("offs", [P, NEXP])
        place = sb("place", [P, NEXP, GT])
        posf = sb("posf", [P, GT])
        pos = sb("pos", [P, NG, GT], I32)
        tab_i = sb("tab_i", [1, NEXP], I32)
        tab_n = sb("tab_n", [1, NEXP])
        tab_end = sb("tab_end", [1, NEXP])
        tab_start = sb("tab_start", [1, NEXP])
        tab_base = sb("tab_base", [1, NEXP])
        tab_e = sb("tab_e", [1, NET])
        tab_r = sb("tab_r", [1, NET])
        tab_u = sb("tab_u", [1, NET])
        tab_row = sb("tab_row", [1, NET], I32)
        tab_exp = sb("tab_exp", [1, NET], I32)
        pad_row = sb("pad_row", [1, NEXP], I32)
        map_q = sb("map_q", [P, NQT], I32)
        map_b = sb("map_b", [P, NKT], I32)
        idx_a = sb("idx_a", [P, NKT], I32)
        idx_k = sb("idx_k", [P, NKT], I32)
        map_k = sb("map_k", [P, NKT], I32)
        row_k = sb("row_k", [P, NKT], I32)
        row_q = sb("row_q", [P, NQT], I32)
        map_row = sb("map_row", [NQT, P], I32)
        masked = sb("masked", [NQT, P])
        vmask = sb("vmask", [P, NKT])
        xqT = sb("xqT", [P, KD, SEQ])
        xkT = sb("xkT", [P, KD, NKEY])
        kT = sb("kT", [P, KD, NKEY])
        q_last = sb("q_last", [P, KD, P])
        vrow = sb("vrow", [P, NKT, D])
        shared = sb("shared", [P, KD * NKB * VW])
        xg = shared[:, 0:NGT * D].rearrange("p (t d) -> p t d", t=NGT)
        vbd = shared[:, :].rearrange("p (k n j) -> p k n j", k=KD, n=NKB)
        sc_max = sb("sc_max", [P, KD, 2])
        sc_bias = sb("sc_bias", [P, KD * 2])
        pr_sum = sb("pr_sum", [P, HEADS])
        pr_inv = sb("pr_inv", [P, HEADS])
        att_row = sb("att_row", [P, D])
        zeros = sb("zeros", [P, XW])
        work = wqkv_sb[:, :, :].rearrange("p k n -> p (k n)")
        pr = work[:, 0:2 * D].rearrange("p (b k n) -> p b k n", b=2, k=KD)
        att = work[:, 4 * D:5 * D].rearrange("p (h d) -> p h d", h=HEADS)
        attT = work[:, 5 * D:6 * D].rearrange("p (k n) -> p k n", k=KD)
        xT_flat = xT[:, :, :, :].rearrange("p a k n -> p (a k n)")
        kbd = xT_flat[:, 0:8 * P].rearrange("p (a k b n) -> p a k b n", a=2, k=KD, b=2)
        TABLE = NET * NEXP
        tab_a = xT_flat[0:1, 8 * P:8 * P + TABLE].rearrange("p (t e) -> p t e", t=NET)
        tab_b = xT_flat[0:1, 8 * P + TABLE:8 * P + 2 * TABLE].rearrange("p (t e) -> p t e", t=NET)
        yb = xT_flat[:, 8 * P + 2 * TABLE:8 * P + 2 * TABLE + D]
        flat = staging[:, :, :].rearrange("p a b -> p (a b)")
        at = [0]

        def carve(n):
            at[0] += n
            return flat[:, at[0] - n:at[0]]

        rows = [carve(XW) for _ in range(SLOTS)]
        zt = [carve(D) for _ in range(SLOTS)]
        yo = [carve(D) for _ in range(SLOTS)]
        fxT = [carve(D).rearrange("p (k n) -> p k n", k=KD) for _ in range(SLOTS)]
        hb = carve(HID)
        hT = carve(HID).rearrange("p (k n) -> p k n", k=KH)
        gate = sb("gate", [P, SLOTS])
        tokf = sb("tokf", [P, SLOTS, 2])
        toki = sb("toki", [P, SLOTS, 2], I32)

        banks = [ctx.enter_context(nc.psum_tensor(f"bank{i}", [P, 512], F32)) for i in range(8)]
        ps_xt = banks[0:2]
        ps_lt, ps_lg, ps_cnt = banks[2], banks[3], banks[4]
        ps_a, ps_b, ps_c = banks[5], banks[6], banks[7]
        ps_misc = [ps_a, ps_b, ps_c]
        ps_scores, ps_att, ps_attT, ps_proj = [ps_a, ps_b], ps_c, banks[0], banks[1]
        ps_rows, ps_hidden, ps_hidT, ps_out = banks[2], banks[4], banks[3], banks[7]

        s_const = sem("constants_ready")
        s_ident = sem("identity_ready")
        s_zero = sem("zero_rows_ready")
        s_pool = sem("pool_chain")
        s_dve = sem("vector_chain")
        s_attw = sem("attention_weights_loaded")
        s_rw = sem("router_weights_loaded")
        s_expw = sem("expert_weights_loaded")
        s_x = [sem(f"x_group_loaded{g}") for g in range(NG)]
        s_map = sem("mapping_loaded")
        s_idx = sem("key_index_ready")
        s_mapk = sem("key_mapping_gathered")
        s_rowk = sem("key_row_index_ready")
        s_gath = sem("rows_gathered")
        s_var = sem("variance_ready")
        s_guess = sem("rstd_guess_ready")
        s_norm = sem("group_normalised")
        s_gnorm = sem("gathered_normalised")
        s_xt = sem("x_transposed")
        s_xtc = sem("x_transpose_copied")
        s_lt = sem("logits_ready")
        s_ltc = sem("logits_copied")
        s_lg = sem("logits_by_token")
        s_lgr = sem("logits_read")
        s_lgc = sem("logits_centred")
        s_lge = sem("logits_exp")
        s_cnt = sem("counts_ready")
        s_pre = sem("prefix_ready")
        s_preu = sem("prefix_used")
        s_pos = sem("positions_ready")
        s_sent = [sem(f"rows_sent{g}") for g in range(NG)]
        s_tab = sem("table_ready")
        s_pads = sem("pad_rows_written")
        s_gt = sem("gathered_transposed")
        s_gtc = sem("gathered_copied")
        s_qkv = sem("projection_ready")
        s_qkvc = sem("query_key_copied")
        s_vc = sem("value_copied")
        s_vst = sem("value_rows_stored")
        s_vz = sem("value_blocks_zeroed")
        s_vbd = sem("value_blocks_loaded")
        s_ql = sem("last_query_ready")
        s_kbd = sem("key_blocks_ready")
        s_sc = sem("scores_ready")
        s_max = sem("scores_max_ready")
        s_bias = sem("exp_bias_ready")
        s_pr = sem("exp_ready")
        s_at = sem("attended")
        s_atn = sem("attended_normalised")
        s_att = sem("attended_transposed")
        s_atc = sem("attended_copied")
        s_y = sem("projected")
        s_z = sem("residual_ready")
        s_zst = sem("residual_stored")
        s_ld = [sem(f"expert_rows_loaded{i}") for i in range(SLOTS)]
        s_ft = sem("expert_rows_transposed")
        s_ftc = sem("expert_rows_copied")
        s_h = sem("hidden_ready")
        s_hb = sem("hidden_biased")
        s_ht = sem("hidden_transposed")
        s_htc = sem("hidden_relu")
        s_fy = sem("expert_out_ready")
        s_tok = sem("token_index_ready")
        s_tstep = sem("token_index_steps")
        s_seen = sem("pool_saw_tile")
        s_yb = sem("expert_out_biased")
        s_zg = [sem(f"residual_gathered{i}") for i in range(SLOTS)]
        s_fo = sem("row_finished")
        s_out = [sem(f"rows_out{i}") for i in range(SLOTS)]

        NCONST = 10
        NQUAD = NT // 4
        ROUNDS = NET // SLOTS
        TILES = [NQT] + list(range(NQT))

        def halves(j):
            if j == NQT:
                return [(slice(0, P), 0, NKB - 1)]
            return [(slice(BLOCK * b, BLOCK * (b + 1)), b, 2 * j + b) for b in range(2)]

        def score_part(i, k, b, r):
            at = (KD * b + k) * P
            return ps_scores[i % 2][:, at + r.start:at + r.stop]

        block = ctx.enter_context(nc.Block())

        @block.sync
        def _(sp):
            block_first = mapping.rearrange("(c n q) -> c n q", n=P // KEYS, q=BLOCK)
            for c in range(2):
                sp.dma_start(map_b[:, c:c + 1], block_first[c, :, 0:1].to_broadcast([P // KEYS, KEYS])).then_inc(s_map, 16)
            sp.dma_start(map_b[:, 2:3], mapping[SEQ - 1:SEQ].unsqueeze(0).to_broadcast([P, 1])).then_inc(s_map, 16)
            sp.dma_start(map_row[:, :], mapping.rearrange("(t p) -> t p", p=P)).then_inc(s_map, 16)
            sp.dma_start(map_q[:, :], mapping.rearrange("(t p) -> p t", p=P)).then_inc(s_map, 16)
            x_t = x2.rearrange("(g t p) d -> g p t d", g=NG, p=P)
            for g in range(NG):
                sp.dma_start(x_sb[:, g * GT:(g + 1) * GT, :], x_t[g]).then_inc(s_x[g], 16)
                if g == 0:
                    sp.dma_start(wr_sb[:, :, :], wr.rearrange("(k p) e -> p k e", p=P)).then_inc(s_rw, 16)
                    sp.dma_start(br_bc[:, :], br.unsqueeze(0).to_broadcast([P, NEXP])).then_inc(s_rw, 16)
                if g == 1:
                    sp.dma_start(wqkv_sb[:, :, :], wqkv.rearrange("(k p) n -> p k n", p=P)).then_inc(s_attw, 16)
                    sp.dma_start(wproj_sb[:, :, :], wproj.rearrange("(k p) n -> p k n", p=P)).then_inc(s_attw, 16)
                    sp.dma_start(bqk_col[:, :], bqkv[0:2 * D].rearrange("(c p) -> p c", p=P)).then_inc(s_attw, 16)
                    sp.dma_start(bv_bc[:, :], bqkv[2 * D:3 * D].unsqueeze(0).to_broadcast([P, D])).then_inc(s_attw, 16)
                    sp.dma_start(bproj_bc[:, :], bproj.unsqueeze(0).to_broadcast([P, D])).then_inc(s_attw, 16)
            for e in range(NEXP):
                sp.dma_start(w1_sb[:, e, :, :], w1[e].rearrange("(k p) n -> p k n", p=P)).then_inc(s_expw, 16)
                sp.dma_start(w2_sb[:, e, :, :], w2[e].rearrange("(k p) n -> p k n", p=P)).then_inc(s_expw, 16)
            sp.dma_start(b1_bc[:, :, :], b1.unsqueeze(0).to_broadcast([P, NEXP, HID])).then_inc(s_expw, 16)
            sp.dma_start(b2_bc[:, :, :], b2.unsqueeze(0).to_broadcast([P, NEXP, D])).then_inc(s_expw, 16)

            sp.wait_ge(s_vc, NKT)
            sp.dma_start(vals[0:2 * P, :].rearrange("(t p) d -> p t d", p=P), vrow[:, 0:2, :]).then_inc(s_vst, 16)
            sp.dma_start(vals[2 * P:NKEY, :], vrow[0:LASTK, 2, :]).then_inc(s_vst, 16)
            sp.wait_ge(s_vst, 32)
            sp.wait_ge(s_vz, 1)
            v_src = vals.rearrange("(n s) (k h d) -> k h s n d", s=KEYS, k=KD, h=HH)
            for k in range(KD):
                for h in range(HH):
                    sp.dma_start(vbd[h * HD:(h + 1) * HD, k, :, h * HD:(h + 1) * HD], v_src[k, h]).then_inc(s_vbd, 16)

            sp.wait_ge(s_zero, 1)
            sp.dma_start(sent[NEXP * REG:NEXP * REG + P, :], zeros[:, :]).then_inc(s_pads, 16)
            sp.wait_ge(s_tab, 1)
            for e in range(NEXP):
                first_pad = sp.value_load(pad_row[0:1, e:e + 1], min_val=e * REG, max_val=e * REG + M)
                sp.dma_start(sent[bass.ds(first_pad, P), :], zeros[:, :]).then_inc(s_pads, 16)

            z_t = zrows.rearrange("(t p) d -> p t d", p=P)
            sp.wait_ge(s_z, 1)
            sp.dma_start(z_t[:, NQT:NT, :], x_sb[:, NQT:NT, :]).then_inc(s_zst, 16)
            for j in range(0, NQT, 4):
                sp.wait_ge(s_z, 1 + j + 4)
                sp.dma_start(z_t[:, j:j + 4, :], x_sb[:, j:j + 4, :]).then_inc(s_zst, 16)

            for g in range(NG):
                sp.wait_ge(s_sent[g], 16 * GT)
            sp.wait_ge(s_pads, 16 * (NEXP + 1))

            def load(t, slot):
                row = sp.value_load(tab_row[0:1, bass.ds(t, 1)], min_val=0, max_val=NEXP * REG)
                sp.dma_start(rows[slot], sent[bass.ds(row, P), :]).then_inc(s_ld[slot], 16)

            for slot in range(SLOTS):
                load(slot, slot)
            with sp.Fori(1, ROUNDS) as r:
                for slot in range(SLOTS):
                    sp.wait_ge(s_ft, (r - 1) * SLOTS + slot + 1)
                    sp.wait_ge(s_tok, (r - 1) * SLOTS + slot + 1)
                    load(r * SLOTS + slot, slot)

        @block.gpsimd
        def _(pool):
            ch = Chain(pool, s_pool)
            pool.memset(zeros[:, :], 0.0).then_inc(s_zero, 1)
            ch.then(pool.memset(ones[:, :], 1.0))
            pool.affine_select(out=ident[:, :], in_=ones[:, :], pattern=[[-1, P]], compare_op=ALU.is_equal,
                               fill=0.0, base=0, channel_multiplier=1).then_inc(s_ident, 1)
            pool.affine_select(out=before[:, :], in_=ones[:, :], pattern=[[1, P]], compare_op=ALU.is_gt,
                               fill=0.0, base=0, channel_multiplier=-1).then_inc(s_const, 1)
            ch.then(pool.affine_select(out=headlow[:, :], in_=ones[:, 0:HH], pattern=[[-HD, HH]], compare_op=ALU.is_ge,
                                       fill=0.0, base=0, channel_multiplier=1))
            pool.affine_select(out=headmask[:, :], in_=headlow[:, :], pattern=[[HD, HH]], compare_op=ALU.is_gt,
                               fill=0.0, base=HD, channel_multiplier=-1).then_inc(s_const, 1)
            pool.memset(restart[:, :, 1:GT], 1.0).then_inc(s_const, 1)
            pool.memset(restart[:, :, 0:1], 0.0).then_inc(s_const, 1)
            pool.memset(minus_half[:, :], -0.5).then_inc(s_const, 1)
            pool.iota(part_i[:, :], pattern=[[0, 1]], base=0, channel_multiplier=1).then_inc(s_const, 1)
            pool.iota(first_i[:, :], pattern=[[-1, NEXP]], base=NEXP, channel_multiplier=0).then_inc(s_const, 1)
            pool.iota(region_i[:, :], pattern=[[REG, NEXP]], base=-1, channel_multiplier=0).then_inc(s_const, 1)
            pool.iota(code_i[:, :], pattern=[[-P, NT]], base=M, channel_multiplier=-1).then_inc(s_const, 1)
            pool.iota(tile_i[:, :], pattern=[[1, NET]], base=0, channel_multiplier=0).then_inc(s_const, 1)

            pool.wait_ge(s_idx, 1)
            table = mapping.unsqueeze(1)
            for c in range(NKT):
                n = P if c < 2 else LASTK
                pool.indirect_dma_start(out=map_k[0:n, c:c + 1], out_offset=None, in_=table,
                                        in_offset=bass.IndirectOffsetOnAxis(ap=idx_k[0:n, c:c + 1], axis=0),
                                        bounds_check=SEQ - 1, oob_is_err=False).then_inc(s_mapk, 16)

            def rstd_guess(n, count):
                pool.wait_ge(s_var, count)
                pool.tensor_tensor(guess[:, 0:n], varp[:, 0:n], minus_half[:, 0:n], ALU.pow).then_inc(s_guess, 1)

            def gather(tile, index, n):
                pool.indirect_dma_start(out=xg[0:n, tile, :], out_offset=None, in_=x2,
                                        in_offset=bass.IndirectOffsetOnAxis(ap=index, axis=0),
                                        bounds_check=M - 1, oob_is_err=False).then_inc(s_gath, 16)

            def send(g):
                pool.wait_ge(s_pos, g + 1)
                for t in range(GT):
                    pool.indirect_dma_start(out=sent, in_=xrow[g % 2][:, t, :], in_offset=None,
                                            out_offset=bass.IndirectOffsetOnAxis(ap=pos[:, g, t:t + 1], axis=0),
                                            bounds_check=NEXP * REG + P - 1, oob_is_err=False).then_inc(s_sent[g], 16)

            rstd_guess(GT, 1)
            for t in range(NQT):
                gather(t, row_q[:, t:t + 1], P)
                if t == 3:
                    rstd_guess(GT, 2)
            pool.wait_ge(s_rowk, 1)
            for c in range(NKT):
                n = P if c < 2 else LASTK
                gather(NQT + c, row_k[0:n, c:c + 1], n)
            rstd_guess(NGT, 3)
            send(0)
            rstd_guess(GT, 4)
            send(1)
            rstd_guess(GT, 5)
            send(2)
            send(3)

            for g in range(NG):
                pool.wait_ge(s_sent[g], 16 * GT)
            pool.wait_ge(s_zst, 16 * (1 + NQT // 4))
            last_row = pool.to_reg(M - 1)

            def await_tile(sem_, tile):
                pool.wait_ge(sem_, tile + 1)
                pool.sem_inc(s_seen, 1)

            def fetch(slot, tile, round_):
                await_tile(s_tok, tile)
                pool.indirect_dma_start(out=zt[slot], out_offset=None, in_=zrows,
                                        in_offset=bass.IndirectOffsetOnAxis(ap=toki[:, slot, 0:1], axis=0),
                                        bounds_check=last_row, oob_is_err=False).then_inc(s_zg[slot], 16)

            def write(slot, tile):
                await_tile(s_fo, tile)
                pool.indirect_dma_start(out=out2, in_=yo[slot], in_offset=None,
                                        out_offset=bass.IndirectOffsetOnAxis(ap=toki[:, slot, 1:2], axis=0),
                                        bounds_check=last_row, oob_is_err=False).then_inc(s_out[slot], 16)

            fetch(0, 0, 0)
            with pool.Fori(0, ROUNDS - 1) as r:
                for slot in range(SLOTS):
                    fetch((slot + 1) % SLOTS, r * SLOTS + slot + 1, r)
                    write(slot, r * SLOTS + slot)
            for slot in range(SLOTS):
                t = (ROUNDS - 1) * SLOTS + slot
                if slot + 1 < SLOTS:
                    fetch(slot + 1, t + 1, ROUNDS - 1)
                write(slot, t)
            for slot in range(SLOTS):
                pool.wait_ge(s_out[slot], 16 * ROUNDS)

        @block.scalar
        def _(act):
            qkv_done, gt_done = [0], [0]

            def router(g):
                for i in range(2):
                    u = 2 * g + i
                    for b in range(2):
                        act.wait_ge(s_xt, 2 * u + b + 1)
                        if u >= 2 and b == 0:
                            act.wait_ge(s_lt, u - 1)
                        nc.scalar.activation(xT[:, u % 2, :, b * 2 * P:(b + 1) * 2 * P].rearrange("p k (t n) -> p t k n", t=2),
                                             ps_xt[b][:, :].rearrange("p (t k n) -> p t k n", t=2, k=KD),
                                             ACT.Copy).then_inc(s_xtc, 1)
                    if u >= 1:
                        logits_copy(u - 1)

            def logits_copy(u):
                act.wait_ge(s_lt, u + 1)
                if u >= 2:
                    act.wait_ge(s_lg, u - 1)
                nc.scalar.activation(logT[:, u % 2, :], ps_lt[0:NEXP, :], ACT.Copy).then_inc(s_ltc, 1)

            def logits_exp(g):
                act.wait_ge(s_lgc, g + 1)
                nc.scalar.activation(lge[:, :, :], lgd[:, :, :], ACT.Exp).then_inc(s_lge, 1)

            def gathered():
                for i in range(NGT):
                    act.wait_ge(s_gt, i + 1)
                    n = LASTK if i == NGT - 1 else P
                    dst = xqT[:, :, i * P:i * P + n] if i < NQT else xkT[:, :, (i - NQT) * P:(i - NQT) * P + n]
                    src = ps_misc[i % 3][:, 0:KD * P].rearrange("p (k n) -> p k n", k=KD)[:, :, 0:n]
                    nc.scalar.activation(dst, src, ACT.Copy).then_inc(s_gtc, 1)

            def projections():
                act.wait_ge(s_attw, 16 * 5)
                for c in range(KD):
                    act.wait_ge(s_qkv, c + 1)
                    nc.scalar.activation(kT[:, c, :], ps_misc[c][:, 0:NKEY], ACT.Identity,
                                         bias=bqk_col[:, KD + c:KD + c + 1]).then_inc(s_qkvc, 1)
                for half in range(2):
                    act.wait_ge(s_qkv, KD + NKT + 2 * half + 2)
                    for c in range(KD):
                        nc.scalar.activation(xqT[:, c, half * 512:(half + 1) * 512], ps_misc[c][:, :], ACT.Identity,
                                             bias=bqk_col[:, c:c + 1]).then_inc(s_qkvc, 1)
                act.wait_ge(s_qkvc, 3 * KD)
                for c in range(KD):
                    nc.scalar.activation(q_last[:, c, :], xqT[:, c, SEQ - 1:SEQ].to_broadcast([P, P]),
                                         ACT.Copy).then_inc(s_ql, 1)

            router(0)
            gathered()
            router(1)
            logits_exp(0)
            projections()
            router(2)
            logits_exp(1)
            router(3)
            logits_copy(NQUAD - 1)
            logits_exp(2)
            logits_exp(3)

            for step in range(len(TILES) + 2):
                if step < len(TILES):
                    act.wait_ge(s_bias, step + 1)
                    if step >= 2:
                        act.wait_ge(s_at, step - 1)
                    for k in range(KD):
                        for r, b, n in halves(TILES[step]):
                            ins = nc.scalar.activation(pr[:, step % 2, k, r], score_part(step, k, b, r), ACT.Exp,
                                                       bias=sc_bias[:, 2 * k + b:2 * k + b + 1], scale=SCALE)
                    ins.then_inc(s_pr, 1)
                if step >= 2:
                    act.wait_ge(s_att, step - 1)
                    nc.scalar.activation(attT[:, :, :], ps_attT[:, 0:D].rearrange("p (k n) -> p k n", k=KD),
                                         ACT.Copy).then_inc(s_atc, 1)

            def rows_copy(slot, tile, guard):
                act.wait_ge(s_ft, tile + 1)
                if guard is not None:
                    act.wait_ge(s_h, guard)
                nc.scalar.activation(fxT[slot], ps_rows[:, 0:D].rearrange("p (k n) -> p k n", k=KD),
                                     ACT.Copy).then_inc(s_ftc, 1)

            def relu(tile):
                act.wait_ge(s_ht, tile + 1)
                nc.scalar.activation(hT, ps_hidT[:, :].rearrange("p (k n) -> p k n", k=KH), ACT.Relu).then_inc(s_htc, 1)

            rows_copy(0, 0, None)
            rows_copy(1, 1, None)
            relu(0)
            rows_copy(2, 2, None)
            relu(1)
            rows_copy(0, 3, 1)
            with act.Fori(1, ROUNDS - 1) as r:
                for slot in range(SLOTS):
                    t = r * SLOTS + slot
                    relu(t - 1)
                    rows_copy((slot + 1) % SLOTS, t + 1, t - 1)
            for slot in range(SLOTS):
                t = (ROUNDS - 1) * SLOTS + slot
                relu(t - 1)
                if t + 1 < NET:
                    rows_copy((slot + 1) % SLOTS, t + 1, t - 1)
            relu(NET - 1)

        @block.vector
        def _(dve):
            ch = Chain(dve, s_dve)
            v = nc.vector

            dve.wait_ge(s_const, NCONST)
            v.tensor_copy(first_of[:, :], first_i[:, :])
            v.tensor_copy(code[:, :], code_i[:, :])
            v.tensor_copy(tile_no[:, :], tile_i[:, :])
            v.tensor_copy(region0[:, :], region_i[:, :])
            v.memset(mv[:, :, :], 0.0)
            ch.then(v.tensor_copy(carry[:, :], region_i[:, :]))
            ch.then(v.tensor_scalar(key_step[:, :], part_i[:, :], KEYS - 1, 2, ALU.bitwise_and, ALU.logical_shift_left))
            dve.wait_ge(s_map, 80)
            ch.then(v.tensor_scalar(idx_a[:, :], map_b[:, :], -SEG, None, ALU.bitwise_and))
            ch.then(v.tensor_tensor(idx_a[:, :], idx_a[:, :], key_step[:, :].to_broadcast([P, NKT]), ALU.bitwise_or))
            v.tensor_scalar(row_q[:, :], map_q[:, :], M - 1, None, ALU.min)
            v.tensor_scalar(masked[:, :], map_row[:, :], M, MASKED, ALU.is_ge, ALU.mult)
            v.tensor_scalar(vmask[:, :], map_b[:, :], M, None, ALU.is_lt)
            v.tensor_scalar(idx_k[:, :], idx_a[:, :], SEQ - 1, None, ALU.min).then_inc(s_idx, 1)

            def layer_norm(rows_of, n, count, out_of):
                for i in range(n):
                    src, pn = rows_of(i), LASTK if n == NGT and i == n - 1 else P
                    ins = v.bn_stats(stats[0:pn, i, :], src)
                ch.then(ins)
                for i in range(n):
                    pn = LASTK if n == NGT and i == n - 1 else P
                    ins = v.bn_aggr(mv[0:pn, i, :], stats[0:pn, i, :])
                ch.then(ins)
                v.tensor_scalar(varp[:, 0:n], mv[:, 0:n, 1], LN_EPS, None, ALU.add).then_inc(s_var, 1)
                dve.wait_ge(s_guess, count)
                ch.then(v.tensor_tensor(nt1[:, 0:n], guess[:, 0:n], guess[:, 0:n], ALU.mult))
                ch.then(v.tensor_tensor(nt2[:, 0:n], nt1[:, 0:n], varp[:, 0:n], ALU.mult))
                ch.then(v.tensor_scalar(nt1[:, 0:n], nt2[:, 0:n], -0.5, 1.5, ALU.mult, ALU.add))
                ch.then(v.tensor_tensor(rstd[:, 0:n], guess[:, 0:n], nt1[:, 0:n], ALU.mult))
                for i in range(n):
                    pn = LASTK if n == NGT and i == n - 1 else P
                    ins = v.tensor_scalar(out_of(i), rows_of(i), mv[0:pn, i, 0:1], rstd[0:pn, i:i + 1],
                                          ALU.subtract, ALU.mult)
                return ins

            def norm_group(g, count):
                dve.wait_ge(s_x[g], 16)
                if g >= 2:
                    dve.wait_ge(s_sent[g - 2], 16 * GT)
                layer_norm(lambda i: x_sb[:, g * GT + i, :], GT, count,
                           lambda i: xrow[g % 2][:, i, 0:D]).then_inc(s_norm, 1)

            def gathered_row(i):
                return xg[0:LASTK if i == NGT - 1 else P, i, :]

            def route(g):
                dve.wait_ge(s_lg, 2 * g + 2)
                v.tensor_tensor(lg[:, :, :], ps_lg[:, g * GT * NEXP:(g + 1) * GT * NEXP].rearrange("p (t e) -> p t e", t=GT),
                                br_bc[:, :].unsqueeze(1).to_broadcast([P, GT, NEXP]), ALU.add).then_inc(s_lgr, 1)
                dve.wait_ge(s_lgr, g + 1)
                ch.then(v.tensor_reduce(lgm[:, :], lg[:, :, :], AX.X, ALU.max))
                v.tensor_tensor(lgd[:, :, :], lg[:, :, :], lgm[:, :].unsqueeze(2).to_broadcast([P, GT, NEXP]),
                                ALU.subtract).then_inc(s_lgc, 1)
                dve.wait_ge(s_lgc, g + 1)
                ch.then(v.scalar_tensor_tensor(out=eqw[:, :, :], in0=lgd[:, :, :], scalar=0.0,
                                               in1=first_of[:, :].unsqueeze(1).to_broadcast([P, GT, NEXP]),
                                               op0=ALU.is_ge, op1=ALU.mult))
                ch.then(v.tensor_reduce(eqm[:, :], eqw[:, :, :], AX.X, ALU.max))
                ch.then(v.tensor_tensor(onehot[:, :, :].rearrange("p e t -> p t e"), eqw[:, :, :],
                                        eqm[:, :].unsqueeze(2).to_broadcast([P, GT, NEXP]), ALU.is_equal))
                ch.then(v.tensor_tensor_scan(rank[:, :, :].rearrange("p e t -> p (e t)"),
                                             restart[:, :, :].rearrange("p e t -> p (e t)"),
                                             onehot[:, :, :].rearrange("p e t -> p (e t)"), 0.0, ALU.mult, ALU.add))
                v.tensor_copy(cnt[:, :], rank[:, :, GT - 1]).then_inc(s_cnt, 1)
                dve.wait_ge(s_lge, g + 1)
                ch.then(v.tensor_reduce(lsum[:, :], lge[:, :, :], AX.X, ALU.add))
                v.reciprocal(xrow[g % 2][:, :, D], lsum[:, :])
                v.tensor_copy(xrow[g % 2][:, :, D + 1], code[:, g * GT:(g + 1) * GT])
                dve.wait_ge(s_pre, g + 1)
                ch.then(v.tensor_tensor(offs[:, :], ps_cnt[:, 0:NEXP], carry[:, :], ALU.add))
                v.tensor_tensor(carry[:, :], ps_cnt[:, NEXP:2 * NEXP], carry[:, :], ALU.add).then_inc(s_preu, 1)
                ch.then(v.tensor_tensor(place[:, :, :], rank[:, :, :], offs[:, :].unsqueeze(2).to_broadcast([P, NEXP, GT]),
                                        ALU.add))
                ch.then(v.tensor_tensor(place[:, :, :], place[:, :, :], onehot[:, :, :], ALU.mult))
                ch.then(v.tensor_reduce(posf[:, :], place[:, :, :].rearrange("p e t -> p t e"), AX.X, ALU.add))
                v.tensor_copy(pos[:, g, :], posf[:, :]).then_inc(s_pos, 1)

            def tile_table():
                dve.wait_ge(s_preu, NG)
                ch.then(v.tensor_scalar(pad_row[:, :], carry[0:1, :], 1.0, None, ALU.add))
                ch.then(v.tensor_tensor(tab_n[:, :], carry[0:1, :], region0[0:1, :], ALU.subtract))
                ch.then(v.tensor_scalar(tab_i[:, :], tab_n[:, :], float(P - 1), None, ALU.add))
                ch.then(v.tensor_scalar(tab_i[:, :], tab_i[:, :], 7, None, ALU.logical_shift_right))
                ch.then(v.tensor_copy(tab_n[:, :], tab_i[:, :]))
                ch.then(v.tensor_tensor_scan(tab_end[:, :], ones[0:1, 0:NEXP], tab_n[:, :], 0.0, ALU.mult, ALU.add))
                ch.then(v.tensor_tensor(tab_start[:, :], tab_end[:, :], tab_n[:, :], ALU.subtract))
                ch.then(v.scalar_tensor_tensor(out=tab_base[:, :], in0=tab_start[:, :], scalar=-float(P),
                                               in1=region0[0:1, :], op0=ALU.mult, op1=ALU.add))
                ch.then(v.tensor_scalar(tab_base[:, :], tab_base[:, :], 1.0, None, ALU.add))
                tiles = tile_no[0:1, :].unsqueeze(2).to_broadcast([1, NET, NEXP])

                def by_expert(a):
                    return a[:, :].unsqueeze(1).to_broadcast([1, NET, NEXP])

                ch.then(v.tensor_tensor(tab_a[:, :, :], by_expert(tab_end), tiles, ALU.is_le))
                ch.then(v.tensor_reduce(tab_e[:, :], tab_a[:, :, :], AX.X, ALU.add))
                ch.then(v.tensor_tensor(tab_b[:, :, :], by_expert(tab_start), tiles, ALU.is_le))
                ch.then(v.tensor_tensor(tab_a[:, :, :], tab_b[:, :, :], tab_a[:, :, :], ALU.subtract))
                ch.then(v.scalar_tensor_tensor(out=tab_b[:, :, :], in0=tiles, scalar=float(P), in1=by_expert(tab_base),
                                               op0=ALU.mult, op1=ALU.add))
                ch.then(v.tensor_tensor(tab_a[:, :, :], tab_b[:, :, :], tab_a[:, :, :], ALU.mult))
                ch.then(v.tensor_reduce(tab_r[:, :], tab_a[:, :, :], AX.X, ALU.add))
                ch.then(v.tensor_scalar(tab_u[:, :], tab_e[:, :], float(NEXP), float(NEXP * REG), ALU.is_ge, ALU.mult))
                ch.then(v.tensor_tensor(tab_row[:, :], tab_r[:, :], tab_u[:, :], ALU.add))
                v.tensor_scalar(tab_exp[:, :], tab_e[:, :], float(NEXP - 1), None, ALU.min).then_inc(s_tab, 1)

            norm_group(0, 1)
            norm_group(1, 2)
            dve.wait_ge(s_mapk, 16 * NKT)
            for c in range(NKT):
                n = P if c < 2 else LASTK
                ins = v.tensor_scalar(row_k[0:n, c:c + 1], map_k[0:n, c:c + 1], M - 1, None, ALU.min)
            ins.then_inc(s_rowk, 1)
            dve.wait_ge(s_gath, 16 * NGT)
            layer_norm(gathered_row, NGT, 3, gathered_row).then_inc(s_gnorm, 1)
            route(0)
            dve.wait_ge(s_attw, 16 * 5)
            for c in range(NKT):
                n = P if c < 2 else LASTK
                dve.wait_ge(s_qkv, KD + c + 1)
                ch.then(v.tensor_tensor(vrow[0:n, c, :], ps_misc[(KD + c) % 3][0:n, 0:D], bv_bc[0:n, :], ALU.add))
                v.tensor_scalar(vrow[0:n, c, :], vrow[0:n, c, :], vmask[0:n, c:c + 1], None, ALU.mult).then_inc(s_vc, 1)
            ch.then(v.memset(shared[:, :], 0.0))
            v.tensor_copy(vbd[:, :, :, P:VW], headmask[:, :].unsqueeze(1).unsqueeze(1)
                          .to_broadcast([P, KD, NKB, HH])).then_inc(s_vz, 1)
            norm_group(2, 4)
            route(1)
            norm_group(3, 5)
            route(2)
            route(3)
            tile_table()

            def key_blocks(i):
                j = TILES[i]
                if i >= 2:
                    dve.wait_ge(s_sc, i - 1)
                for k in range(KD):
                    for b, n in enumerate([NKB - 1] if j == NQT else [2 * j, 2 * j + 1]):
                        ins = v.tensor_tensor(kbd[:, i % 2, k, b, :].rearrange("p (h s) -> p h s", h=HH),
                                              kT[:, k, n * KEYS:(n + 1) * KEYS].unsqueeze(1).to_broadcast([P, HH, KEYS]),
                                              headmask[:, :].unsqueeze(2).to_broadcast([P, HH, KEYS]), ALU.mult)
                ins.then_inc(s_kbd, 1)

            ch.then(v.memset(sc_max[:, :, :], 0.0))
            dve.wait_ge(s_qkvc, KD)
            key_blocks(0)
            for step in range(len(TILES) + 2):
                if step + 1 < len(TILES):
                    key_blocks(step + 1)
                if step < len(TILES):
                    dve.wait_ge(s_sc, step + 1)
                    if step >= 1:
                        dve.wait_ge(s_bias, step)
                    for r, b, n in halves(TILES[step]):
                        src = ps_scores[step % 2][:, KD * b * P:KD * (b + 1) * P].rearrange("p (k n) -> p k n", k=KD)
                        ins = v.tensor_reduce(sc_max[:, :, b], src[:, :, r], AX.X, ALU.max)
                    ins.then_inc(s_max, 1)
                    dve.wait_ge(s_max, step + 1)
                    if step >= 1:
                        dve.wait_ge(s_pr, step)
                    v.tensor_scalar(sc_bias[:, :], sc_max[:, :, :].rearrange("p k b -> p (k b)"), -SCALE, None,
                                    ALU.mult).then_inc(s_bias, 1)
                if 1 <= step <= len(TILES):
                    dve.wait_ge(s_at, step)
                    got = ps_att[:, 0:KD * VW].rearrange("p (k j) -> p k j", k=KD)
                    ch.then(v.tensor_scalar(pr_sum[:, :].rearrange("p (k h) -> p k h", k=KD), got[:, :, P:VW], SUM_EPS, None,
                                            ALU.add))
                    ch.then(v.reciprocal(pr_inv[:, :], pr_sum[:, :]))
                    if step >= 2:
                        dve.wait_ge(s_att, step - 1)
                    for k in range(KD):
                        ins = v.tensor_tensor(att[:, k * HH:(k + 1) * HH, :], got[:, k, 0:P].rearrange("p (h d) -> p h d", h=HH),
                                              pr_inv[:, k * HH:(k + 1) * HH].unsqueeze(2).to_broadcast([P, HH, HD]), ALU.mult)
                    ins.then_inc(s_atn, 1)
                if step >= 2:
                    i, j = step - 2, TILES[step - 2]
                    dve.wait_ge(s_y, i + 1)
                    ch.then(v.tensor_tensor(att_row[:, :], ps_proj[:, 0:D], bproj_bc[:, :], ALU.add))
                    if j == NQT:
                        ins = v.tensor_tensor(x_sb[:, NQT:NT, :], x_sb[:, NQT:NT, :],
                                              att_row[:, :].unsqueeze(1).to_broadcast([P, NT - NQT, D]), ALU.add)
                    else:
                        ins = v.tensor_tensor(x_sb[:, j, :], x_sb[:, j, :], att_row[:, :], ALU.add)
                    ins.then_inc(s_z, 1)
                    dve.wait_ge(s_z, i + 1)

            dve.wait_ge(s_expw, 16 * (2 * NEXP + 2))

            def tokens(tile, slot, rnd, reused):
                dve.wait_ge(s_ld[slot], 16 * rnd + 16)
                if reused:
                    dve.wait_ge(s_out[slot], 16 * rnd)
                    dve.wait_ge(s_fo, tile - 2)
                v.tensor_copy(gate[:, slot:slot + 1], rows[slot][:, D:D + 1])
                v.tensor_scalar(tokf[:, slot, 1:2], rows[slot][:, D + 1:D + 2], -1.0, float(M), ALU.mult,
                                ALU.add).then_inc(s_tstep, 1)
                dve.wait_ge(s_tstep, 2 * tile + 1)
                v.tensor_scalar(tokf[:, slot, 0:1], tokf[:, slot, 1:2], float(M - 1), None, ALU.min).then_inc(s_tstep, 1)
                dve.wait_ge(s_tstep, 2 * tile + 2)
                v.tensor_copy(toki[:, slot, :], tokf[:, slot, :]).then_inc(s_tok, 1)

            def expert_of(tile):
                return dve.value_load(tab_exp[0:1, bass.ds(tile, 1)], min_val=0, max_val=NEXP - 1)

            def hidden_bias(tile, peeled_first):
                e = expert_of(tile)
                dve.wait_ge(s_h, tile + 1)
                if not peeled_first:
                    dve.wait_ge(s_ht, tile)
                v.tensor_tensor(hb, ps_hidden[:, :], b1_bc[:, bass.ds(e, 1), :].rearrange("p a n -> p (a n)"),
                                ALU.add).then_inc(s_hb, 1)

            def finish(tile, slot, rnd):
                e = expert_of(tile)
                dve.wait_ge(s_fy, tile + 1)
                v.tensor_tensor(yb, ps_out[:, 0:D], b2_bc[:, bass.ds(e, 1), :].rearrange("p a n -> p (a n)"),
                                ALU.add).then_inc(s_yb, 1)
                dve.wait_ge(s_yb, tile + 1)
                dve.wait_ge(s_zg[slot], 16 * rnd + 16)
                v.scalar_tensor_tensor(out=yo[slot], in0=yb, scalar=gate[:, slot:slot + 1], in1=zt[slot],
                                       op0=ALU.mult, op1=ALU.add).then_inc(s_fo, 1)

            def step(rnd, slot, first_step=False, last_step=False, reused=True):
                t = rnd * SLOTS + slot
                hidden_bias(t, first_step)
                if not first_step:
                    finish(t - 1, (slot - 1) % SLOTS, rnd - (slot == 0))
                if not last_step:
                    tokens(t + 1, (slot + 1) % SLOTS, rnd + (slot == SLOTS - 1), reused)

            tokens(0, 0, 0, False)
            for slot in range(SLOTS):
                step(0, slot, first_step=slot == 0, reused=slot == SLOTS - 1)
            with dve.Fori(1, ROUNDS - 1) as r:
                for slot in range(SLOTS):
                    step(r, slot)
            for slot in range(SLOTS):
                step(ROUNDS - 1, slot, last_step=slot == SLOTS - 1)
            dve.wait_ge(s_fo, NET - 1)
            finish(NET - 1, SLOTS - 1, ROUNDS - 1)

        @block.tensor
        def _(pe):
            def transpose(dst, src, n=P):
                return pe.transpose(dst, src, ident[0:n, 0:n])

            def quad_transposes(u):
                g = u // 2
                pe.wait_ge(s_norm, g + 1)
                for b in range(2):
                    if u >= 1:
                        pe.wait_ge(s_xtc, 2 * u + b - 1)
                    for t in range(2):
                        for k in range(KD):
                            ins = transpose(ps_xt[b][:, (t * KD + k) * P:(t * KD + k + 1) * P],
                                            xrow[g % 2][:, (u % 2) * 4 + 2 * b + t, k * P:(k + 1) * P])
                    ins.then_inc(s_xt, 1)

            def quad_logits(u):
                pe.wait_ge(s_xtc, 2 * u + 2)
                if u >= 1:
                    pe.wait_ge(s_ltc, u)
                for k in range(KD):
                    ins = pe.matmul(ps_lt[0:NEXP, :], wr_sb[:, k, :], xT[:, u % 2, k, :], start=(k == 0), stop=(k == KD - 1))
                ins.then_inc(s_lt, 1)

            def quad_by_token(u):
                pe.wait_ge(s_ltc, u + 1)
                if u >= 2:
                    pe.wait_ge(s_lgr, u // 2)
                for t in range(4):
                    ins = transpose(ps_lg[:, (4 * u + t) * NEXP:(4 * u + t + 1) * NEXP],
                                    logT[:, u % 2, t * P:(t + 1) * P], NEXP)
                ins.then_inc(s_lg, 1)

            def router(g):
                for u in (2 * g, 2 * g + 1):
                    quad_transposes(u)
                    if u >= 1:
                        quad_logits(u - 1)
                    if u >= 2:
                        quad_by_token(u - 2)

            def counts(g):
                pe.wait_ge(s_cnt, g + 1)
                if g >= 1:
                    pe.wait_ge(s_preu, g)
                pe.matmul(ps_cnt[:, 0:NEXP], before[:, :], cnt[:, :], start=True, stop=True)
                pe.matmul(ps_cnt[:, NEXP:2 * NEXP], ones[:, :], cnt[:, :], start=True, stop=True).then_inc(s_pre, 1)

            pe.wait_ge(s_ident, 1)
            pe.wait_ge(s_const, NCONST)
            pe.wait_ge(s_rw, 32)
            router(0)

            pe.wait_ge(s_gnorm, 1)
            for i in range(NGT):
                n = LASTK if i == NGT - 1 else P
                if i >= 3:
                    pe.wait_ge(s_gtc, i - 2)
                for k in range(KD):
                    ins = transpose(ps_misc[i % 3][:, k * P:k * P + n], xg[0:n, i, k * P:(k + 1) * P], n)
                ins.then_inc(s_gt, 1)

            router(1)
            counts(0)

            pe.wait_ge(s_attw, 16 * 5)
            pe.wait_ge(s_gtc, NGT)
            for c in range(KD):
                for k in range(KD):
                    ins = pe.matmul(ps_misc[c][:, 0:NKEY], wqkv_sb[:, k, D + c * P:D + (c + 1) * P], xkT[:, k, :],
                                    start=(k == 0), stop=(k == KD - 1))
                ins.then_inc(s_qkv, 1)
            for c in range(NKT):
                n = P if c < 2 else LASTK
                if c >= 1:
                    pe.wait_ge(s_qkvc, c)
                for k in range(KD):
                    ins = pe.matmul(ps_misc[(KD + c) % 3][0:n, 0:D], xkT[:, k, c * P:c * P + n], wqkv_sb[:, k, 2 * D:3 * D],
                                    start=(k == 0), stop=(k == KD - 1))
                ins.then_inc(s_qkv, 1)
            for half in range(2):
                for c in range(KD):
                    if half == 0:
                        pe.wait_ge(s_vc, c + 2)
                    else:
                        pe.wait_ge(s_qkvc, KD + c + 1)
                    for k in range(KD):
                        ins = pe.matmul(ps_misc[c][:, :], wqkv_sb[:, k, c * P:(c + 1) * P],
                                        xqT[:, k, half * 512:(half + 1) * 512], start=(k == 0), stop=(k == KD - 1))
                    ins.then_inc(s_qkv, 1)

            router(2)
            counts(1)
            router(3)
            quad_logits(NQUAD - 1)
            quad_by_token(NQUAD - 2)
            quad_by_token(NQUAD - 1)
            counts(2)
            counts(3)

            pe.wait_ge(s_qkvc, 3 * KD)
            pe.wait_ge(s_ql, KD)
            pe.wait_ge(s_xtc, 2 * NQUAD)
            for step in range(len(TILES) + 2):
                if step < len(TILES):
                    j = TILES[step]
                    pe.wait_ge(s_kbd, step + 1)
                    if step >= 2:
                        pe.wait_ge(s_pr, step - 1)
                    q = q_last[:, :, :] if j == NQT else xqT[:, :, j * P:(j + 1) * P]
                    own = min(j, NQT - 1)
                    mask = masked[:, P - 1:P].to_broadcast([NQT, P]) if j == NQT else masked[:, :]
                    for r, b, n in halves(j):
                        for k in range(KD):
                            out_ = ps_scores[step % 2][:, (KD * b + k) * P:(KD * b + k + 1) * P]
                            pe.matmul(out_, ident[0:NQT, own:own + 1].to_broadcast([NQT, P]), mask,
                                      start=True, stop=False)
                            ins = pe.matmul(out_, kbd[:, step % 2, k, b, :], q[:, k, :], start=False, stop=True)
                    ins.then_inc(s_sc, 1)
                if step >= 2:
                    pe.wait_ge(s_atn, step - 1)
                    for k in range(KD):
                        ins = transpose(ps_attT[:, k * P:(k + 1) * P],
                                        att[:, k * HH:(k + 1) * HH, :].rearrange("p h d -> p (h d)"))
                    ins.then_inc(s_att, 1)
                if 1 <= step <= len(TILES):
                    j = TILES[step - 1]
                    pe.wait_ge(s_pr, step)
                    if step == 1:
                        pe.wait_ge(s_vbd, 16 * KD * HH)
                    else:
                        pe.wait_ge(s_atn, step - 1)
                    for r, b, n in halves(j):
                        for k in range(KD):
                            ins = pe.matmul(ps_att[r, k * VW:(k + 1) * VW], pr[:, (step - 1) % 2, k, r], vbd[:, k, n, :],
                                            start=True, stop=True)
                    ins.then_inc(s_at, 1)
                if step >= 2:
                    pe.wait_ge(s_atc, step - 1)
                    if step >= 3:
                        pe.wait_ge(s_z, step - 2)
                    for k in range(KD):
                        ins = pe.matmul(ps_proj[:, 0:D], attT[:, k, :], wproj_sb[:, k, :], start=(k == 0), stop=(k == KD - 1))
                    ins.then_inc(s_y, 1)

            def expert_of(tile):
                return pe.value_load(tab_exp[0:1, bass.ds(tile, 1)], min_val=0, max_val=NEXP - 1)

            def hidden_transposes(tile, early):
                pe.wait_ge(s_hb, tile + 1)
                if not early:
                    pe.wait_ge(s_htc, tile)
                for k in range(KH):
                    ins = transpose(ps_hidT[:, k * P:(k + 1) * P], hb[:, k * P:(k + 1) * P])
                ins.then_inc(s_ht, 1)

            def row_transposes(tile, slot, rnd, early=False):
                pe.wait_ge(s_ld[slot], 16 * rnd + 16)
                if not early:
                    pe.wait_ge(s_ftc, tile)
                for k in range(KD):
                    ins = transpose(ps_rows[:, k * P:(k + 1) * P], rows[slot][:, k * P:(k + 1) * P])
                ins.then_inc(s_ft, 1)

            def hidden(tile, slot, early):
                e = expert_of(tile)
                pe.wait_ge(s_ftc, tile + 1)
                if not early:
                    pe.wait_ge(s_hb, tile)
                for k in range(KD):
                    ins = pe.matmul(ps_hidden[:, :], fxT[slot][:, k, :],
                                    w1_sb[:, bass.ds(e, 1), k, :].rearrange("p a n -> p (a n)"),
                                    start=(k == 0), stop=(k == KD - 1))
                ins.then_inc(s_h, 1)

            def expert_out(tile, early):
                e = expert_of(tile)
                pe.wait_ge(s_htc, tile + 1)
                if not early:
                    pe.wait_ge(s_yb, tile)
                for k in range(KH):
                    ins = pe.matmul(ps_out[:, 0:D], hT[:, k, :],
                                    w2_sb[:, bass.ds(e, 1), k, :].rearrange("p a n -> p (a n)"),
                                    start=(k == 0), stop=(k == KH - 1))
                ins.then_inc(s_fy, 1)

            def step(rnd, slot, warm=2, last_step=False):
                t = rnd * SLOTS + slot
                if warm >= 1:
                    hidden_transposes(t - 1, early=warm < 2)
                if not last_step:
                    row_transposes(t + 1, (slot + 1) % SLOTS, rnd + (slot == SLOTS - 1))
                hidden(t, slot, early=warm < 1)
                if warm >= 1:
                    expert_out(t - 1, early=warm < 2)

            pe.wait_ge(s_expw, 16 * (2 * NEXP + 2))
            pe.wait_ge(s_tab, 1)
            pe.wait_ge(s_ltc, NQUAD)
            pe.wait_ge(s_preu, NG)
            pe.wait_ge(s_lgr, NG)
            pe.wait_ge(s_atn, len(TILES))
            row_transposes(0, 0, 0, early=True)
            for slot in range(SLOTS):
                step(0, slot, warm=min(slot, 2))
            with pe.Fori(1, ROUNDS - 1) as r:
                for slot in range(SLOTS):
                    step(r, slot)
            for slot in range(SLOTS):
                step(ROUNDS - 1, slot, last_step=slot == SLOTS - 1)
            hidden_transposes(NET - 1, early=False)
            expert_out(NET - 1, early=False)


_INS = ["L0_attn_x", "L0_attn_Wqkv", "L0_attn_bqkv", "L0_attn_Wproj", "L0_attn_bproj", "L0_attn_mapping",
        "L0_ffn_Wr", "L0_ffn_br", "L0_ffn_W1", "L0_ffn_b1", "L0_ffn_W2", "L0_ffn_b2"]


def kernel(**inputs):
    import numpy as _np
    import concourse.bacc as _bacc
    from concourse import mybir as _mybir
    from concourse.bass_utils import run_bass_kernel_spmd as _run

    nc = _bacc.Bacc("TRN2", target_bir_lowering=False, num_devices=1)
    arrays, args = {}, []
    for name in _INS:
        a = _np.ascontiguousarray(inputs[name])
        arrays[f"in_{name}_dram"] = a
        args.append(nc.dram_tensor(f"in_{name}_dram", a.shape, _mybir.dt.from_np(a.dtype), kind="ExternalInput").ap())
    out = nc.dram_tensor("out_0_dram", (1, M, D), F32, kind="ExternalOutput").ap()
    build(nc, *args, out)
    r = _run(nc, [arrays], core_ids=[0])
    return r.results[0]["out_0_dram"]
```

```python
from contextlib import ExitStack

import concourse.bass as bass
from concourse import mybir

F32 = mybir.dt.float32
F32R = mybir.dt.float32r
BF16 = mybir.dt.bfloat16
I32 = mybir.dt.int32
ALU = mybir.AluOpType
ACT = mybir.ActivationFunctionType
AX = mybir.AxisListType

P = 128
M, D = 4096, 256
SEQ = 1024
HEADS, HD = 16, 16
BLOCK, KEYS = 64, 16
SEG, DIL = 64, 4
SCALE = HD ** -0.5
NEXP, HID = 8, 512
LN_EPS, SUM_EPS = 1e-5, 1e-6

KD = D // P
KH = HID // P
NT = M // P
GT = 8
NG = NT // GT
NQT = SEQ // P
NKB = SEQ // BLOCK + 1
NKEY = NKB * KEYS
NKT = 3
LASTK = NKEY - 2 * P
NGT = NQT + NKT
HH = P // HD
VW = P + HH
MASKED = -1e9 / SCALE
NET = M // P + NEXP - 1
REG = M + P
RSTD, SHIFT, GATE, ATT_ROW, TOKEN = range(D, D + 5)
XW = D + 5
SLOTS = 3
NLN = NT + NGT
PIECE = 512
HI1, LO1, HI2, LO2 = range(4)
PIECES = 4
RAW = 3
EARLY = 5


class Chain:

    def __init__(self, eng, sem):
        self.eng, self.sem, self.n = eng, sem, 0

    def then(self, ins):
        self.n = self.n + 1
        ins.then_inc(self.sem, 1)
        self.eng.wait_ge(self.sem, self.n)


def build(nc, x, wqkv, bqkv, wproj, bproj, mapping, wr, br, w1, b1, w2, b2, out):
    sent = nc.dram_tensor("sent_rows", (NEXP * REG + P, XW), F32, kind="Internal").ap()
    vals = nc.dram_tensor("value_rows", (NKEY, D), F32, kind="Internal").ap()
    att_rows = nc.dram_tensor("attention_rows", (SEQ + 1, D), F32, kind="Internal").ap()
    x2 = x.rearrange("b m d -> (b m) d")
    out2 = out.rearrange("b m d -> (b m) d")

    with ExitStack() as ctx:
        ctx.enter_context(nc.allow_non_contiguous_dma(reason="short columns of the mapping and of biases"))

        def sb(name, shape, dt=F32):
            return ctx.enter_context(nc.sbuf_tensor(name, shape, dt))

        def sem(name):
            return ctx.enter_context(nc.semaphore(name))

        ident = sb("ident", [P, P])
        ident_h = sb("ident_h", [NQT, NQT], BF16)
        ones = sb("ones", [P, P])
        before = sb("before", [P, P])
        headmask = sb("headmask", [P, HH])
        headlow = sb("headlow", [P, HH])
        first_of = sb("first_of", [P, NEXP])
        restart = sb("restart", [P, NEXP, GT])
        minus_half = sb("minus_half", [P, NGT])
        region0 = sb("region0", [P, NEXP])
        key_step = sb("key_step", [P, 1], I32)
        part_i = sb("part_i", [P, 1], I32)
        part_f = sb("part_f", [P, 1])
        first_i = sb("first_i", [P, NEXP], I32)
        region_i = sb("region_i", [P, NEXP], I32)
        token_i = sb("token_i", [P, NT], I32)
        wproj_sb = sb("wproj_sb", [P, KD, D])
        wr_sb = sb("wr_sb", [P, KD, NEXP])
        bqk_col = sb("bqk_col", [P, 2 * KD])
        bproj_bc = sb("bproj_bc", [P, D])
        br_bc = sb("br_bc", [P, NEXP])
        b1_bc = sb("b1_bc", [P, NEXP, HID])
        raw = sb("raw", [P, RAW, PIECE])
        stats = sb("stats", [P, NLN, 6])
        mv = sb("mv", [P, NLN, 2])
        guess = sb("guess", [P, NLN])
        varp = sb("varp", [P, NLN])
        nt1 = sb("nt1", [P, NLN])
        nt2 = sb("nt2", [P, NLN])
        rstd = sb("rstd", [P, NGT])
        lg = sb("lg", [P, GT, NEXP])
        lgm = sb("lgm", [P, GT])
        lgd = sb("lgd", [P, GT, NEXP])
        lge = sb("lge", [P, GT, NEXP])
        lsum = sb("lsum", [P, GT])
        eqw = sb("eqw", [P, GT, NEXP])
        eqm = sb("eqm", [P, GT])
        onehot = sb("onehot", [P, NEXP, GT])
        rank = sb("rank", [P, NEXP, GT])
        cnt = sb("cnt", [P, NEXP])
        carry = sb("carry", [P, NEXP])
        offs = sb("offs", [P, NEXP])
        place = sb("place", [P, NEXP, GT])
        posf = sb("posf", [P, GT])
        pos = sb("pos", [P, NG, GT], I32)
        tab_i = sb("tab_i", [P, NEXP], I32)
        tab_n = sb("tab_n", [P, NEXP])
        tab_end = sb("tab_end", [P, NEXP])
        tab_start = sb("tab_start", [P, NEXP])
        tab_base = sb("tab_base", [P, NEXP])
        tab_a = sb("tab_a", [P, NEXP])
        tab_b = sb("tab_b", [P, NEXP])
        tab_e = sb("tab_e", [P, 1])
        tab_r = sb("tab_r", [P, 1])
        tab_u = sb("tab_u", [P, 1])
        tab_col = sb("tab_col", [P, 2])
        tab_row = sb("tab_row", [1, NET], I32)
        tab_exp = sb("tab_exp", [1, NET], I32)
        pad_row = sb("pad_row", [1, NEXP], I32)
        map_q = sb("map_q", [P, NQT], I32)
        map_b = sb("map_b", [P, NKT], I32)
        idx_a = sb("idx_a", [P, NKT], I32)
        idx_k = sb("idx_k", [P, NKT], I32)
        map_k = sb("map_k", [P, NKT], I32)
        row_k = sb("row_k", [P, NKT], I32)
        row_q = sb("row_q", [P, NQT], I32)
        map_row = sb("map_row", [NQT, P], I32)
        masked = sb("masked", [NQT, P], BF16)
        vmask = sb("vmask", [P, NKT])
        sc_max = sb("sc_max", [P, KD, 2])
        sc_bias = sb("sc_bias", [P, KD * 2])
        pr_sum = sb("pr_sum", [P, HEADS])
        pr_inv = sb("pr_inv", [P, HEADS])
        rows = [sb(f"rows{i}", [P, XW]) for i in range(SLOTS)]
        fxn = sb("fxn", [P, D])
        toki = sb("toki", [P, SLOTS, 2], I32)

        lent = ExitStack()

        def lend(name, shape, dt=F32):
            return lent.enter_context(nc.sbuf_tensor(name, shape, dt))

        KEEP = EARLY * 8 * PIECE + NT * XW + 8 * D + KD * 4 * P + NKT * D + D + XW - NEXP * 8 * PIECE
        assert KEEP >= 0
        lend("early_experts", [P, EARLY * 4 * 2 * PIECE])
        x_sb = lend("x_sb", [P, NT, XW])
        xn = lend("xn", [P, 2, 4, D])
        xT = lend("xT", [P, KD, 4 * P])
        vrow = lend("vrow", [P, NKT, D])
        bv_bc = lend("bv_bc", [P, D])
        zeros = lend("pad_rows", [P, XW])
        lent_key = lend("lent_key", [P, 4 * P + KD * NKEY])
        logT = lent_key[0:NEXP, 0:4 * P]
        xkT = lent_key[:, 4 * P:4 * P + KD * NKEY].rearrange("p (k n) -> p k n", k=KD)
        kbd = lent_key[:, 0:8 * P].rearrange("p (a k b n) -> p a k b n", a=2, k=KD, b=2)
        shared = lend("shared", [P, KD * NKB * VW])
        xg = shared[:, 0:NGT * D].rearrange("p (t d) -> p t d", t=NGT)
        vbd = shared[:, :].rearrange("p (k n j) -> p k n j", k=KD, n=NKB)
        xqT = lend("xqT", [P, KD, SEQ])
        kT = lend("kT", [P, KD, NKEY])
        wqkv_sb = lend("wqkv_sb", [P, KD, 3 * D])
        work = wqkv_sb[:, :, :].rearrange("p k n -> p (k n)")
        pr = work[:, 0:2 * D].rearrange("p (b k n) -> p b k n", b=2, k=KD)
        att = work[:, 2 * D:3 * D].rearrange("p (h d) -> p h d", h=HEADS)
        attT = work[:, 3 * D:4 * D].rearrange("p (k n) -> p k n", k=KD)
        att_out = work[:, 4 * D:6 * D].rearrange("p (b d) -> p b d", b=2)
        lent.close()

        w_sb = sb("w_sb", [P, NEXP, 4, 2 * PIECE], F32R)
        sb("kept_for_keys", [P, 4 * P + KD * NKEY + KEEP])
        fx_hi = [sb(f"fx_hi{i}", [P, KD, P], F32R) for i in range(SLOTS)]
        fx_lo = [sb(f"fx_lo{i}", [P, KD, P], F32R) for i in range(SLOTS)]
        hb = sb("hb", [P, HID])
        h_hi = sb("h_hi", [P, KH, P], F32R)
        h_lo = sb("h_lo", [P, KH, P], F32R)
        b2_bc = sb("b2_bc", [P, NEXP, D])
        res = [sb(f"res{i}", [P, GATE + 1]) for i in range(SLOTS)]
        yb = sb("yb", [P, D])
        yo = [sb(f"yo{i}", [P, D]) for i in range(SLOTS)]

        banks = [ctx.enter_context(nc.psum_tensor(f"bank{i}", [P, 512], F32)) for i in range(8)]
        ps_xt = banks[0:2]
        ps_lt, ps_lg, ps_cnt = banks[2], banks[3], banks[4]
        ps_a, ps_b, ps_c = banks[5], banks[6], banks[7]
        ps_misc = [ps_a, ps_b, ps_c]
        ps_scores, ps_att, ps_attT, ps_proj = [ps_a, ps_b], ps_c, banks[0], banks[1]
        ps_rows, ps_hidden, ps_hidT, ps_out = banks[2], banks[4], banks[3], banks[7]
        TAB0, TAB1 = 2 * NEXP, 2 * NEXP + NET

        s_const = sem("constants_ready")
        s_ident = sem("identity_ready")
        s_zero = sem("pad_rows_ready")
        s_pool = sem("pool_chain")
        s_dve = sem("vector_chain")
        s_attw = sem("attention_weights_loaded")
        s_rw = sem("router_weights_loaded")
        s_b1 = sem("hidden_biases_loaded")
        s_b2 = sem("output_biases_loaded")
        s_raw = [sem(f"weight_piece_loaded{i}") for i in range(RAW)]
        s_whi = sem("weight_piece_high")
        s_wlo = sem("weight_piece_low")
        s_x = [sem(f"x_group_loaded{g}") for g in range(NG)]
        s_map = sem("mapping_loaded")
        s_idx = sem("key_index_ready")
        s_mapk = sem("key_mapping_gathered")
        s_rowk = sem("key_row_index_ready")
        s_gath = sem("rows_gathered")
        s_var = sem("variance_ready")
        s_guess = sem("rstd_guess_ready")
        s_norm = sem("group_scale_shift_ready")
        s_gnorm = sem("gathered_normalised")
        s_xn = sem("quad_normalised")
        s_xt = sem("x_transposed")
        s_xtc = sem("x_transpose_copied")
        s_lt = sem("logits_ready")
        s_ltc = sem("logits_copied")
        s_lg = sem("logits_by_token")
        s_lgr = sem("logits_read")
        s_lgc = sem("logits_centred")
        s_lge = sem("logits_exp")
        s_cnt = sem("counts_ready")
        s_pre = sem("prefix_ready")
        s_preu = sem("prefix_used")
        s_pos = sem("positions_ready")
        s_sent = [sem(f"rows_sent{g}") for g in range(NG)]
        s_padr = sem("pad_places_ready")
        s_tabc = sem("table_columns_ready")
        s_tabp = sem("table_transposed")
        s_tab = sem("table_ready")
        s_pads = sem("pad_rows_written")
        s_gt = sem("gathered_transposed")
        s_gtc = sem("gathered_copied")
        s_qkv = sem("projection_ready")
        s_qkvc = sem("query_key_copied")
        s_vc = sem("value_copied")
        s_vst = sem("value_rows_stored")
        s_vm = sem("value_blocks_cleared")
        s_vz = sem("value_blocks_zeroed")
        s_vbd = sem("value_blocks_loaded")
        s_kbd = sem("key_blocks_ready")
        s_sc = sem("scores_ready")
        s_max = sem("scores_max_ready")
        s_bias = sem("exp_bias_ready")
        s_pr = sem("exp_ready")
        s_at = sem("attended")
        s_atn = sem("attended_normalised")
        s_att = sem("attended_transposed")
        s_atc = sem("attended_copied")
        s_y = sem("projected")
        s_z = sem("attention_rows_ready")
        s_zst = [sem(f"attention_rows_stored{i}") for i in range(2)]
        s_ld = [sem(f"expert_rows_loaded{i}") for i in range(SLOTS)]
        s_fn = sem("expert_rows_normalised")
        s_ft = sem("expert_rows_transposed")
        s_fh = sem("expert_rows_high")
        s_fl = sem("expert_rows_low")
        s_res = sem("expert_residual_copied")
        s_h = sem("hidden_ready")
        s_hb = sem("hidden_biased")
        s_ht = sem("hidden_transposed")
        s_hh = sem("hidden_high")
        s_hl = sem("hidden_low")
        s_fy = sem("expert_out_ready")
        s_tok = sem("token_index_ready")
        s_seen = sem("pool_saw_tile")
        s_yb = sem("expert_out_biased")
        s_zg = [sem(f"attention_row_added{i}") for i in range(SLOTS)]
        s_fo = sem("row_finished")
        s_out = [sem(f"rows_out{i}") for i in range(SLOTS)]

        NCONST = 9
        NQUAD = NT // 4
        ROUNDS = NET // SLOTS
        TILES = [NQT] + list(range(NQT))
        NPIECE = NEXP * PIECES
        NEARLY = EARLY * PIECES
        SPLIT = [2, 6, 12]
        assert sum(SPLIT) == NEARLY
        LATE = [0, 0, 2, 2, 2, 2, 2, 2, 0, 0, 0]
        assert sum(LATE) == NPIECE - NEARLY and len(LATE) == len(TILES) + 2

        def halves(j):
            if j == NQT:
                return [(slice(0, P), 0, NKB - 1)]
            return [(slice(BLOCK * b, BLOCK * (b + 1)), b, 2 * j + b) for b in range(2)]

        def score_part(i, k, b, r):
            at = (KD * b + k) * P
            return ps_scores[i % 2][:, at + r.start:at + r.stop]

        def parts_of(n):
            e, q = n // PIECES, n % PIECES
            hi = HI1 if q < 2 else HI2
            cols = slice((q % 2) * PIECE, (q % 2 + 1) * PIECE)
            return w_sb[:, e, hi, cols], w_sb[:, e, hi + 1, cols]

        block = ctx.enter_context(nc.Block())

        @block.sync
        def _(sp):
            block_first = mapping.rearrange("(c n q) -> c n q", n=P // KEYS, q=BLOCK)
            for c in range(2):
                sp.dma_start(map_b[:, c:c + 1], block_first[c, :, 0:1].to_broadcast([P // KEYS, KEYS])).then_inc(s_map, 16)
            sp.dma_start(map_b[:, 2:3], mapping[SEQ - 1:SEQ].unsqueeze(0).to_broadcast([P, 1])).then_inc(s_map, 16)
            sp.dma_start(map_row[:, :], mapping.rearrange("(t p) -> t p", p=P)).then_inc(s_map, 16)
            sp.dma_start(map_q[:, :], mapping.rearrange("(t p) -> p t", p=P)).then_inc(s_map, 16)
            x_t = x2.rearrange("(g t p) d -> g p t d", g=NG, p=P)
            for g in range(NG):
                sp.dma_start(x_sb[:, g * GT:(g + 1) * GT, 0:D], x_t[g]).then_inc(s_x[g], 16)
                if g == 0:
                    sp.dma_start(wr_sb[:, :, :], wr.rearrange("(k p) e -> p k e", p=P)).then_inc(s_rw, 16)
                    sp.dma_start(br_bc[:, :], br.unsqueeze(0).to_broadcast([P, NEXP])).then_inc(s_rw, 16)

            sp.wait_ge(s_gath, 16 * NGT)
            sp.dma_start(wqkv_sb[:, :, :], wqkv.rearrange("(k p) n -> p k n", p=P)).then_inc(s_attw, 16)
            sp.dma_start(bqk_col[:, :], bqkv[0:2 * D].rearrange("(c p) -> p c", p=P)).then_inc(s_attw, 16)
            sp.dma_start(bv_bc[:, :], bqkv[2 * D:3 * D].unsqueeze(0).to_broadcast([P, D])).then_inc(s_attw, 16)
            sp.dma_start(wproj_sb[:, :, :], wproj.rearrange("(k p) n -> p k n", p=P)).then_inc(s_attw, 16)
            sp.dma_start(bproj_bc[:, :], bproj.unsqueeze(0).to_broadcast([P, D])).then_inc(s_attw, 16)

            def load_piece(n):
                e, q = n // PIECES, n % PIECES
                if n >= RAW:
                    sp.wait_ge(s_wlo, n - RAW + 1)
                dst = raw[:, n % RAW, :]
                if q < 2:
                    sp.dma_start(dst, w1[e, q * P:(q + 1) * P, :]).then_inc(s_raw[n % RAW], 16)
                else:
                    src = w2[e].rearrange("(k p) n -> p k n", p=P)[:, 2 * (q - 2):2 * (q - 1), :]
                    sp.dma_start(dst.rearrange("p (k n) -> p k n", k=2), src).then_inc(s_raw[n % RAW], 16)

            for n in range(8):
                load_piece(n)
            sp.wait_ge(s_vc, NKT)
            sp.dma_start(vals[0:2 * P, :].rearrange("(t p) d -> p t d", p=P), vrow[:, 0:2, :]).then_inc(s_vst, 16)
            sp.dma_start(vals[2 * P:NKEY, :], vrow[0:LASTK, 2, :]).then_inc(s_vst, 16)
            for n in range(8, 10):
                load_piece(n)
            sp.wait_ge(s_vst, 32)
            sp.wait_ge(s_vz, 1)
            v_src = vals.rearrange("(n s) (k h d) -> k h s n d", s=KEYS, k=KD, h=HH)
            for k in range(KD):
                for h in range(HH):
                    sp.dma_start(vbd[h * HD:(h + 1) * HD, k, :, h * HD:(h + 1) * HD], v_src[k, h]).then_inc(s_vbd, 16)
            for n in range(10, NEARLY):
                load_piece(n)
            sp.dma_start(b1_bc[:, :, :], b1.unsqueeze(0).to_broadcast([P, NEXP, HID])).then_inc(s_b1, 16)

            sp.wait_ge(s_zero, 1)
            sp.dma_start(sent[NEXP * REG:NEXP * REG + P, :], zeros[:, :]).then_inc(s_pads, 16)
            sp.wait_ge(s_padr, 1)
            for e in range(NEXP):
                first_pad = sp.value_load(pad_row[0:1, e:e + 1], min_val=e * REG, max_val=e * REG + M)
                sp.dma_start(sent[bass.ds(first_pad, P), :], zeros[:, :]).then_inc(s_pads, 16)

            for n in range(NEARLY, NPIECE):
                load_piece(n)

            for g in range(NG):
                sp.wait_ge(s_sent[g], 16 * GT)
            sp.wait_ge(s_pads, 16 * (NEXP + 1))
            sp.wait_ge(s_tab, 1)

            def load(t, slot):
                row = sp.value_load(tab_row[0:1, bass.ds(t, 1)], min_val=0, max_val=NEXP * REG)
                sp.dma_start(rows[slot][:, :], sent[bass.ds(row, P), :]).then_inc(s_ld[slot], 16)

            for slot in range(SLOTS):
                load(slot, slot)
            sp.wait_ge(s_z, len(TILES))
            sp.dma_start(b2_bc[:, :, :], b2.unsqueeze(0).to_broadcast([P, NEXP, D])).then_inc(s_b2, 16)
            with sp.Fori(1, ROUNDS) as r:
                for slot in range(SLOTS):
                    sp.wait_ge(s_fn, (r - 1) * SLOTS + slot + 1)
                    sp.wait_ge(s_res, (r - 1) * SLOTS + slot + 1)
                    sp.wait_ge(s_tok, (r - 1) * SLOTS + slot + 1)
                    load(r * SLOTS + slot, slot)

        @block.gpsimd
        def _(pool):
            ch = Chain(pool, s_pool)
            ch.then(pool.memset(ones[:, :], 1.0))
            pool.affine_select(out=ident[:, :], in_=ones[:, :], pattern=[[-1, P]], compare_op=ALU.is_equal,
                               fill=0.0, base=0, channel_multiplier=1).then_inc(s_ident, 1)
            pool.iota(part_i[:, :], pattern=[[0, 1]], base=0, channel_multiplier=1).then_inc(s_const, 1)
            pool.iota(first_i[:, :], pattern=[[-1, NEXP]], base=NEXP, channel_multiplier=0).then_inc(s_const, 1)
            pool.iota(region_i[:, :], pattern=[[REG, NEXP]], base=-1, channel_multiplier=0).then_inc(s_const, 1)
            pool.iota(token_i[:, :], pattern=[[P, NT]], base=0, channel_multiplier=1).then_inc(s_const, 1)
            pool.affine_select(out=before[:, :], in_=ones[:, :], pattern=[[1, P]], compare_op=ALU.is_gt,
                               fill=0.0, base=0, channel_multiplier=-1).then_inc(s_const, 1)
            ch.then(pool.affine_select(out=headlow[:, :], in_=ones[:, 0:HH], pattern=[[-HD, HH]], compare_op=ALU.is_ge,
                                       fill=0.0, base=0, channel_multiplier=1))
            pool.affine_select(out=headmask[:, :], in_=headlow[:, :], pattern=[[HD, HH]], compare_op=ALU.is_gt,
                               fill=0.0, base=HD, channel_multiplier=-1).then_inc(s_const, 1)
            pool.memset(restart[:, :, 1:GT], 1.0).then_inc(s_const, 1)
            pool.memset(restart[:, :, 0:1], 0.0).then_inc(s_const, 1)
            pool.memset(minus_half[:, :], -0.5).then_inc(s_const, 1)
            ch.then(pool.memset(zeros[:, :], 0.0))
            pool.iota(zeros[:, :].bitcast(I32)[:, TOKEN:TOKEN + 1], pattern=[[0, 1]], base=M,
                      channel_multiplier=0).then_inc(s_zero, 1)

            pool.wait_ge(s_idx, 1)
            table = mapping.unsqueeze(1)
            for c in range(NKT):
                n = P if c < 2 else LASTK
                pool.indirect_dma_start(out=map_k[0:n, c:c + 1], out_offset=None, in_=table,
                                        in_offset=bass.IndirectOffsetOnAxis(ap=idx_k[0:n, c:c + 1], axis=0),
                                        bounds_check=SEQ - 1, oob_is_err=False).then_inc(s_mapk, 16)

            def rstd_guess(count, at, n):
                pool.wait_ge(s_var, count)
                pool.tensor_tensor(guess[:, at:at + n], varp[:, at:at + n], minus_half[:, 0:n], ALU.pow).then_inc(s_guess, 1)

            def gather(tile, index, n):
                pool.indirect_dma_start(out=xg[0:n, tile, :], out_offset=None, in_=x2,
                                        in_offset=bass.IndirectOffsetOnAxis(ap=index, axis=0),
                                        bounds_check=M - 1, oob_is_err=False).then_inc(s_gath, 16)

            def send(g):
                pool.wait_ge(s_pos, g + 1)
                for t in range(GT):
                    pool.indirect_dma_start(out=sent, in_=x_sb[:, g * GT + t, :], in_offset=None,
                                            out_offset=bass.IndirectOffsetOnAxis(ap=pos[:, g, t:t + 1], axis=0),
                                            bounds_check=NEXP * REG + P - 1, oob_is_err=False).then_inc(s_sent[g], 16)

            rstd_guess(1, 0, GT)
            for t in range(NQT):
                gather(t, row_q[:, t:t + 1], P)
                if t == 3:
                    rstd_guess(2, GT, GT)
            pool.wait_ge(s_rowk, 1)
            for c in range(NKT):
                n = P if c < 2 else LASTK
                gather(NQT + c, row_k[0:n, c:c + 1], n)
            rstd_guess(3, 2 * GT, GT)
            rstd_guess(4, 3 * GT, GT)
            rstd_guess(5, NT, NGT)
            pool.wait_ge(s_gt, NGT)
            pool.memset(shared[:, :], 0.0).then_inc(s_vm, 1)
            for g in range(NG):
                send(g)

            for i, j in enumerate(TILES):
                pool.wait_ge(s_z, i + 1)
                if j == NQT:
                    pool.dma_start(att_rows[SEQ:SEQ + 1, :], att_out[0:1, i % 2, :]).then_inc(s_zst[i % 2], 16)
                else:
                    pool.dma_start(att_rows[j * P:(j + 1) * P, :], att_out[:, i % 2, :]).then_inc(s_zst[i % 2], 16)
            pool.wait_ge(s_zst[0], 16 * 5)
            pool.wait_ge(s_zst[1], 16 * 4)
            last_row = pool.to_reg(M - 1)
            last_att = pool.to_reg(SEQ)

            def await_tile(sem_, tile):
                pool.wait_ge(sem_, tile + 1)
                pool.sem_inc(s_seen, 1)

            def fetch(slot, tile):
                await_tile(s_tok, tile)
                await_tile(s_res, tile)
                pool.indirect_dma_start(out=res[slot][:, 0:D], out_offset=None, in_=att_rows,
                                        in_offset=bass.IndirectOffsetOnAxis(ap=toki[:, slot, 0:1], axis=0),
                                        bounds_check=last_att, oob_is_err=True,
                                        compute_op=ALU.add).then_inc(s_zg[slot], 16)

            def write(slot, tile):
                await_tile(s_fo, tile)
                pool.indirect_dma_start(out=out2, in_=yo[slot][:, :], in_offset=None,
                                        out_offset=bass.IndirectOffsetOnAxis(ap=toki[:, slot, 1:2], axis=0),
                                        bounds_check=last_row, oob_is_err=False).then_inc(s_out[slot], 16)

            fetch(0, 0)
            with pool.Fori(0, ROUNDS - 1) as r:
                for slot in range(SLOTS):
                    fetch((slot + 1) % SLOTS, r * SLOTS + slot + 1)
                    write(slot, r * SLOTS + slot)
            for slot in range(SLOTS):
                t = (ROUNDS - 1) * SLOTS + slot
                if slot + 1 < SLOTS:
                    fetch(slot + 1, t + 1)
                write(slot, t)
            for slot in range(SLOTS):
                pool.wait_ge(s_out[slot], 16 * ROUNDS)

        @block.scalar
        def _(act):
            split = [0]

            def high_parts(count):
                for _ in range(count):
                    n = split[0]
                    act.wait_ge(s_raw[n % RAW], 16 * (n // RAW + 1))
                    if n == NEARLY:
                        for g in range(NG):
                            act.wait_ge(s_sent[g], 16 * GT)
                    if n == (NEXP - 1) * PIECES:
                        act.wait_ge(s_lt, NQUAD)
                        act.wait_ge(s_vst, 32)
                        act.wait_ge(s_pads, 16 * (NEXP + 1))
                    nc.scalar.activation(parts_of(n)[0], raw[:, n % RAW, :], ACT.Copy).then_inc(s_whi, 1)
                    split[0] = n + 1

            def normalise(u):
                act.wait_ge(s_norm, u // 2 + 1)
                if u >= 2:
                    act.wait_ge(s_xt, 2 * (u - 1))
                for t in range(4):
                    row = x_sb[:, 4 * u + t, :]
                    ins = nc.scalar.activation(xn[:, u % 2, t, :], row[:, 0:D], ACT.Identity,
                                               bias=row[:, SHIFT:SHIFT + 1], scale=row[:, RSTD:RSTD + 1])
                ins.then_inc(s_xn, 1)

            def rows_copies(u):
                for b in range(2):
                    act.wait_ge(s_xt, 2 * u + b + 1)
                    if u >= 1 and b == 0:
                        act.wait_ge(s_lt, u)
                    nc.scalar.activation(xT[:, :, b * 2 * P:(b + 1) * 2 * P].rearrange("p k (t n) -> p t k n", t=2),
                                         ps_xt[b][:, :].rearrange("p (t k n) -> p t k n", t=2, k=KD),
                                         ACT.Copy).then_inc(s_xtc, 1)

            def logits_copy(u):
                act.wait_ge(s_lt, u + 1)
                if u >= 1:
                    act.wait_ge(s_lg, u)
                nc.scalar.activation(logT, ps_lt[0:NEXP, :], ACT.Copy).then_inc(s_ltc, 1)

            def logits_exp(g):
                act.wait_ge(s_lgc, g + 1)
                nc.scalar.activation(lge[:, :, :], lgd[:, :, :], ACT.Exp).then_inc(s_lge, 1)

            def router(first, count):
                normalise(first)
                for u in range(first, first + count):
                    if u % 2 == 0:
                        normalise(u + 1)
                    rows_copies(u)
                    if u > first:
                        logits_copy(u - 1)
                    if u % 2 == 1 and u + 1 < first + count:
                        normalise(u + 1)
                logits_copy(first + count - 1)

            def gathered():
                for i in range(NGT):
                    act.wait_ge(s_gt, i + 1)
                    n = LASTK if i == NGT - 1 else P
                    dst = xqT[:, :, i * P:i * P + n] if i < NQT else xkT[:, :, (i - NQT) * P:(i - NQT) * P + n]
                    src = ps_misc[i % 3][:, 0:KD * P].rearrange("p (k n) -> p k n", k=KD)[:, :, 0:n]
                    nc.scalar.activation(dst, src, ACT.Copy).then_inc(s_gtc, 1)

            def projections():
                act.wait_ge(s_attw, 16 * 5)
                for c in range(KD):
                    act.wait_ge(s_qkv, c + 1)
                    nc.scalar.activation(kT[:, c, :], ps_misc[c][:, 0:NKEY], ACT.Identity,
                                         bias=bqk_col[:, KD + c:KD + c + 1]).then_inc(s_qkvc, 1)
                for half in range(2):
                    act.wait_ge(s_qkv, KD + NKT + 2 * half + 2)
                    for c in range(KD):
                        nc.scalar.activation(xqT[:, c, half * 512:(half + 1) * 512], ps_misc[c][:, :], ACT.Identity,
                                             bias=bqk_col[:, c:c + 1]).then_inc(s_qkvc, 1)

            router(0, 4)
            logits_exp(0)
            logits_exp(1)
            gathered()
            high_parts(SPLIT[0])
            projections()
            high_parts(SPLIT[1])
            router(4, 4)
            logits_exp(2)
            logits_exp(3)
            high_parts(SPLIT[2])

            for step in range(len(TILES) + 2):
                if step < len(TILES):
                    act.wait_ge(s_bias, step + 1)
                    if step >= 2:
                        act.wait_ge(s_at, step - 1)
                    for k in range(KD):
                        for r, b, n in halves(TILES[step]):
                            ins = nc.scalar.activation(pr[:, step % 2, k, r], score_part(step, k, b, r), ACT.Exp,
                                                       bias=sc_bias[:, 2 * k + b:2 * k + b + 1], scale=SCALE)
                    ins.then_inc(s_pr, 1)
                if step >= 2:
                    act.wait_ge(s_att, step - 1)
                    nc.scalar.activation(attT[:, :, :], ps_attT[:, 0:D].rearrange("p (k n) -> p k n", k=KD),
                                         ACT.Copy).then_inc(s_atc, 1)
                high_parts(LATE[step])

            def normal_rows(tile, slot, rnd, early=False):
                act.wait_ge(s_ld[slot], 16 * rnd + 16)
                if not early:
                    act.wait_ge(s_ft, tile)
                nc.scalar.activation(fxn[:, :], rows[slot][:, 0:D], ACT.Identity,
                                     bias=rows[slot][:, SHIFT:SHIFT + 1],
                                     scale=rows[slot][:, RSTD:RSTD + 1]).then_inc(s_fn, 1)

            def residual(tile, slot, early=False):
                if not early:
                    act.wait_ge(s_fo, tile - 2)
                nc.scalar.activation(res[slot][:, :], rows[slot][:, 0:GATE + 1], ACT.Copy).then_inc(s_res, 1)

            def rows_high(tile, slot, early=False):
                act.wait_ge(s_ft, tile + 1)
                if not early:
                    act.wait_ge(s_h, tile - 2)
                nc.scalar.activation(fx_hi[slot][:, :, :], ps_rows[:, 0:D].rearrange("p (k n) -> p k n", k=KD),
                                     ACT.Copy).then_inc(s_fh, 1)

            def hidden_high(tile, early=False):
                act.wait_ge(s_ht, tile + 1)
                if not early:
                    act.wait_ge(s_fy, tile)
                nc.scalar.activation(h_hi[:, :, :], ps_hidT[:, :].rearrange("p (k n) -> p k n", k=KH),
                                     ACT.Relu).then_inc(s_hh, 1)

            def step(rnd, slot, first_round=False, last_round=False):
                t = rnd * SLOTS + slot
                left = NET if not last_round else SLOTS - slot
                if not (first_round and slot == 0):
                    hidden_high(t - 1, early=first_round and slot == 1)
                if left > 1:
                    nxt, nrnd = (slot + 1) % SLOTS, rnd + (slot + 1 == SLOTS)
                    rows_high(t + 1, nxt, early=first_round and slot < 2)
                    if left > 2:
                        normal_rows(t + 2, (slot + 2) % SLOTS, rnd + (slot + 2 >= SLOTS))
                    residual(t + 1, nxt, early=first_round and slot < 2)

            normal_rows(0, 0, 0, early=True)
            act.wait_ge(s_y, len(TILES))
            act.wait_ge(s_z, len(TILES))
            rows_high(0, 0, early=True)
            normal_rows(1, 1, 0)
            residual(0, 0, early=True)
            for slot in range(SLOTS):
                step(0, slot, first_round=True)
            with act.Fori(1, ROUNDS - 1) as r:
                for slot in range(SLOTS):
                    step(r, slot)
            for slot in range(SLOTS):
                step(ROUNDS - 1, slot, last_round=True)
            hidden_high(NET - 1)

        @block.vector
        def _(dve):
            ch = Chain(dve, s_dve)
            v = nc.vector
            split = [0]

            def low_parts(count):
                for _ in range(count):
                    n = split[0]
                    hi, lo = parts_of(n)
                    dve.wait_ge(s_raw[n % RAW], 16 * (n // RAW + 1))
                    dve.wait_ge(s_whi, n + 1)
                    v.tensor_tensor(lo, raw[:, n % RAW, :], hi.bitcast(F32), ALU.subtract).then_inc(s_wlo, 1)
                    split[0] = n + 1

            dve.wait_ge(s_const, NCONST)
            ch.then(v.tensor_scalar(key_step[:, :], part_i[:, :], KEYS - 1, 2, ALU.bitwise_and, ALU.logical_shift_left))
            dve.wait_ge(s_map, 80)
            ch.then(v.tensor_scalar(idx_a[:, :], map_b[:, :], -SEG, None, ALU.bitwise_and))
            ch.then(v.tensor_tensor(idx_a[:, :], idx_a[:, :], key_step[:, :].to_broadcast([P, NKT]), ALU.bitwise_or))
            v.tensor_scalar(row_q[:, :], map_q[:, :], M - 1, None, ALU.min)
            v.tensor_scalar(idx_k[:, :], idx_a[:, :], SEQ - 1, None, ALU.min).then_inc(s_idx, 1)
            v.tensor_scalar(masked[:, :], map_row[:, :], M, MASKED, ALU.is_ge, ALU.mult)
            v.tensor_scalar(vmask[:, :], map_b[:, :], M, None, ALU.is_lt)
            v.tensor_copy(first_of[:, :], first_i[:, :])
            v.tensor_copy(part_f[:, :], part_i[:, :])
            v.tensor_copy(region0[:, :], region_i[:, :])
            v.tensor_copy(carry[:, :], region_i[:, :])
            dve.wait_ge(s_ident, 1)
            v.tensor_copy(ident_h[:, :], ident[0:NQT, 0:NQT])
            x_bits = x_sb[:, :, :].bitcast(I32)
            v.tensor_scalar(x_bits[:, :, ATT_ROW], token_i[:, :], SEQ, None, ALU.min)
            v.tensor_copy(x_bits[:, :, TOKEN], token_i[:, :])
            ch.then(v.memset(mv[:, :, :], 0.0))

            def moments(rows_of, at, n):
                for i in range(n):
                    pn = LASTK if at + i == NLN - 1 else P
                    ins = v.bn_stats(stats[0:pn, at + i, :], rows_of(i))
                ch.then(ins)
                for i in range(n):
                    pn = LASTK if at + i == NLN - 1 else P
                    ins = v.bn_aggr(mv[0:pn, at + i, :], stats[0:pn, at + i, :])
                ch.then(ins)
                v.tensor_scalar(varp[:, at:at + n], mv[:, at:at + n, 1], LN_EPS, None, ALU.add).then_inc(s_var, 1)

            def refine(out_, at, n, count):
                c = slice(at, at + n)
                dve.wait_ge(s_guess, count)
                ch.then(v.tensor_tensor(nt1[:, c], guess[:, c], guess[:, c], ALU.mult))
                ch.then(v.tensor_tensor(nt2[:, c], nt1[:, c], varp[:, c], ALU.mult))
                ch.then(v.tensor_scalar(nt1[:, c], nt2[:, c], -0.5, 1.5, ALU.mult, ALU.add))
                ch.then(v.tensor_tensor(out_, guess[:, c], nt1[:, c], ALU.mult))

            def group_moments(g):
                dve.wait_ge(s_x[g], 16)
                moments(lambda i: x_sb[:, g * GT + i, 0:D], g * GT, GT)

            def group_scale(g):
                tiles = slice(g * GT, (g + 1) * GT)
                refine(x_sb[:, tiles, RSTD], g * GT, GT, g + 1)
                v.scalar_tensor_tensor(out=x_sb[:, tiles, SHIFT], in0=mv[:, tiles, 0], scalar=-1.0,
                                       in1=x_sb[:, tiles, RSTD], op0=ALU.mult, op1=ALU.mult).then_inc(s_norm, 1)

            def gathered_row(i):
                return xg[0:LASTK if i == NGT - 1 else P, i, :]

            def route(g):
                tiles = slice(g * GT, (g + 1) * GT)
                dve.wait_ge(s_lg, 2 * g + 2)
                v.tensor_tensor(lg[:, :, :], ps_lg[:, g * GT * NEXP:(g + 1) * GT * NEXP].rearrange("p (t e) -> p t e", t=GT),
                                br_bc[:, :].unsqueeze(1).to_broadcast([P, GT, NEXP]), ALU.add).then_inc(s_lgr, 1)
                dve.wait_ge(s_lgr, g + 1)
                ch.then(v.tensor_reduce(lgm[:, :], lg[:, :, :], AX.X, ALU.max))
                v.tensor_tensor(lgd[:, :, :], lg[:, :, :], lgm[:, :].unsqueeze(2).to_broadcast([P, GT, NEXP]),
                                ALU.subtract).then_inc(s_lgc, 1)
                dve.wait_ge(s_lgc, g + 1)
                ch.then(v.scalar_tensor_tensor(out=eqw[:, :, :], in0=lgd[:, :, :], scalar=0.0,
                                               in1=first_of[:, :].unsqueeze(1).to_broadcast([P, GT, NEXP]),
                                               op0=ALU.is_ge, op1=ALU.mult))
                ch.then(v.tensor_reduce(eqm[:, :], eqw[:, :, :], AX.X, ALU.max))
                ch.then(v.tensor_tensor(onehot[:, :, :].rearrange("p e t -> p t e"), eqw[:, :, :],
                                        eqm[:, :].unsqueeze(2).to_broadcast([P, GT, NEXP]), ALU.is_equal))
                ch.then(v.tensor_tensor_scan(rank[:, :, :].rearrange("p e t -> p (e t)"),
                                             restart[:, :, :].rearrange("p e t -> p (e t)"),
                                             onehot[:, :, :].rearrange("p e t -> p (e t)"), 0.0, ALU.mult, ALU.add))
                v.tensor_copy(cnt[:, :], rank[:, :, GT - 1]).then_inc(s_cnt, 1)
                dve.wait_ge(s_lge, g + 1)
                ch.then(v.tensor_reduce(lsum[:, :], lge[:, :, :], AX.X, ALU.add))
                v.reciprocal(x_sb[:, tiles, GATE], lsum[:, :])
                dve.wait_ge(s_pre, g + 1)
                ch.then(v.tensor_tensor(offs[:, :], ps_cnt[:, 0:NEXP], carry[:, :], ALU.add))
                v.tensor_tensor(carry[:, :], ps_cnt[:, NEXP:2 * NEXP], carry[:, :], ALU.add).then_inc(s_preu, 1)
                ch.then(v.tensor_tensor(place[:, :, :], rank[:, :, :], offs[:, :].unsqueeze(2).to_broadcast([P, NEXP, GT]),
                                        ALU.add))
                ch.then(v.tensor_tensor(place[:, :, :], place[:, :, :], onehot[:, :, :], ALU.mult))
                ch.then(v.tensor_reduce(posf[:, :], place[:, :, :].rearrange("p e t -> p t e"), AX.X, ALU.add))
                v.tensor_copy(pos[:, g, :], posf[:, :]).then_inc(s_pos, 1)

            def tile_table():
                dve.wait_ge(s_preu, NG)
                v.tensor_scalar(pad_row[:, :], carry[0:1, :], 1.0, None, ALU.add).then_inc(s_padr, 1)
                ch.then(v.tensor_tensor(tab_n[:, :], carry[:, :], region0[:, :], ALU.subtract))
                ch.then(v.tensor_scalar(tab_i[:, :], tab_n[:, :], float(P - 1), None, ALU.add))
                ch.then(v.tensor_scalar(tab_i[:, :], tab_i[:, :], 7, None, ALU.logical_shift_right))
                ch.then(v.tensor_copy(tab_n[:, :], tab_i[:, :]))
                ch.then(v.tensor_tensor_scan(tab_end[:, :], ones[:, 0:NEXP], tab_n[:, :], 0.0, ALU.mult, ALU.add))
                ch.then(v.tensor_tensor(tab_start[:, :], tab_end[:, :], tab_n[:, :], ALU.subtract))
                ch.then(v.scalar_tensor_tensor(out=tab_base[:, :], in0=tab_start[:, :], scalar=-float(P),
                                               in1=region0[:, :], op0=ALU.mult, op1=ALU.add))
                v.tensor_scalar(tab_base[:, :], tab_base[:, :], 1.0, None, ALU.add)
                tile = part_f[:, :].to_broadcast([P, NEXP])
                ch.then(v.tensor_tensor(tab_a[:, :], tab_end[:, :], tile, ALU.is_le))
                v.tensor_reduce(tab_e[:, :], tab_a[:, :], AX.X, ALU.add)
                ch.then(v.tensor_tensor(tab_b[:, :], tab_start[:, :], tile, ALU.is_le))
                ch.then(v.tensor_tensor(tab_a[:, :], tab_b[:, :], tab_a[:, :], ALU.subtract))
                ch.then(v.scalar_tensor_tensor(out=tab_b[:, :], in0=tile, scalar=float(P), in1=tab_base[:, :],
                                               op0=ALU.mult, op1=ALU.add))
                ch.then(v.tensor_tensor(tab_a[:, :], tab_b[:, :], tab_a[:, :], ALU.mult))
                v.tensor_reduce(tab_r[:, :], tab_a[:, :], AX.X, ALU.add)
                ch.then(v.tensor_scalar(tab_u[:, :], tab_e[:, :], float(NEXP), float(NEXP * REG), ALU.is_ge, ALU.mult))
                v.tensor_scalar(tab_col[:, 1:2], tab_e[:, :], float(NEXP - 1), None, ALU.min)
                v.tensor_tensor(tab_col[:, 0:1], tab_r[:, :], tab_u[:, :], ALU.add).then_inc(s_tabc, 1)

            group_moments(0)
            group_moments(1)
            group_scale(0)
            dve.wait_ge(s_mapk, 16 * NKT)
            for c in range(NKT):
                n = P if c < 2 else LASTK
                ins = v.tensor_scalar(row_k[0:n, c:c + 1], map_k[0:n, c:c + 1], M - 1, None, ALU.min)
            ins.then_inc(s_rowk, 1)
            group_scale(1)
            group_moments(2)
            group_moments(3)
            group_scale(2)
            group_scale(3)
            route(0)
            route(1)
            dve.wait_ge(s_gath, 16 * NGT)
            moments(gathered_row, NT, NGT)
            refine(rstd[:, :], NT, NGT, NG + 1)
            for i in range(NGT):
                pn = LASTK if i == NGT - 1 else P
                v.tensor_scalar(gathered_row(i), gathered_row(i), mv[0:pn, NT + i, 0:1], rstd[0:pn, i:i + 1],
                                ALU.subtract, ALU.mult).then_inc(s_gnorm, 1)
            low_parts(SPLIT[0])
            dve.wait_ge(s_attw, 16 * 5)
            for c in range(NKT):
                n = P if c < 2 else LASTK
                dve.wait_ge(s_qkv, KD + c + 1)
                ch.then(v.tensor_tensor(vrow[0:n, c, :], ps_misc[(KD + c) % 3][0:n, 0:D], bv_bc[0:n, :], ALU.add))
                v.tensor_scalar(vrow[0:n, c, :], vrow[0:n, c, :], vmask[0:n, c:c + 1], None, ALU.mult).then_inc(s_vc, 1)
            dve.wait_ge(s_vm, 1)
            v.tensor_copy(vbd[:, :, :, P:VW], headmask[:, :].unsqueeze(1).unsqueeze(1)
                          .to_broadcast([P, KD, NKB, HH])).then_inc(s_vz, 1)
            low_parts(SPLIT[1])
            route(2)
            route(3)
            tile_table()
            low_parts(SPLIT[2])

            def key_blocks(i):
                j = TILES[i]
                if i >= 2:
                    dve.wait_ge(s_sc, i - 1)
                for k in range(KD):
                    for b, n in enumerate([NKB - 1] if j == NQT else [2 * j, 2 * j + 1]):
                        ins = v.tensor_tensor(kbd[:, i % 2, k, b, :].rearrange("p (h s) -> p h s", h=HH),
                                              kT[:, k, n * KEYS:(n + 1) * KEYS].unsqueeze(1).to_broadcast([P, HH, KEYS]),
                                              headmask[:, :].unsqueeze(2).to_broadcast([P, HH, KEYS]), ALU.mult)
                ins.then_inc(s_kbd, 1)

            ch.then(v.memset(sc_max[:, :, :], 0.0))
            dve.wait_ge(s_qkvc, KD)
            dve.wait_ge(s_qkv, KD + NKT)
            dve.wait_ge(s_lg, NQUAD)
            key_blocks(0)
            for step in range(len(TILES) + 2):
                if step + 1 < len(TILES):
                    key_blocks(step + 1)
                if step < len(TILES):
                    dve.wait_ge(s_sc, step + 1)
                    if step >= 1:
                        dve.wait_ge(s_bias, step)
                    for r, b, n in halves(TILES[step]):
                        src = ps_scores[step % 2][:, KD * b * P:KD * (b + 1) * P].rearrange("p (k n) -> p k n", k=KD)
                        ins = v.tensor_reduce(sc_max[:, :, b], src[:, :, r], AX.X, ALU.max)
                    ins.then_inc(s_max, 1)
                    dve.wait_ge(s_max, step + 1)
                    if step >= 1:
                        dve.wait_ge(s_pr, step)
                    v.tensor_scalar(sc_bias[:, :], sc_max[:, :, :].rearrange("p k b -> p (k b)"), -SCALE, None,
                                    ALU.mult).then_inc(s_bias, 1)
                if 1 <= step <= len(TILES):
                    dve.wait_ge(s_at, step)
                    got = ps_att[:, 0:KD * VW].rearrange("p (k j) -> p k j", k=KD)
                    ch.then(v.tensor_scalar(pr_sum[:, :].rearrange("p (k h) -> p k h", k=KD), got[:, :, P:VW], SUM_EPS, None,
                                            ALU.add))
                    ch.then(v.reciprocal(pr_inv[:, :], pr_sum[:, :]))
                    if step >= 2:
                        dve.wait_ge(s_att, step - 1)
                    for k in range(KD):
                        ins = v.tensor_tensor(att[:, k * HH:(k + 1) * HH, :], got[:, k, 0:P].rearrange("p (h d) -> p h d", h=HH),
                                              pr_inv[:, k * HH:(k + 1) * HH].unsqueeze(2).to_broadcast([P, HH, HD]), ALU.mult)
                    ins.then_inc(s_atn, 1)
                if step >= 2:
                    i = step - 2
                    dve.wait_ge(s_y, i + 1)
                    if i >= 2:
                        dve.wait_ge(s_zst[i % 2], 16 * (i // 2))
                    v.tensor_tensor(att_out[:, i % 2, :], ps_proj[:, 0:D], bproj_bc[:, :], ALU.add).then_inc(s_z, 1)
                if step == 1:
                    dve.wait_ge(s_tabp, 1)
                    v.tensor_copy(tab_row[:, :], ps_cnt[0:1, TAB0:TAB0 + NET])
                    v.tensor_copy(tab_exp[:, :], ps_cnt[0:1, TAB1:TAB1 + NET]).then_inc(s_tab, 1)
                low_parts(LATE[step])

            def rows_low(tile, slot):
                dve.wait_ge(s_fh, tile + 1)
                v.tensor_tensor(fx_lo[slot][:, :, :], ps_rows[:, 0:D].rearrange("p (k n) -> p k n", k=KD),
                                fx_hi[slot][:, :, :].bitcast(F32), ALU.subtract).then_inc(s_fl, 1)

            def hidden_low(tile):
                dve.wait_ge(s_hh, tile + 1)
                v.scalar_tensor_tensor(out=h_lo[:, :, :], in0=ps_hidT[:, :].rearrange("p (k n) -> p k n", k=KH), scalar=0.0,
                                       in1=h_hi[:, :, :].bitcast(F32), op0=ALU.max, op1=ALU.subtract).then_inc(s_hl, 1)

            def tokens(tile, slot, rnd, reused=True):
                dve.wait_ge(s_ld[slot], 16 * rnd + 16)
                if reused:
                    dve.wait_ge(s_out[slot], 16 * rnd)
                v.tensor_copy(toki[:, slot, :], rows[slot][:, :].bitcast(I32)[:, ATT_ROW:TOKEN + 1]).then_inc(s_tok, 1)

            def expert_of(tile):
                return dve.value_load(tab_exp[0:1, bass.ds(tile, 1)], min_val=0, max_val=NEXP - 1)

            def hidden_bias(tile, early=False):
                e = expert_of(tile)
                dve.wait_ge(s_h, tile + 1)
                if not early:
                    dve.wait_ge(s_ht, tile)
                v.tensor_tensor(hb[:, :], ps_hidden[:, :], b1_bc[:, bass.ds(e, 1), :].rearrange("p a n -> p (a n)"),
                                ALU.add).then_inc(s_hb, 1)

            def finish(tile, slot, rnd, early=False):
                e = expert_of(tile)
                dve.wait_ge(s_fy, tile + 1)
                if not early:
                    dve.wait_ge(s_fo, tile)
                v.tensor_tensor(yb[:, :], ps_out[:, 0:D], b2_bc[:, bass.ds(e, 1), :].rearrange("p a n -> p (a n)"),
                                ALU.add).then_inc(s_yb, 1)
                dve.wait_ge(s_yb, tile + 1)
                dve.wait_ge(s_zg[slot], 16 * rnd + 16)
                v.scalar_tensor_tensor(out=yo[slot][:, :], in0=yb[:, :], scalar=res[slot][:, GATE:GATE + 1],
                                       in1=res[slot][:, 0:D], op0=ALU.mult, op1=ALU.add).then_inc(s_fo, 1)

            def step(rnd, slot, first_round=False, last_round=False):
                t = rnd * SLOTS + slot
                first, last = first_round and slot == 0, last_round and slot == SLOTS - 1
                nxt, nrnd = (slot + 1) % SLOTS, rnd + (slot + 1 == SLOTS)
                if not first:
                    hidden_low(t - 1)
                if not last:
                    rows_low(t + 1, nxt)
                hidden_bias(t, early=first)
                if not first:
                    finish(t - 1, (slot - 1) % SLOTS, rnd - (slot == 0), early=first_round and slot == 1)
                if not last:
                    tokens(t + 1, nxt, nrnd, reused=not first_round or slot == SLOTS - 1)

            tokens(0, 0, 0, reused=False)
            rows_low(0, 0)
            dve.wait_ge(s_b1, 16)
            dve.wait_ge(s_b2, 16)
            for slot in range(SLOTS):
                step(0, slot, first_round=True)
            with dve.Fori(1, ROUNDS - 1) as r:
                for slot in range(SLOTS):
                    step(r, slot)
            for slot in range(SLOTS):
                step(ROUNDS - 1, slot, last_round=True)
            hidden_low(NET - 1)
            finish(NET - 1, SLOTS - 1, ROUNDS - 1)

        @block.tensor
        def _(pe):
            def transpose(dst, src, n=P):
                return pe.transpose(dst, src, ident[0:n, 0:n])

            def quad_transposes(u):
                pe.wait_ge(s_xn, u + 1)
                for b in range(2):
                    if u >= 1:
                        pe.wait_ge(s_xtc, 2 * u + b - 1)
                    for t in range(2):
                        for k in range(KD):
                            ins = transpose(ps_xt[b][:, (t * KD + k) * P:(t * KD + k + 1) * P],
                                            xn[:, u % 2, 2 * b + t, k * P:(k + 1) * P])
                    ins.then_inc(s_xt, 1)

            def quad_logits(u):
                pe.wait_ge(s_xtc, 2 * u + 2)
                if u >= 1:
                    pe.wait_ge(s_ltc, u)
                for k in range(KD):
                    ins = pe.matmul(ps_lt[0:NEXP, :], wr_sb[:, k, :], xT[:, k, :], start=(k == 0), stop=(k == KD - 1))
                ins.then_inc(s_lt, 1)

            def quad_by_token(u):
                pe.wait_ge(s_ltc, u + 1)
                if u >= 2:
                    pe.wait_ge(s_lgr, u // 2)
                for t in range(4):
                    ins = transpose(ps_lg[:, (4 * u + t) * NEXP:(4 * u + t + 1) * NEXP],
                                    logT[:, t * P:(t + 1) * P], NEXP)
                ins.then_inc(s_lg, 1)

            def router(first, count):
                for u in range(first, first + count):
                    quad_transposes(u)
                    if u > first:
                        quad_logits(u - 1)
                    if u > first + 1:
                        quad_by_token(u - 2)
                quad_by_token(first + count - 2)
                quad_logits(first + count - 1)
                quad_by_token(first + count - 1)

            def counts(g):
                pe.wait_ge(s_cnt, g + 1)
                if g >= 1:
                    pe.wait_ge(s_preu, g)
                pe.matmul(ps_cnt[:, 0:NEXP], before[:, :], cnt[:, :], start=True, stop=True)
                pe.matmul(ps_cnt[:, NEXP:2 * NEXP], ones[:, :], cnt[:, :], start=True, stop=True).then_inc(s_pre, 1)

            pe.wait_ge(s_ident, 1)
            pe.wait_ge(s_const, NCONST)
            pe.wait_ge(s_rw, 32)
            router(0, 4)
            counts(0)
            counts(1)

            for i in range(NGT):
                n = LASTK if i == NGT - 1 else P
                pe.wait_ge(s_gnorm, i + 1)
                if i >= 3:
                    pe.wait_ge(s_gtc, i - 2)
                for k in range(KD):
                    ins = transpose(ps_misc[i % 3][:, k * P:k * P + n], xg[0:n, i, k * P:(k + 1) * P], n)
                ins.then_inc(s_gt, 1)

            pe.wait_ge(s_attw, 16 * 5)
            pe.wait_ge(s_gtc, NGT)
            for c in range(KD):
                for k in range(KD):
                    ins = pe.matmul(ps_misc[c][:, 0:NKEY], wqkv_sb[:, k, D + c * P:D + (c + 1) * P], xkT[:, k, :],
                                    start=(k == 0), stop=(k == KD - 1))
                ins.then_inc(s_qkv, 1)
            for c in range(NKT):
                n = P if c < 2 else LASTK
                if c >= 1:
                    pe.wait_ge(s_qkvc, c)
                for k in range(KD):
                    ins = pe.matmul(ps_misc[(KD + c) % 3][0:n, 0:D], xkT[:, k, c * P:c * P + n], wqkv_sb[:, k, 2 * D:3 * D],
                                    start=(k == 0), stop=(k == KD - 1))
                ins.then_inc(s_qkv, 1)
            for half in range(2):
                for c in range(KD):
                    if half == 0:
                        pe.wait_ge(s_vc, c + 2)
                    else:
                        pe.wait_ge(s_qkvc, KD + c + 1)
                    for k in range(KD):
                        ins = pe.matmul(ps_misc[c][:, :], wqkv_sb[:, k, c * P:(c + 1) * P],
                                        xqT[:, k, half * 512:(half + 1) * 512], start=(k == 0), stop=(k == KD - 1))
                    ins.then_inc(s_qkv, 1)

            router(4, 4)
            counts(2)
            counts(3)

            pe.wait_ge(s_qkvc, 3 * KD)
            pe.wait_ge(s_xtc, 2 * NQUAD)
            for step in range(len(TILES) + 2):
                if step < len(TILES):
                    j = TILES[step]
                    pe.wait_ge(s_kbd, step + 1)
                    if step >= 2:
                        pe.wait_ge(s_pr, step - 1)
                    own = min(j, NQT - 1)
                    blocks = halves(j)
                    parts = len(blocks) * KD
                    mask = masked[:, P - 1:P].to_broadcast([NQT, P]) if j == NQT else masked[:, :]
                    pe.matmul(ps_scores[step % 2][:, 0:parts * P].rearrange("p (a n) -> p a n", a=parts),
                              ident_h[:, own:own + 1].to_broadcast([NQT, P]),
                              mask.unsqueeze(1).to_broadcast([NQT, parts, P]), start=True, stop=False)
                    for r, b, n in blocks:
                        for k in range(KD):
                            q = xqT[:, k, SEQ - 1:SEQ].to_broadcast([P, P]) if j == NQT else xqT[:, k, j * P:(j + 1) * P]
                            ins = pe.matmul(ps_scores[step % 2][:, (KD * b + k) * P:(KD * b + k + 1) * P],
                                            kbd[:, step % 2, k, b, :], q, start=False,
                                            stop=KD * b + k == parts - 1)
                    ins.then_inc(s_sc, 1)
                if step == 0:
                    pe.wait_ge(s_tabc, 1)
                    for c, at in enumerate((TAB0, TAB1)):
                        ins = pe.matmul(ps_cnt[0:1, at:at + NET], tab_col[:, c:c + 1], ident[:, 0:NET], start=True, stop=True)
                    ins.then_inc(s_tabp, 1)
                if step >= 2:
                    pe.wait_ge(s_atn, step - 1)
                    for k in range(KD):
                        ins = transpose(ps_attT[:, k * P:(k + 1) * P],
                                        att[:, k * HH:(k + 1) * HH, :].rearrange("p h d -> p (h d)"))
                    ins.then_inc(s_att, 1)
                if 1 <= step <= len(TILES):
                    j = TILES[step - 1]
                    pe.wait_ge(s_pr, step)
                    if step == 1:
                        pe.wait_ge(s_vbd, 16 * KD * HH)
                    else:
                        pe.wait_ge(s_atn, step - 1)
                    for r, b, n in halves(j):
                        for k in range(KD):
                            ins = pe.matmul(ps_att[r, k * VW:(k + 1) * VW], pr[:, (step - 1) % 2, k, r], vbd[:, k, n, :],
                                            start=True, stop=True)
                    ins.then_inc(s_at, 1)
                if step >= 2:
                    pe.wait_ge(s_atc, step - 1)
                    if step >= 3:
                        pe.wait_ge(s_z, step - 2)
                    for k in range(KD):
                        ins = pe.matmul(ps_proj[:, 0:D], attT[:, k, :], wproj_sb[:, k, :], start=(k == 0), stop=(k == KD - 1))
                    ins.then_inc(s_y, 1)

            def expert_of(tile):
                return pe.value_load(tab_exp[0:1, bass.ds(tile, 1)], min_val=0, max_val=NEXP - 1)

            def weights(e, part, k, n):
                return w_sb[:, bass.ds(e, 1), part, k * n:(k + 1) * n].rearrange("p a n -> p (a n)")

            def hidden_transposes(tile, early=False):
                pe.wait_ge(s_hb, tile + 1)
                if not early:
                    pe.wait_ge(s_hl, tile)
                for k in range(KH):
                    ins = transpose(ps_hidT[:, k * P:(k + 1) * P], hb[:, k * P:(k + 1) * P])
                ins.then_inc(s_ht, 1)

            def row_transposes(tile, early=False):
                pe.wait_ge(s_fn, tile + 1)
                if not early:
                    pe.wait_ge(s_fl, tile)
                for k in range(KD):
                    ins = transpose(ps_rows[:, k * P:(k + 1) * P], fxn[:, k * P:(k + 1) * P])
                ins.then_inc(s_ft, 1)

            def hidden(tile, slot, early=False):
                e = expert_of(tile)
                pe.wait_ge(s_fl, tile + 1)
                if not early:
                    pe.wait_ge(s_hb, tile)
                for k in range(KD):
                    for a, part in ((fx_hi, HI1), (fx_hi, LO1), (fx_lo, HI1)):
                        ins = pe.matmul(ps_hidden[:, :], a[slot][:, k, :], weights(e, part, k, HID),
                                        start=(k == 0 and a is fx_hi and part == HI1), stop=(k == KD - 1 and a is fx_lo))
                ins.then_inc(s_h, 1)

            def expert_out(tile, early=False):
                e = expert_of(tile)
                pe.wait_ge(s_hl, tile + 1)
                if not early:
                    pe.wait_ge(s_yb, tile)
                for k in range(KH):
                    for a, part in ((h_hi, HI2), (h_hi, LO2), (h_lo, HI2)):
                        ins = pe.matmul(ps_out[:, 0:D], a[:, k, :], weights(e, part, k, D),
                                        start=(k == 0 and a is h_hi and part == HI2), stop=(k == KH - 1 and a is h_lo))
                ins.then_inc(s_fy, 1)

            def step(rnd, slot, first_round=False, last_round=False):
                t = rnd * SLOTS + slot
                first, last = first_round and slot == 0, last_round and slot == SLOTS - 1
                early = first_round and slot == 1
                if not first:
                    hidden_transposes(t - 1, early)
                if not last:
                    row_transposes(t + 1)
                hidden(t, slot, early=first)
                if not first:
                    expert_out(t - 1, early)

            row_transposes(0, early=True)
            pe.wait_ge(s_wlo, NPIECE)
            pe.wait_ge(s_tab, 1)
            pe.wait_ge(s_atn, len(TILES))
            for slot in range(SLOTS):
                step(0, slot, first_round=True)
            with pe.Fori(1, ROUNDS - 1) as r:
                for slot in range(SLOTS):
                    step(r, slot)
            for slot in range(SLOTS):
                step(ROUNDS - 1, slot, last_round=True)
            hidden_transposes(NET - 1)
            expert_out(NET - 1)


_INS = ["L0_attn_x", "L0_attn_Wqkv", "L0_attn_bqkv", "L0_attn_Wproj", "L0_attn_bproj", "L0_attn_mapping",
        "L0_ffn_Wr", "L0_ffn_br", "L0_ffn_W1", "L0_ffn_b1", "L0_ffn_W2", "L0_ffn_b2"]


def kernel(**inputs):
    import numpy as _np
    import concourse.bacc as _bacc
    from concourse import mybir as _mybir
    from concourse.bass_utils import run_bass_kernel_spmd as _run

    nc = _bacc.Bacc("TRN2", target_bir_lowering=False, num_devices=1)
    arrays, args = {}, []
    for name in _INS:
        a = _np.ascontiguousarray(inputs[name])
        arrays[f"in_{name}_dram"] = a
        args.append(nc.dram_tensor(f"in_{name}_dram", a.shape, _mybir.dt.from_np(a.dtype), kind="ExternalInput").ap())
    out = nc.dram_tensor("out_0_dram", (1, M, D), F32, kind="ExternalOutput").ap()
    build(nc, *args, out)
    r = _run(nc, [arrays], core_ids=[0])
    return r.results[0]["out_0_dram"]
```

```python
from contextlib import ExitStack

import concourse.bass as bass
from concourse import mybir

F32 = mybir.dt.float32
F32R = mybir.dt.float32r
BF16 = mybir.dt.bfloat16
I32 = mybir.dt.int32
ALU = mybir.AluOpType
ACT = mybir.ActivationFunctionType
AX = mybir.AxisListType

P = 128
M, D = 4096, 256
SEQ = 1024
HEADS, HD = 16, 16
BLOCK, KEYS = 64, 16
SEG, DIL = 64, 4
SCALE = HD ** -0.5
NEXP, HID = 8, 512
LN_EPS, SUM_EPS = 1e-5, 1e-6

KD = D // P
KH = HID // P
NT = M // P
GT = 8
NG = NT // GT
NQT = SEQ // P
NKB = SEQ // BLOCK + 1
NKEY = NKB * KEYS
NKT = 3
LASTK = NKEY - 2 * P
NGT = NQT + NKT
HH = P // HD
VW = P + HH
MASKED = -1e9 / SCALE
NET = M // P + NEXP - 1
REG = M + P
RSTD, SHIFT, GATE, ATT_ROW, TOKEN = range(D, D + 5)
XW = D + 5
SLOTS = 3
NLN = NT + NGT
PIECE = 512
HI1, LO1, HI2, LO2 = range(4)
PIECES = 4
RAW, OWN_RAW = 6, 3
EARLY = 5


class Chain:

    def __init__(self, eng, sem):
        self.eng, self.sem, self.n = eng, sem, 0

    def then(self, ins):
        self.n = self.n + 1
        ins.then_inc(self.sem, 1)
        self.eng.wait_ge(self.sem, self.n)


def build(nc, x, wqkv, bqkv, wproj, bproj, mapping, wr, br, w1, b1, w2, b2, out):
    sent = nc.dram_tensor("sent_rows", (NEXP * REG + P, XW), F32, kind="Internal").ap()
    vals = nc.dram_tensor("value_rows", (NKEY, D), F32, kind="Internal").ap()
    att_rows = nc.dram_tensor("attention_rows", (SEQ + 1, D), F32, kind="Internal").ap()
    x2 = x.rearrange("b m d -> (b m) d")
    out2 = out.rearrange("b m d -> (b m) d")

    with ExitStack() as ctx:
        ctx.enter_context(nc.allow_non_contiguous_dma(reason="short columns of the mapping and of biases"))

        def sb(name, shape, dt=F32):
            return ctx.enter_context(nc.sbuf_tensor(name, shape, dt))

        def sem(name):
            return ctx.enter_context(nc.semaphore(name))

        ident = sb("ident", [P, P])
        ident_h = sb("ident_h", [NQT, NQT], BF16)
        ones = sb("ones", [P, P])
        before = sb("before", [P, P])
        headmask = sb("headmask", [P, HH])
        headlow = sb("headlow", [P, HH])
        first_of = sb("first_of", [P, NEXP])
        restart = sb("restart", [P, NEXP, GT])
        minus_half = sb("minus_half", [P, NGT])
        region0 = sb("region0", [P, NEXP])
        key_step = sb("key_step", [P, 1], I32)
        part_i = sb("part_i", [P, 1], I32)
        part_f = sb("part_f", [P, 1])
        first_i = sb("first_i", [P, NEXP], I32)
        region_i = sb("region_i", [P, NEXP], I32)
        token_i = sb("token_i", [P, NT], I32)
        wproj_sb = sb("wproj_sb", [P, KD, D])
        wr_sb = sb("wr_sb", [P, KD, NEXP])
        bqk_col = sb("bqk_col", [P, 2 * KD])
        bproj_bc = sb("bproj_bc", [P, D])
        br_bc = sb("br_bc", [P, NEXP])
        b1_bc = sb("b1_bc", [P, NEXP, HID])
        raw = sb("raw", [P, OWN_RAW, PIECE])
        stats = sb("stats", [P, NLN, 6])
        mv = sb("mv", [P, NLN, 2])
        guess = sb("guess", [P, NLN])
        varp = sb("varp", [P, NLN])
        nt1 = sb("nt1", [P, NLN])
        nt2 = sb("nt2", [P, NLN])
        rstd = sb("rstd", [P, NGT])
        lg = sb("lg", [P, GT, NEXP])
        logT = sb("logT", [NEXP, 4 * P])
        lgm = sb("lgm", [P, GT])
        lgd = sb("lgd", [P, GT, NEXP])
        lge = sb("lge", [P, GT, NEXP])
        lsum = sb("lsum", [P, GT])
        eqw = sb("eqw", [P, GT, NEXP])
        eqm = sb("eqm", [P, GT])
        onehot = sb("onehot", [P, NEXP, GT])
        rank = sb("rank", [P, NEXP, GT])
        cnt = sb("cnt", [P, NEXP])
        carry = sb("carry", [P, NEXP])
        offs = sb("offs", [P, NEXP])
        place = sb("place", [P, NEXP, GT])
        posf = sb("posf", [P, GT])
        pos = sb("pos", [P, NG, GT], I32)
        tab_i = sb("tab_i", [P, NEXP], I32)
        tab_n = sb("tab_n", [P, NEXP])
        tab_end = sb("tab_end", [P, NEXP])
        tab_start = sb("tab_start", [P, NEXP])
        tab_base = sb("tab_base", [P, NEXP])
        tab_a = sb("tab_a", [P, NEXP])
        tab_b = sb("tab_b", [P, NEXP])
        tab_e = sb("tab_e", [P, 1])
        tab_r = sb("tab_r", [P, 1])
        tab_u = sb("tab_u", [P, 1])
        tab_col = sb("tab_col", [P, 2])
        tab_row = sb("tab_row", [1, NET], I32)
        tab_exp = sb("tab_exp", [1, NET], I32)
        pad_row = sb("pad_row", [1, NEXP], I32)
        map_q = sb("map_q", [P, NQT], I32)
        map_b = sb("map_b", [P, NKT], I32)
        idx_a = sb("idx_a", [P, NKT], I32)
        idx_k = sb("idx_k", [P, NKT], I32)
        map_k = sb("map_k", [P, NKT], I32)
        row_k = sb("row_k", [P, NKT], I32)
        row_q = sb("row_q", [P, NQT], I32)
        map_row = sb("map_row", [NQT, P], I32)
        masked = sb("masked", [NQT, P], BF16)
        vmask = sb("vmask", [P, NKT])
        sc_max = sb("sc_max", [P, KD, 2])
        sc_bias = sb("sc_bias", [P, KD * 2])
        pr_sum = sb("pr_sum", [P, HEADS])
        pr_inv = sb("pr_inv", [P, HEADS])
        rows = [sb(f"rows{i}", [P, XW]) for i in range(SLOTS)]
        fxn = sb("fxn", [P, D])
        toki = sb("toki", [P, SLOTS, 2], I32)

        lent = ExitStack()

        def lend(name, shape, dt=F32):
            return lent.enter_context(nc.sbuf_tensor(name, shape, dt))

        KEEP = EARLY * 8 * PIECE + NT * XW + 4 * D + 2 * KD * 4 * P + NKT * D + D + XW - NEXP * 8 * PIECE
        assert KEEP >= 0
        lend("early_experts", [P, EARLY * 4 * 2 * PIECE])
        x_sb = lend("x_sb", [P, NT, XW])
        xn = lend("xn", [P, 2, 2, D])
        xT = lend("xT", [P, 2, KD, 4 * P])
        vrow = lend("vrow", [P, NKT, D])
        bv_bc = lend("bv_bc", [P, D])
        zeros = lend("pad_rows", [P, XW])
        lent_key = lend("lent_key", [P, 8 * P])
        xkT = lent_key[:, 0:KD * NKEY].rearrange("p (k n) -> p k n", k=KD)
        kbd = lent_key[:, :].rearrange("p (a k b n) -> p a k b n", a=2, k=KD, b=2)
        shared = lend("shared", [P, KD * NKB * VW])
        xg = shared[:, 0:NGT * D].rearrange("p (t d) -> p t d", t=NGT)
        vbd = shared[:, :].rearrange("p (k n j) -> p k n j", k=KD, n=NKB)
        xqT = lend("xqT", [P, KD, SEQ])
        kT = lend("kT", [P, KD, NKEY])
        wqkv_sb = lend("wqkv_sb", [P, KD, 3 * D])
        work = wqkv_sb[:, :, :].rearrange("p k n -> p (k n)")
        pr = work[:, 0:2 * D].rearrange("p (b k n) -> p b k n", b=2, k=KD)
        att = work[:, 2 * D:3 * D].rearrange("p (h d) -> p h d", h=HEADS)
        attT = work[:, 3 * D:4 * D].rearrange("p (k n) -> p k n", k=KD)
        att_out = work[:, 4 * D:6 * D].rearrange("p (b d) -> p b d", b=2)
        lent.close()

        w_sb = sb("w_sb", [P, NEXP, 4, 2 * PIECE], F32R)
        sb("kept_for_keys", [P, 8 * P + KEEP])
        fx_hi = [sb(f"fx_hi{i}", [P, KD, P], F32R) for i in range(SLOTS)]
        fx_lo = [sb(f"fx_lo{i}", [P, KD, P], F32R) for i in range(SLOTS)]
        hb = sb("hb", [P, HID])
        h_hi = sb("h_hi", [P, KH, P], F32R)
        h_lo = sb("h_lo", [P, KH, P], F32R)
        b2_bc = sb("b2_bc", [P, NEXP, D])
        res = [sb(f"res{i}", [P, GATE + 1]) for i in range(SLOTS)]
        yb = sb("yb", [P, D])
        yo = [sb(f"yo{i}", [P, D]) for i in range(SLOTS)]

        banks = [ctx.enter_context(nc.psum_tensor(f"bank{i}", [P, 512], F32)) for i in range(8)]
        ps_xt = banks[0:2]
        ps_lt, ps_lg = banks[2], banks[3]
        ps_cnt = ps_lg[:, NT * NEXP:]
        ps_a, ps_b, ps_c = banks[5], banks[6], banks[7]
        ps_misc = [ps_a, ps_b, ps_c]
        ps_scores, ps_att, ps_attT, ps_proj = [ps_a, ps_b], ps_c, banks[4][:, 0:D], banks[4][:, D:2 * D]
        ps_rows, ps_hidden, ps_hidT, ps_out = banks[2], banks[4], [banks[3], banks[5]], banks[7]
        TAB0, TAB1 = 2 * NEXP, 2 * NEXP + NET

        s_const = sem("constants_ready")
        s_ident = sem("identity_ready")
        s_zero = sem("pad_rows_ready")
        s_pool = sem("pool_chain")
        s_dve = sem("vector_chain")
        s_attw = sem("attention_weights_loaded")
        s_rw = sem("router_weights_loaded")
        s_b1 = sem("hidden_biases_loaded")
        s_b1_late = sem("last_hidden_biases_loaded")
        s_b2 = sem("output_biases_loaded")
        s_raw = [sem(f"weight_piece_loaded{i}") for i in range(RAW)]
        s_whi = sem("weight_piece_high")
        s_wlo = sem("weight_piece_low")
        s_x = [sem(f"x_group_loaded{g}") for g in range(NG)]
        s_map = sem("mapping_loaded")
        s_idx = sem("key_index_ready")
        s_mapk = sem("key_mapping_gathered")
        s_rowk = sem("key_row_index_ready")
        s_gath = sem("rows_gathered")
        s_var = sem("variance_ready")
        s_guess = sem("rstd_guess_ready")
        s_norm = sem("group_scale_shift_ready")
        s_gnorm = sem("gathered_normalised")
        s_xn = sem("tiles_normalised")
        s_xnv = sem("tiles_normalised_by_vector")
        s_xt = sem("x_transposed")
        s_xtc = sem("x_transpose_copied")
        s_lt = sem("logits_ready")
        s_ltc = sem("logits_copied")
        s_lg = sem("logits_by_token")
        s_lgr = sem("logits_read")
        s_lgc = sem("logits_centred")
        s_lge = sem("logits_exp")
        s_cnt = sem("counts_ready")
        s_pre = sem("prefix_ready")
        s_preu = sem("prefix_used")
        s_pos = sem("positions_ready")
        s_sent = [sem(f"rows_sent{g}") for g in range(NG)]
        s_padr = sem("pad_places_ready")
        s_tabc = sem("table_columns_ready")
        s_tabp = sem("table_transposed")
        s_tab = sem("table_ready")
        s_pads = sem("pad_rows_written")
        s_padq = sem("pad_rows_written_by_gpsimd")
        s_gt = sem("gathered_transposed")
        s_gtc = sem("gathered_copied")
        s_qkv = sem("projection_ready")
        s_qkvc = sem("query_key_copied")
        s_vc = sem("value_copied")
        s_vst = sem("value_rows_stored")
        s_vm = sem("value_blocks_cleared")
        s_vz = sem("value_blocks_zeroed")
        s_vbd = sem("value_blocks_loaded")
        s_kbd = sem("key_blocks_ready")
        s_sc = sem("scores_ready")
        s_max = sem("scores_max_ready")
        s_bias = sem("exp_bias_ready")
        s_pr = sem("exp_ready")
        s_at = sem("attended")
        s_atn = sem("attended_normalised")
        s_att = sem("attended_transposed")
        s_atc = sem("attended_copied")
        s_y = sem("projected")
        s_z = sem("attention_rows_ready")
        s_zst = [sem(f"attention_rows_stored{i}") for i in range(2)]
        s_ld = [sem(f"expert_rows_loaded{i}") for i in range(SLOTS)]
        s_fn = sem("expert_rows_normalised")
        s_ft = sem("expert_rows_transposed")
        s_fh = sem("expert_rows_high")
        s_fl = sem("expert_rows_low")
        s_res = sem("expert_residual_copied")
        s_h = sem("hidden_ready")
        s_hb = sem("hidden_biased")
        s_ht = sem("hidden_transposed")
        s_hh = [sem(f"hidden_high{i}") for i in range(2)]
        s_hl = [sem(f"hidden_low{i}") for i in range(2)]
        s_fy = sem("expert_out_ready")
        s_tok = sem("token_index_ready")
        s_seen = sem("pool_saw_tile")
        s_yb = sem("expert_out_biased")
        s_zg = [sem(f"attention_row_added{i}") for i in range(SLOTS)]
        s_fo = sem("row_finished")
        s_out = [sem(f"rows_out{i}") for i in range(SLOTS)]

        NCONST = 9
        NQUAD = NT // 4
        ROUNDS = NET // SLOTS
        assert NET % SLOTS == 0 and ROUNDS % 2 == 1
        TILES = [NQT] + list(range(NQT))
        NPIECE = NEXP * PIECES
        NEARLY = EARLY * PIECES
        BEFORE = [1, 1, 3]
        DURING = [2, 2, 2, 2, 2, 2, 3, 3, 4, 4, 1]
        assert sum(BEFORE) + sum(DURING) == NPIECE and len(DURING) == len(TILES) + 2
        SENT_BEFORE = {NEARLY: (0, 1), NEARLY + PIECES: (2,), NEARLY + PIECES + 2: (3,)}
        LAST_EXPERT = (NEXP - 1) * PIECES
        PADS_FROM = NPIECE - 8
        SP_PADS = 4

        def halves(j):
            if j == NQT:
                return [(slice(0, P), 0, NKB - 1)]
            return [(slice(BLOCK * b, BLOCK * (b + 1)), b, 2 * j + b) for b in range(2)]

        def score_part(i, k, b, r):
            at = (KD * b + k) * P
            return ps_scores[i % 2][:, at + r.start:at + r.stop]

        def raw_of(n):
            return n % RAW

        def raw_at(n):
            i = raw_of(n)
            return raw[:, i, :] if i < OWN_RAW else b1_bc[:, NEXP - RAW + i, :]

        def raw_before(n):
            return [m for m in range(n) if raw_of(m) == raw_of(n)]

        def parts_of(n):
            e, q = n // PIECES, n % PIECES
            hi = HI1 if q < 2 else HI2
            cols = slice((q % 2) * PIECE, (q % 2 + 1) * PIECE)
            return w_sb[:, e, hi, cols], w_sb[:, e, hi + 1, cols]

        def pad_region(eng, e, done):
            first_pad = eng.value_load(pad_row[0:1, e:e + 1], min_val=e * REG, max_val=e * REG + M)
            eng.dma_start(sent[bass.ds(first_pad, P), :], zeros[:, :]).then_inc(done, 16)

        block = ctx.enter_context(nc.Block())

        @block.sync
        def _(sp):
            block_first = mapping.rearrange("(c n q) -> c n q", n=P // KEYS, q=BLOCK)
            for c in range(2):
                sp.dma_start(map_b[:, c:c + 1], block_first[c, :, 0:1].to_broadcast([P // KEYS, KEYS])).then_inc(s_map, 16)
            sp.dma_start(map_b[:, 2:3], mapping[SEQ - 1:SEQ].unsqueeze(0).to_broadcast([P, 1])).then_inc(s_map, 16)
            sp.dma_start(map_row[:, :], mapping.rearrange("(t p) -> t p", p=P)).then_inc(s_map, 16)
            sp.dma_start(map_q[:, :], mapping.rearrange("(t p) -> p t", p=P)).then_inc(s_map, 16)
            x_t = x2.rearrange("(g t p) d -> g p t d", g=NG, p=P)
            for g in range(NG):
                sp.dma_start(x_sb[:, g * GT:(g + 1) * GT, 0:D], x_t[g]).then_inc(s_x[g], 16)
                if g == 0:
                    sp.dma_start(wr_sb[:, :, :], wr.rearrange("(k p) e -> p k e", p=P)).then_inc(s_rw, 16)
                    sp.dma_start(br_bc[:, :], br.unsqueeze(0).to_broadcast([P, NEXP])).then_inc(s_rw, 16)

            sp.wait_ge(s_gath, 16 * NGT)
            sp.dma_start(wqkv_sb[:, :, :], wqkv.rearrange("(k p) n -> p k n", p=P)).then_inc(s_attw, 16)
            sp.dma_start(bqk_col[:, :], bqkv[0:2 * D].rearrange("(c p) -> p c", p=P)).then_inc(s_attw, 16)
            sp.dma_start(bv_bc[:, :], bqkv[2 * D:3 * D].unsqueeze(0).to_broadcast([P, D])).then_inc(s_attw, 16)
            sp.dma_start(wproj_sb[:, :, :], wproj.rearrange("(k p) n -> p k n", p=P)).then_inc(s_attw, 16)
            sp.dma_start(bproj_bc[:, :], bproj.unsqueeze(0).to_broadcast([P, D])).then_inc(s_attw, 16)

            def load_piece(n):
                e, q = n // PIECES, n % PIECES
                if raw_before(n):
                    sp.wait_ge(s_wlo, raw_before(n)[-1] + 1)
                dst = raw_at(n)
                if q < 2:
                    sp.dma_start(dst, w1[e, q * P:(q + 1) * P, :]).then_inc(s_raw[raw_of(n)], 16)
                else:
                    src = w2[e].rearrange("(k p) n -> p k n", p=P)[:, 2 * (q - 2):2 * (q - 1), :]
                    sp.dma_start(dst.rearrange("p (k n) -> p k n", k=2), src).then_inc(s_raw[raw_of(n)], 16)

            for n in range(6):
                load_piece(n)
            sp.wait_ge(s_vc, NKT)
            sp.dma_start(vals[0:2 * P, :].rearrange("(t p) d -> p t d", p=P), vrow[:, 0:2, :]).then_inc(s_vst, 16)
            sp.dma_start(vals[2 * P:NKEY, :], vrow[0:LASTK, 2, :]).then_inc(s_vst, 16)
            for n in range(6, 7):
                load_piece(n)
            sp.wait_ge(s_vst, 32)
            sp.wait_ge(s_vz, 1)
            v_src = vals.rearrange("(n s) (k h d) -> h s k n d", s=KEYS, k=KD, h=HH)
            for h in range(HH):
                sp.dma_start(vbd[h * HD:(h + 1) * HD, :, :, h * HD:(h + 1) * HD], v_src[h]).then_inc(s_vbd, 16)
            for n in range(7, 16):
                load_piece(n)
            b1_all = b1.unsqueeze(0).to_broadcast([P, NEXP, HID])
            lent_b1 = NEXP - RAW + OWN_RAW
            sp.dma_start(b1_bc[:, 0:lent_b1, :], b1_all[:, 0:lent_b1, :]).then_inc(s_b1, 16)

            sp.wait_ge(s_zero, 1)
            sp.dma_start(sent[NEXP * REG:NEXP * REG + P, :], zeros[:, :]).then_inc(s_pads, 16)
            for n in range(16, PADS_FROM):
                load_piece(n)
            sp.wait_ge(s_padr, 1)
            for i in range(SP_PADS):
                pad_region(sp, i, s_pads)
                load_piece(PADS_FROM + i)
            for n in range(PADS_FROM + SP_PADS, NPIECE):
                load_piece(n)

            for g in range(NG):
                sp.wait_ge(s_sent[g], 16 * GT)
            sp.wait_ge(s_pads, 16 * (SP_PADS + 1))
            sp.wait_ge(s_padq, 16 * (NEXP - SP_PADS))
            sp.wait_ge(s_tab, 1)

            def load(t, slot):
                row = sp.value_load(tab_row[0:1, bass.ds(t, 1)], min_val=0, max_val=NEXP * REG)
                sp.dma_start(rows[slot][:, :], sent[bass.ds(row, P), :]).then_inc(s_ld[slot], 16)

            for slot in range(SLOTS):
                load(slot, slot)
            sp.wait_ge(s_wlo, NPIECE)
            sp.dma_start(b1_bc[:, lent_b1:NEXP, :], b1_all[:, lent_b1:NEXP, :]).then_inc(s_b1_late, 16)
            sp.wait_ge(s_z, len(TILES))
            sp.dma_start(b2_bc[:, :, :], b2.unsqueeze(0).to_broadcast([P, NEXP, D])).then_inc(s_b2, 16)
            with sp.Fori(1, ROUNDS) as r:
                for slot in range(SLOTS):
                    sp.wait_ge(s_fn, (r - 1) * SLOTS + slot + 1)
                    sp.wait_ge(s_res, (r - 1) * SLOTS + slot + 1)
                    sp.wait_ge(s_tok, (r - 1) * SLOTS + slot + 1)
                    load(r * SLOTS + slot, slot)

        @block.gpsimd
        def _(pool):
            ch = Chain(pool, s_pool)
            ch.then(pool.memset(ones[:, :], 1.0))
            pool.affine_select(out=ident[:, :], in_=ones[:, :], pattern=[[-1, P]], compare_op=ALU.is_equal,
                               fill=0.0, base=0, channel_multiplier=1).then_inc(s_ident, 1)
            pool.iota(part_i[:, :], pattern=[[0, 1]], base=0, channel_multiplier=1).then_inc(s_const, 1)
            pool.iota(first_i[:, :], pattern=[[-1, NEXP]], base=NEXP, channel_multiplier=0).then_inc(s_const, 1)
            pool.iota(region_i[:, :], pattern=[[REG, NEXP]], base=-1, channel_multiplier=0).then_inc(s_const, 1)
            pool.iota(token_i[:, :], pattern=[[P, NT]], base=0, channel_multiplier=1).then_inc(s_const, 1)
            pool.affine_select(out=before[:, :], in_=ones[:, :], pattern=[[1, P]], compare_op=ALU.is_gt,
                               fill=0.0, base=0, channel_multiplier=-1).then_inc(s_const, 1)
            ch.then(pool.affine_select(out=headlow[:, :], in_=ones[:, 0:HH], pattern=[[-HD, HH]], compare_op=ALU.is_ge,
                                       fill=0.0, base=0, channel_multiplier=1))
            pool.affine_select(out=headmask[:, :], in_=headlow[:, :], pattern=[[HD, HH]], compare_op=ALU.is_gt,
                               fill=0.0, base=HD, channel_multiplier=-1).then_inc(s_const, 1)
            pool.memset(restart[:, :, 1:GT], 1.0).then_inc(s_const, 1)
            pool.memset(restart[:, :, 0:1], 0.0).then_inc(s_const, 1)
            pool.memset(minus_half[:, :], -0.5).then_inc(s_const, 1)
            ch.then(pool.memset(zeros[:, :], 0.0))
            pool.iota(zeros[:, :].bitcast(I32)[:, TOKEN:TOKEN + 1], pattern=[[0, 1]], base=M,
                      channel_multiplier=0).then_inc(s_zero, 1)

            pool.wait_ge(s_idx, 1)
            table = mapping.unsqueeze(1)
            for c in range(NKT):
                n = P if c < 2 else LASTK
                pool.indirect_dma_start(out=map_k[0:n, c:c + 1], out_offset=None, in_=table,
                                        in_offset=bass.IndirectOffsetOnAxis(ap=idx_k[0:n, c:c + 1], axis=0),
                                        bounds_check=SEQ - 1, oob_is_err=False).then_inc(s_mapk, 16)

            def rstd_guess(count, at, n):
                pool.wait_ge(s_var, count)
                pool.tensor_tensor(guess[:, at:at + n], varp[:, at:at + n], minus_half[:, 0:n], ALU.pow).then_inc(s_guess, 1)

            def gather(tile, index, n):
                pool.indirect_dma_start(out=xg[0:n, tile, :], out_offset=None, in_=x2,
                                        in_offset=bass.IndirectOffsetOnAxis(ap=index, axis=0),
                                        bounds_check=M - 1, oob_is_err=False).then_inc(s_gath, 16)

            def send(g):
                pool.wait_ge(s_pos, g + 1)
                for t in range(GT):
                    pool.indirect_dma_start(out=sent, in_=x_sb[:, g * GT + t, :], in_offset=None,
                                            out_offset=bass.IndirectOffsetOnAxis(ap=pos[:, g, t:t + 1], axis=0),
                                            bounds_check=NEXP * REG + P - 1, oob_is_err=False).then_inc(s_sent[g], 16)

            for t in range(NQT):
                gather(t, row_q[:, t:t + 1], P)
                if t == 2:
                    rstd_guess(1, 0, GT)
            pool.wait_ge(s_rowk, 1)
            for c in range(NKT):
                n = P if c < 2 else LASTK
                gather(NQT + c, row_k[0:n, c:c + 1], n)
            rstd_guess(2, GT, GT)
            rstd_guess(3, 2 * GT, GT)
            rstd_guess(4, NT, NGT)
            rstd_guess(5, 3 * GT, GT)
            pool.wait_ge(s_gt, NGT)
            pool.memset(shared[:, :], 0.0).then_inc(s_vm, 1)
            for g in range(NG):
                send(g)

            pool.wait_ge(s_padr, 1)
            for e in range(SP_PADS, NEXP):
                pad_region(pool, e, s_padq)

            pool.wait_ge(s_zst[0], 16 * ((len(TILES) + 1) // 2))
            pool.wait_ge(s_zst[1], 16 * (len(TILES) // 2))
            last_row = pool.to_reg(M - 1)
            last_att = pool.to_reg(SEQ)

            def await_tile(sem_, tile):
                pool.wait_ge(sem_, tile + 1)
                pool.sem_inc(s_seen, 1)

            def fetch(slot, tile):
                await_tile(s_tok, tile)
                await_tile(s_res, tile)
                pool.indirect_dma_start(out=res[slot][:, 0:D], out_offset=None, in_=att_rows,
                                        in_offset=bass.IndirectOffsetOnAxis(ap=toki[:, slot, 0:1], axis=0),
                                        bounds_check=last_att, oob_is_err=True,
                                        compute_op=ALU.add).then_inc(s_zg[slot], 16)

            def write(slot, tile):
                await_tile(s_fo, tile)
                pool.indirect_dma_start(out=out2, in_=yo[slot][:, :], in_offset=None,
                                        out_offset=bass.IndirectOffsetOnAxis(ap=toki[:, slot, 1:2], axis=0),
                                        bounds_check=last_row, oob_is_err=False).then_inc(s_out[slot], 16)

            fetch(0, 0)
            with pool.Fori(0, ROUNDS - 1) as r:
                for slot in range(SLOTS):
                    fetch((slot + 1) % SLOTS, r * SLOTS + slot + 1)
                    write(slot, r * SLOTS + slot)
            for slot in range(SLOTS):
                t = (ROUNDS - 1) * SLOTS + slot
                if slot + 1 < SLOTS:
                    fetch(slot + 1, t + 1)
                write(slot, t)
            for slot in range(SLOTS):
                pool.wait_ge(s_out[slot], 16 * ROUNDS)

        @block.scalar
        def _(act):
            split = [0]

            def high_parts(count):
                for _ in range(count):
                    n = split[0]
                    act.wait_ge(s_raw[raw_of(n)], 16 * (len(raw_before(n)) + 1))
                    for g in SENT_BEFORE.get(n, ()):
                        act.wait_ge(s_sent[g], 16 * GT)
                    if n == LAST_EXPERT:
                        act.wait_ge(s_lt, NQUAD)
                        act.wait_ge(s_vst, 32)
                        act.wait_ge(s_vc, NKT)
                    nc.scalar.activation(parts_of(n)[0], raw_at(n), ACT.Copy).then_inc(s_whi, 1)
                    split[0] = n + 1

            def normalise(h):
                act.wait_ge(s_norm, h // 4 + 1)
                if h >= 2:
                    act.wait_ge(s_xt, h - 1)
                for t in range(2):
                    row = x_sb[:, 2 * h + t, :]
                    ins = nc.scalar.activation(xn[:, h % 2, t, :], row[:, 0:D], ACT.Identity,
                                               bias=row[:, SHIFT:SHIFT + 1], scale=row[:, RSTD:RSTD + 1])
                ins.then_inc(s_xn, 1)

            def rows_copy(h):
                u, b = h // 2, h % 2
                act.wait_ge(s_xt, h + 1)
                if u >= 2 and b == 0:
                    act.wait_ge(s_lt, u - 1)
                nc.scalar.activation(xT[:, u % 2, :, b * 2 * P:(b + 1) * 2 * P].rearrange("p k (t n) -> p t k n", t=2),
                                     ps_xt[b][:, :].rearrange("p (t k n) -> p t k n", t=2, k=KD),
                                     ACT.Copy).then_inc(s_xtc, 1)

            def logits_copy(u):
                act.wait_ge(s_lt, u + 1)
                if u >= 1:
                    act.wait_ge(s_lg, u)
                nc.scalar.activation(logT[:, :], ps_lt[0:NEXP, :], ACT.Copy).then_inc(s_ltc, 1)

            def logits_exp(g):
                act.wait_ge(s_lgc, g + 1)
                nc.scalar.activation(lge[:, :, :], lgd[:, :, :], ACT.Exp).then_inc(s_lge, 1)

            def quad(u, last, shared_work=False):
                for h in (2 * u, 2 * u + 1):
                    rows_copy(h)
                    if h + 2 < 2 * last + 2 and not (shared_work and h % 2 == 1):
                        normalise(h + 2)

            def gathered():
                for i in range(NGT):
                    act.wait_ge(s_gt, i + 1)
                    n = LASTK if i == NGT - 1 else P
                    dst = xqT[:, :, i * P:i * P + n] if i < NQT else xkT[:, :, (i - NQT) * P:(i - NQT) * P + n]
                    src = ps_misc[i % 3][:, 0:KD * P].rearrange("p (k n) -> p k n", k=KD)[:, :, 0:n]
                    nc.scalar.activation(dst, src, ACT.Copy).then_inc(s_gtc, 1)

            def keys():
                act.wait_ge(s_attw, 16 * 5)
                for c in range(KD):
                    act.wait_ge(s_qkv, c + 1)
                    nc.scalar.activation(kT[:, c, :], ps_misc[c][:, 0:NKEY], ACT.Identity,
                                         bias=bqk_col[:, KD + c:KD + c + 1]).then_inc(s_qkvc, 1)

            def queries(half):
                act.wait_ge(s_qkv, KD + NKT + 2 * half + 2)
                for c in range(KD):
                    nc.scalar.activation(xqT[:, c, half * 512:(half + 1) * 512], ps_misc[c][:, :], ACT.Identity,
                                         bias=bqk_col[:, c:c + 1]).then_inc(s_qkvc, 1)

            normalise(0)
            normalise(1)
            for u in range(4):
                quad(u, last=3)
                if u >= 1:
                    logits_copy(u - 1)
            logits_copy(3)
            gathered()
            keys()
            logits_exp(0)
            high_parts(BEFORE[0])
            queries(0)
            high_parts(BEFORE[1])
            logits_exp(1)
            queries(1)
            normalise(8)
            quad(4, last=7, shared_work=True)
            high_parts(BEFORE[2])

            def router_step(step):
                if step < 3:
                    quad(5 + step, last=7, shared_work=True)
                if step < 2:
                    logits_copy(4 + step)
                if step == 3:
                    logits_copy(6)
                if step == 4:
                    logits_exp(2)
                if step == 5:
                    logits_copy(7)
                if step == 6:
                    logits_exp(3)

            def store_attention(i):
                j = TILES[i]
                act.wait_ge(s_z, i + 1)
                if j == NQT:
                    act.dma_start(att_rows[SEQ:SEQ + 1, :], att_out[0:1, i % 2, :]).then_inc(s_zst[i % 2], 16)
                else:
                    act.dma_start(att_rows[j * P:(j + 1) * P, :], att_out[:, i % 2, :]).then_inc(s_zst[i % 2], 16)

            for step in range(len(TILES) + 2):
                if step >= 2:
                    act.wait_ge(s_att, step - 1)
                    nc.scalar.activation(attT[:, :, :], ps_attT[:, 0:D].rearrange("p (k n) -> p k n", k=KD),
                                         ACT.Copy).then_inc(s_atc, 1)
                if step < len(TILES):
                    act.wait_ge(s_bias, step + 1)
                    if step >= 2:
                        act.wait_ge(s_at, step - 1)
                    for k in range(KD):
                        for r, b, n in halves(TILES[step]):
                            ins = nc.scalar.activation(pr[:, step % 2, k, r], score_part(step, k, b, r), ACT.Exp,
                                                       bias=sc_bias[:, 2 * k + b:2 * k + b + 1], scale=SCALE)
                    ins.then_inc(s_pr, 1)
                if step >= 3:
                    store_attention(step - 3)
                if step >= 3:
                    router_step(step)
                high_parts(DURING[step])
                if step < 3:
                    router_step(step)
            store_attention(len(TILES) - 1)

            def normal_rows(tile, slot, rnd, early=False):
                act.wait_ge(s_ld[slot], 16 * rnd + 16)
                if not early:
                    act.wait_ge(s_ft, tile)
                nc.scalar.activation(fxn[:, :], rows[slot][:, 0:D], ACT.Identity,
                                     bias=rows[slot][:, SHIFT:SHIFT + 1],
                                     scale=rows[slot][:, RSTD:RSTD + 1]).then_inc(s_fn, 1)

            def residual(tile, slot, early=False):
                if not early:
                    act.wait_ge(s_fo, tile - 2)
                nc.scalar.activation(res[slot][:, :], rows[slot][:, 0:GATE + 1], ACT.Copy).then_inc(s_res, 1)

            def rows_high(tile, slot, early=False):
                act.wait_ge(s_ft, tile + 1)
                if not early:
                    act.wait_ge(s_h, tile - 2)
                nc.scalar.activation(fx_hi[slot][:, :, :], ps_rows[:, 0:D].rearrange("p (k n) -> p k n", k=KD),
                                     ACT.Copy).then_inc(s_fh, 1)

            def hidden_high(tile, early=False):
                act.wait_ge(s_ht, tile + 1)
                if not early:
                    act.wait_ge(s_fy, tile)
                for i in range(2):
                    nc.scalar.activation(h_hi[:, 2 * i:2 * i + 2, :], ps_hidT[i][:, 0:2 * P].rearrange("p (k n) -> p k n", k=2),
                                         ACT.Relu).then_inc(s_hh[i], 1)

            def step(rnd, slot, first_round=False, last_round=False):
                t = rnd * SLOTS + slot
                left = NET if not last_round else SLOTS - slot
                if not (first_round and slot == 0):
                    hidden_high(t - 1, early=first_round and slot == 1)
                if left > 1:
                    nxt = (slot + 1) % SLOTS
                    rows_high(t + 1, nxt, early=first_round and slot < 2)
                    if left > 2:
                        normal_rows(t + 2, (slot + 2) % SLOTS, rnd + (slot + 2 >= SLOTS))
                    residual(t + 1, nxt, early=first_round and slot < 2)

            normal_rows(0, 0, 0, early=True)
            act.wait_ge(s_y, len(TILES))
            act.wait_ge(s_z, len(TILES))
            rows_high(0, 0, early=True)
            normal_rows(1, 1, 0)
            residual(0, 0, early=True)
            for slot in range(SLOTS):
                step(0, slot, first_round=True)
            for slot in range(SLOTS):
                step(1, slot)
            with act.Fori(1, ROUNDS // 2) as pair:
                for r in (2 * pair, 2 * pair + 1):
                    for slot in range(SLOTS):
                        step(r, slot)
            for slot in range(SLOTS):
                step(ROUNDS - 1, slot, last_round=True)
            hidden_high(NET - 1)

        @block.vector
        def _(dve):
            ch = Chain(dve, s_dve)
            v = nc.vector
            split = [0]

            def low_parts(count):
                for _ in range(count):
                    n = split[0]
                    hi, lo = parts_of(n)
                    dve.wait_ge(s_raw[raw_of(n)], 16 * (len(raw_before(n)) + 1))
                    dve.wait_ge(s_whi, n + 1)
                    v.tensor_tensor(lo, raw_at(n), hi.bitcast(F32), ALU.subtract).then_inc(s_wlo, 1)
                    split[0] = n + 1

            dve.wait_ge(s_const, NCONST)
            ch.then(v.tensor_scalar(key_step[:, :], part_i[:, :], KEYS - 1, 2, ALU.bitwise_and, ALU.logical_shift_left))
            dve.wait_ge(s_map, 80)
            ch.then(v.tensor_scalar(idx_a[:, :], map_b[:, :], -SEG, None, ALU.bitwise_and))
            ch.then(v.tensor_tensor(idx_a[:, :], idx_a[:, :], key_step[:, :].to_broadcast([P, NKT]), ALU.bitwise_or))
            v.tensor_scalar(row_q[:, :], map_q[:, :], M - 1, None, ALU.min)
            v.tensor_scalar(idx_k[:, :], idx_a[:, :], SEQ - 1, None, ALU.min).then_inc(s_idx, 1)
            ch.then(v.memset(mv[:, :, :], 0.0))

            def constants():
                v.tensor_scalar(masked[:, :], map_row[:, :], M, MASKED, ALU.is_ge, ALU.mult)
                v.tensor_scalar(vmask[:, :], map_b[:, :], M, None, ALU.is_lt)
                v.tensor_copy(first_of[:, :], first_i[:, :])
                v.tensor_copy(part_f[:, :], part_i[:, :])
                v.tensor_copy(region0[:, :], region_i[:, :])
                v.tensor_copy(carry[:, :], region_i[:, :])
                dve.wait_ge(s_ident, 1)
                v.tensor_copy(ident_h[:, :], ident[0:NQT, 0:NQT])
                x_bits = x_sb[:, :, :].bitcast(I32)
                v.tensor_scalar(x_bits[:, :, ATT_ROW], token_i[:, :], SEQ, None, ALU.min)
                ch.then(v.tensor_copy(x_bits[:, :, TOKEN], token_i[:, :]))

            def moments(rows_of, at, n):
                for i in range(n):
                    pn = LASTK if at + i == NLN - 1 else P
                    ins = v.bn_stats(stats[0:pn, at + i, :], rows_of(i))
                ch.then(ins)
                for i in range(n):
                    pn = LASTK if at + i == NLN - 1 else P
                    ins = v.bn_aggr(mv[0:pn, at + i, :], stats[0:pn, at + i, :])
                ch.then(ins)
                v.tensor_scalar(varp[:, at:at + n], mv[:, at:at + n, 1], LN_EPS, None, ALU.add).then_inc(s_var, 1)

            def refine(out_, at, n, count):
                c = slice(at, at + n)
                dve.wait_ge(s_guess, count)
                ch.then(v.tensor_tensor(nt1[:, c], guess[:, c], guess[:, c], ALU.mult))
                ch.then(v.tensor_tensor(nt2[:, c], nt1[:, c], varp[:, c], ALU.mult))
                ch.then(v.tensor_scalar(nt1[:, c], nt2[:, c], -0.5, 1.5, ALU.mult, ALU.add))
                ch.then(v.tensor_tensor(out_, guess[:, c], nt1[:, c], ALU.mult))

            def group_moments(g):
                dve.wait_ge(s_x[g], 16)
                moments(lambda i: x_sb[:, g * GT + i, 0:D], g * GT, GT)

            def group_scale(g):
                tiles = slice(g * GT, (g + 1) * GT)
                refine(x_sb[:, tiles, RSTD], g * GT, GT, g + 1 if g < 3 else 5)
                v.scalar_tensor_tensor(out=x_sb[:, tiles, SHIFT], in0=mv[:, tiles, 0], scalar=-1.0,
                                       in1=x_sb[:, tiles, RSTD], op0=ALU.mult, op1=ALU.mult).then_inc(s_norm, 1)

            def normalise(h):
                dve.wait_ge(s_xt, h - 1)
                for t in range(2):
                    row = x_sb[:, 2 * h + t, :]
                    ins = v.tensor_scalar(xn[:, 1, t, :], row[:, 0:D], row[:, RSTD:RSTD + 1], row[:, SHIFT:SHIFT + 1],
                                          ALU.mult, ALU.add)
                ins.then_inc(s_xnv, 1)

            def gathered_row(i):
                return xg[0:LASTK if i == NGT - 1 else P, i, :]

            def choose(g):
                dve.wait_ge(s_lg, 2 * g + 2)
                v.tensor_tensor(lg[:, :, :], ps_lg[:, g * GT * NEXP:(g + 1) * GT * NEXP].rearrange("p (t e) -> p t e", t=GT),
                                br_bc[:, :].unsqueeze(1).to_broadcast([P, GT, NEXP]), ALU.add).then_inc(s_lgr, 1)
                dve.wait_ge(s_lgr, g + 1)
                ch.then(v.tensor_reduce(lgm[:, :], lg[:, :, :], AX.X, ALU.max))
                v.tensor_tensor(lgd[:, :, :], lg[:, :, :], lgm[:, :].unsqueeze(2).to_broadcast([P, GT, NEXP]),
                                ALU.subtract).then_inc(s_lgc, 1)
                dve.wait_ge(s_lgc, g + 1)
                ch.then(v.scalar_tensor_tensor(out=eqw[:, :, :], in0=lgd[:, :, :], scalar=0.0,
                                               in1=first_of[:, :].unsqueeze(1).to_broadcast([P, GT, NEXP]),
                                               op0=ALU.is_ge, op1=ALU.mult))
                ch.then(v.tensor_reduce(eqm[:, :], eqw[:, :, :], AX.X, ALU.max))
                ch.then(v.tensor_tensor(onehot[:, :, :].rearrange("p e t -> p t e"), eqw[:, :, :],
                                        eqm[:, :].unsqueeze(2).to_broadcast([P, GT, NEXP]), ALU.is_equal))
                ch.then(v.tensor_tensor_scan(rank[:, :, :].rearrange("p e t -> p (e t)"),
                                             restart[:, :, :].rearrange("p e t -> p (e t)"),
                                             onehot[:, :, :].rearrange("p e t -> p (e t)"), 0.0, ALU.mult, ALU.add))
                v.tensor_copy(cnt[:, :], rank[:, :, GT - 1]).then_inc(s_cnt, 1)

            def place_tokens(g):
                tiles = slice(g * GT, (g + 1) * GT)
                dve.wait_ge(s_lge, g + 1)
                ch.then(v.tensor_reduce(lsum[:, :], lge[:, :, :], AX.X, ALU.add))
                v.reciprocal(x_sb[:, tiles, GATE], lsum[:, :])
                dve.wait_ge(s_pre, g + 1)
                ch.then(v.tensor_tensor(offs[:, :], ps_cnt[:, 0:NEXP], carry[:, :], ALU.add))
                v.tensor_tensor(carry[:, :], ps_cnt[:, NEXP:2 * NEXP], carry[:, :], ALU.add).then_inc(s_preu, 1)
                ch.then(v.tensor_tensor(place[:, :, :], rank[:, :, :], offs[:, :].unsqueeze(2).to_broadcast([P, NEXP, GT]),
                                        ALU.add))
                ch.then(v.tensor_tensor(place[:, :, :], place[:, :, :], onehot[:, :, :], ALU.mult))
                ch.then(v.tensor_reduce(posf[:, :], place[:, :, :].rearrange("p e t -> p t e"), AX.X, ALU.add))
                v.tensor_copy(pos[:, g, :], posf[:, :]).then_inc(s_pos, 1)

            def tile_table():
                dve.wait_ge(s_preu, NG)
                v.tensor_scalar(pad_row[:, :], carry[0:1, :], 1.0, None, ALU.add).then_inc(s_padr, 1)
                ch.then(v.tensor_tensor(tab_n[:, :], carry[:, :], region0[:, :], ALU.subtract))
                ch.then(v.tensor_scalar(tab_i[:, :], tab_n[:, :], float(P - 1), None, ALU.add))
                ch.then(v.tensor_scalar(tab_i[:, :], tab_i[:, :], 7, None, ALU.logical_shift_right))
                ch.then(v.tensor_copy(tab_n[:, :], tab_i[:, :]))
                ch.then(v.tensor_tensor_scan(tab_end[:, :], ones[:, 0:NEXP], tab_n[:, :], 0.0, ALU.mult, ALU.add))
                ch.then(v.tensor_tensor(tab_start[:, :], tab_end[:, :], tab_n[:, :], ALU.subtract))
                ch.then(v.scalar_tensor_tensor(out=tab_base[:, :], in0=tab_start[:, :], scalar=-float(P),
                                               in1=region0[:, :], op0=ALU.mult, op1=ALU.add))
                v.tensor_scalar(tab_base[:, :], tab_base[:, :], 1.0, None, ALU.add)
                tile = part_f[:, :].to_broadcast([P, NEXP])
                ch.then(v.tensor_tensor(tab_a[:, :], tab_end[:, :], tile, ALU.is_le))
                v.tensor_reduce(tab_e[:, :], tab_a[:, :], AX.X, ALU.add)
                ch.then(v.tensor_tensor(tab_b[:, :], tab_start[:, :], tile, ALU.is_le))
                ch.then(v.tensor_tensor(tab_a[:, :], tab_b[:, :], tab_a[:, :], ALU.subtract))
                ch.then(v.scalar_tensor_tensor(out=tab_b[:, :], in0=tile, scalar=float(P), in1=tab_base[:, :],
                                               op0=ALU.mult, op1=ALU.add))
                ch.then(v.tensor_tensor(tab_a[:, :], tab_b[:, :], tab_a[:, :], ALU.mult))
                v.tensor_reduce(tab_r[:, :], tab_a[:, :], AX.X, ALU.add)
                ch.then(v.tensor_scalar(tab_u[:, :], tab_e[:, :], float(NEXP), float(NEXP * REG), ALU.is_ge, ALU.mult))
                v.tensor_scalar(tab_col[:, 1:2], tab_e[:, :], float(NEXP - 1), None, ALU.min)
                v.tensor_tensor(tab_col[:, 0:1], tab_r[:, :], tab_u[:, :], ALU.add).then_inc(s_tabc, 1)

            group_moments(0)
            constants()
            group_scale(0)
            dve.wait_ge(s_mapk, 16 * NKT)
            for c in range(NKT):
                n = P if c < 2 else LASTK
                ins = v.tensor_scalar(row_k[0:n, c:c + 1], map_k[0:n, c:c + 1], M - 1, None, ALU.min)
            ins.then_inc(s_rowk, 1)
            group_moments(1)
            group_moments(2)
            group_scale(1)
            dve.wait_ge(s_gath, 16 * NGT)
            moments(gathered_row, NT, NGT)
            group_scale(2)
            group_moments(3)
            refine(rstd[:, :], NT, NGT, 4)
            for i in range(NGT):
                pn = LASTK if i == NGT - 1 else P
                v.tensor_scalar(gathered_row(i), gathered_row(i), mv[0:pn, NT + i, 0:1], rstd[0:pn, i:i + 1],
                                ALU.subtract, ALU.mult).then_inc(s_gnorm, 1)
            group_scale(3)
            choose(0)
            place_tokens(0)
            dve.wait_ge(s_attw, 16 * 5)
            for c in range(NKT):
                n = P if c < 2 else LASTK
                dve.wait_ge(s_qkv, KD + c + 1)
                ch.then(v.tensor_tensor(vrow[0:n, c, :], ps_misc[(KD + c) % 3][0:n, 0:D], bv_bc[0:n, :], ALU.add))
                v.tensor_scalar(vrow[0:n, c, :], vrow[0:n, c, :], vmask[0:n, c:c + 1], None, ALU.mult).then_inc(s_vc, 1)
            dve.wait_ge(s_vm, 1)
            v.tensor_copy(vbd[:, :, :, P:VW], headmask[:, :].unsqueeze(1).unsqueeze(1)
                          .to_broadcast([P, KD, NKB, HH])).then_inc(s_vz, 1)
            low_parts(BEFORE[0])
            choose(1)
            low_parts(BEFORE[1])
            place_tokens(1)
            normalise(9)

            def key_blocks(i):
                j = TILES[i]
                if i >= 2:
                    dve.wait_ge(s_sc, i - 1)
                n, count = (NKB - 1, 1) if j == NQT else (2 * j, 2)
                for k in range(KD):
                    own = kT[:, k, n * KEYS:(n + count) * KEYS].rearrange("p (b s) -> p b s", b=count)
                    ins = v.tensor_tensor(kbd[:, i % 2, k, 0:count, :].rearrange("p b (h s) -> p b h s", h=HH),
                                          own.unsqueeze(2).to_broadcast([P, count, HH, KEYS]),
                                          headmask[:, :].unsqueeze(1).unsqueeze(3).to_broadcast([P, count, HH, KEYS]),
                                          ALU.mult)
                ins.then_inc(s_kbd, 1)

            ch.then(v.memset(sc_max[:, :, :], 0.0))
            dve.wait_ge(s_qkvc, KD)
            dve.wait_ge(s_qkv, KD + NKT)
            key_blocks(0)
            for step in range(len(TILES) + 2):
                if step < 3:
                    normalise(11 + 2 * step)
                if step + 1 < len(TILES):
                    key_blocks(step + 1)
                if step < len(TILES):
                    dve.wait_ge(s_sc, step + 1)
                    if step >= 1:
                        dve.wait_ge(s_bias, step)
                    for r, b, n in halves(TILES[step]):
                        src = ps_scores[step % 2][:, KD * b * P:KD * (b + 1) * P].rearrange("p (k n) -> p k n", k=KD)
                        ins = v.tensor_reduce(sc_max[:, :, b], src[:, :, r], AX.X, ALU.max)
                    ins.then_inc(s_max, 1)
                    dve.wait_ge(s_max, step + 1)
                    if step >= 1:
                        dve.wait_ge(s_pr, step)
                    v.tensor_scalar(sc_bias[:, :], sc_max[:, :, :].rearrange("p k b -> p (k b)"), -SCALE, None,
                                    ALU.mult).then_inc(s_bias, 1)
                low_parts(DURING[step - 1] if step >= 1 else BEFORE[2])
                if 1 <= step <= len(TILES):
                    dve.wait_ge(s_at, step)
                    got = ps_att[:, 0:KD * VW].rearrange("p (k j) -> p k j", k=KD)
                    ch.then(v.tensor_scalar(pr_sum[:, :].rearrange("p (k h) -> p k h", k=KD), got[:, :, P:VW], SUM_EPS, None,
                                            ALU.add))
                    ch.then(v.reciprocal(pr_inv[:, :], pr_sum[:, :]))
                    if step >= 2:
                        dve.wait_ge(s_att, step - 1)
                    for k in range(KD):
                        ins = v.tensor_tensor(att[:, k * HH:(k + 1) * HH, :], got[:, k, 0:P].rearrange("p (h d) -> p h d", h=HH),
                                              pr_inv[:, k * HH:(k + 1) * HH].unsqueeze(2).to_broadcast([P, HH, HD]), ALU.mult)
                    ins.then_inc(s_atn, 1)
                if step >= 2:
                    i = step - 2
                    dve.wait_ge(s_y, i + 1)
                    if i >= 2:
                        dve.wait_ge(s_zst[i % 2], 16 * (i // 2))
                    v.tensor_tensor(att_out[:, i % 2, :], ps_proj[:, 0:D], bproj_bc[:, :], ALU.add).then_inc(s_z, 1)
                if step == 3:
                    choose(2)
                if step == 4:
                    place_tokens(2)
                if step == 5:
                    choose(3)
                if step == 6:
                    place_tokens(3)
                    tile_table()
                if step == 8:
                    dve.wait_ge(s_tabp, 1)
                    v.tensor_copy(tab_row[:, :], ps_cnt[0:1, TAB0:TAB0 + NET])
                    v.tensor_copy(tab_exp[:, :], ps_cnt[0:1, TAB1:TAB1 + NET]).then_inc(s_tab, 1)

            low_parts(DURING[-1])

            def rows_low(tile, slot):
                dve.wait_ge(s_fh, tile + 1)
                v.tensor_tensor(fx_lo[slot][:, :, :], ps_rows[:, 0:D].rearrange("p (k n) -> p k n", k=KD),
                                fx_hi[slot][:, :, :].bitcast(F32), ALU.subtract).then_inc(s_fl, 1)

            def hidden_low(tile):
                for i in range(2):
                    k = slice(2 * i, 2 * i + 2)
                    dve.wait_ge(s_hh[i], tile + 1)
                    v.scalar_tensor_tensor(out=h_lo[:, k, :], in0=ps_hidT[i][:, 0:2 * P].rearrange("p (k n) -> p k n", k=2),
                                           scalar=0.0, in1=h_hi[:, k, :].bitcast(F32), op0=ALU.max,
                                           op1=ALU.subtract).then_inc(s_hl[i], 1)

            def tokens(tile, slot, rnd, reused=True):
                dve.wait_ge(s_ld[slot], 16 * rnd + 16)
                if reused:
                    dve.wait_ge(s_out[slot], 16 * rnd)
                v.tensor_copy(toki[:, slot, :], rows[slot][:, :].bitcast(I32)[:, ATT_ROW:TOKEN + 1]).then_inc(s_tok, 1)

            experts = [dve.alloc_register(f"vector_expert{i}") for i in range(SLOTS)]

            def expert(slot):
                return dve.snap(experts[slot], min_val=0, max_val=NEXP - 1)

            def load_expert(tile, slot):
                dve.reg_load(experts[slot], tab_exp[0:1, bass.ds(tile, 1)])

            def hidden_bias(tile, slot, early=False):
                e = expert(slot)
                dve.wait_ge(s_h, tile + 1)
                if not early:
                    dve.wait_ge(s_ht, tile)
                v.tensor_tensor(hb[:, :], ps_hidden[:, :], b1_bc[:, bass.ds(e, 1), :].rearrange("p a n -> p (a n)"),
                                ALU.add).then_inc(s_hb, 1)

            def finish(tile, slot, rnd, early=False):
                e = expert(slot)
                dve.wait_ge(s_fy, tile + 1)
                if early:
                    dve.wait_ge(s_b2, 16)
                else:
                    dve.wait_ge(s_fo, tile)
                v.tensor_tensor(yb[:, :], ps_out[:, 0:D], b2_bc[:, bass.ds(e, 1), :].rearrange("p a n -> p (a n)"),
                                ALU.add).then_inc(s_yb, 1)
                dve.wait_ge(s_yb, tile + 1)
                dve.wait_ge(s_zg[slot], 16 * rnd + 16)
                v.scalar_tensor_tensor(out=yo[slot][:, :], in0=yb[:, :], scalar=res[slot][:, GATE:GATE + 1],
                                       in1=res[slot][:, 0:D], op0=ALU.mult, op1=ALU.add).then_inc(s_fo, 1)

            def step(rnd, slot, first_round=False, last_round=False):
                t = rnd * SLOTS + slot
                first, last = first_round and slot == 0, last_round and slot == SLOTS - 1
                nxt, nrnd = (slot + 1) % SLOTS, rnd + (slot + 1 == SLOTS)
                if not first:
                    hidden_low(t - 1)
                if not last:
                    rows_low(t + 1, nxt)
                hidden_bias(t, slot, early=first)
                if not last:
                    load_expert(t + 1, nxt)
                if not first:
                    finish(t - 1, (slot - 1) % SLOTS, rnd - (slot == 0), early=first_round and slot == 1)
                if not last:
                    tokens(t + 1, nxt, nrnd, reused=not first_round or slot == SLOTS - 1)

            tokens(0, 0, 0, reused=False)
            rows_low(0, 0)
            dve.wait_ge(s_b1, 16)
            dve.wait_ge(s_b1_late, 16)
            load_expert(0, 0)
            for slot in range(SLOTS):
                step(0, slot, first_round=True)
            for slot in range(SLOTS):
                step(1, slot)
            with dve.Fori(1, ROUNDS // 2) as pair:
                for r in (2 * pair, 2 * pair + 1):
                    for slot in range(SLOTS):
                        step(r, slot)
            for slot in range(SLOTS):
                step(ROUNDS - 1, slot, last_round=True)
            hidden_low(NET - 1)
            finish(NET - 1, SLOTS - 1, ROUNDS - 1)

        @block.tensor
        def _(pe):
            def transpose(dst, src, n=P):
                return pe.transpose(dst, src, ident[0:n, 0:n])

            def half_transposes(h):
                if h < 8:
                    pe.wait_ge(s_xn, h + 1)
                elif h % 2 == 0:
                    pe.wait_ge(s_xn, 8 + (h - 8) // 2 + 1)
                else:
                    pe.wait_ge(s_xnv, (h - 8) // 2 + 1)
                if h >= 2:
                    pe.wait_ge(s_xtc, h - 1)
                for t in range(2):
                    for k in range(KD):
                        ins = transpose(ps_xt[h % 2][:, (t * KD + k) * P:(t * KD + k + 1) * P],
                                        xn[:, h % 2, t, k * P:(k + 1) * P])
                ins.then_inc(s_xt, 1)

            def quad_transposes(u):
                half_transposes(2 * u)
                half_transposes(2 * u + 1)

            def quad_logits(u):
                pe.wait_ge(s_xtc, 2 * u + 2)
                if u >= 1:
                    pe.wait_ge(s_ltc, u)
                for k in range(KD):
                    ins = pe.matmul(ps_lt[0:NEXP, :], wr_sb[:, k, :], xT[:, u % 2, k, :], start=(k == 0), stop=(k == KD - 1))
                ins.then_inc(s_lt, 1)

            def quad_by_token(u):
                pe.wait_ge(s_ltc, u + 1)
                if u >= 2:
                    pe.wait_ge(s_lgr, u // 2)
                if u >= 4:
                    pe.wait_ge(s_preu, 2)
                for t in range(4):
                    ins = transpose(ps_lg[:, (4 * u + t) * NEXP:(4 * u + t + 1) * NEXP],
                                    logT[:, t * P:(t + 1) * P], NEXP)
                ins.then_inc(s_lg, 1)

            def counts(g):
                pe.wait_ge(s_cnt, g + 1)
                if g >= 1:
                    pe.wait_ge(s_preu, g)
                pe.matmul(ps_cnt[:, 0:NEXP], before[:, :], cnt[:, :], start=True, stop=True)
                pe.matmul(ps_cnt[:, NEXP:2 * NEXP], ones[:, :], cnt[:, :], start=True, stop=True).then_inc(s_pre, 1)

            pe.wait_ge(s_ident, 1)
            pe.wait_ge(s_const, NCONST)
            pe.wait_ge(s_rw, 32)
            for u in range(4):
                quad_transposes(u)
                if u >= 1:
                    quad_logits(u - 1)
                if u >= 2:
                    quad_by_token(u - 2)
            quad_logits(3)
            quad_by_token(2)
            quad_by_token(3)

            for i in range(NGT):
                n = LASTK if i == NGT - 1 else P
                pe.wait_ge(s_gnorm, i + 1)
                if i >= 3:
                    pe.wait_ge(s_gtc, i - 2)
                for k in range(KD):
                    ins = transpose(ps_misc[i % 3][:, k * P:k * P + n], xg[0:n, i, k * P:(k + 1) * P], n)
                ins.then_inc(s_gt, 1)

            pe.wait_ge(s_attw, 16 * 5)
            pe.wait_ge(s_gtc, NGT)
            for c in range(KD):
                for k in range(KD):
                    ins = pe.matmul(ps_misc[c][:, 0:NKEY], wqkv_sb[:, k, D + c * P:D + (c + 1) * P], xkT[:, k, :],
                                    start=(k == 0), stop=(k == KD - 1))
                ins.then_inc(s_qkv, 1)
            counts(0)
            for c in range(NKT):
                n = P if c < 2 else LASTK
                if c >= 1:
                    pe.wait_ge(s_qkvc, c)
                for k in range(KD):
                    ins = pe.matmul(ps_misc[(KD + c) % 3][0:n, 0:D], xkT[:, k, c * P:c * P + n], wqkv_sb[:, k, 2 * D:3 * D],
                                    start=(k == 0), stop=(k == KD - 1))
                ins.then_inc(s_qkv, 1)
            for half in range(2):
                for c in range(KD):
                    if half == 0:
                        pe.wait_ge(s_vc, c + 2)
                    else:
                        pe.wait_ge(s_qkvc, KD + c + 1)
                    for k in range(KD):
                        ins = pe.matmul(ps_misc[c][:, :], wqkv_sb[:, k, c * P:(c + 1) * P],
                                        xqT[:, k, half * 512:(half + 1) * 512], start=(k == 0), stop=(k == KD - 1))
                    ins.then_inc(s_qkv, 1)
                if half == 0:
                    counts(1)
            quad_transposes(4)

            def router_step(step):
                if step < 3:
                    quad_transposes(5 + step)
                if step < 4:
                    quad_logits(4 + step)
                if step in (1, 2):
                    quad_by_token(3 + step)
                if step == 4:
                    quad_by_token(6)
                    counts(2)
                if step == 5:
                    quad_by_token(7)
                if step == 6:
                    counts(3)

            pe.wait_ge(s_qkvc, 3 * KD)
            for step in range(len(TILES) + 2):
                if step >= 2:
                    pe.wait_ge(s_atn, step - 1)
                    if step >= 3:
                        pe.wait_ge(s_z, step - 2)
                    for k in range(KD):
                        ins = transpose(ps_attT[:, k * P:(k + 1) * P],
                                        att[:, k * HH:(k + 1) * HH, :].rearrange("p h d -> p (h d)"))
                    ins.then_inc(s_att, 1)
                if step < len(TILES):
                    j = TILES[step]
                    pe.wait_ge(s_kbd, step + 1)
                    if step >= 2:
                        pe.wait_ge(s_pr, step - 1)
                    own = min(j, NQT - 1)
                    blocks = halves(j)
                    parts = len(blocks) * KD
                    mask = masked[:, P - 1:P].to_broadcast([NQT, P]) if j == NQT else masked[:, :]
                    pe.matmul(ps_scores[step % 2][:, 0:parts * P].rearrange("p (a n) -> p a n", a=parts),
                              ident_h[:, own:own + 1].to_broadcast([NQT, P]),
                              mask.unsqueeze(1).to_broadcast([NQT, parts, P]), start=True, stop=False)
                    for r, b, n in blocks:
                        for k in range(KD):
                            q = xqT[:, k, SEQ - 1:SEQ].to_broadcast([P, P]) if j == NQT else xqT[:, k, j * P:(j + 1) * P]
                            ins = pe.matmul(ps_scores[step % 2][:, (KD * b + k) * P:(KD * b + k + 1) * P],
                                            kbd[:, step % 2, k, b, :], q, start=False,
                                            stop=KD * b + k == parts - 1)
                    ins.then_inc(s_sc, 1)
                if 1 <= step <= len(TILES):
                    j = TILES[step - 1]
                    pe.wait_ge(s_pr, step)
                    if step == 1:
                        pe.wait_ge(s_vbd, 16 * HH)
                    else:
                        pe.wait_ge(s_atn, step - 1)
                    for r, b, n in halves(j):
                        for k in range(KD):
                            ins = pe.matmul(ps_att[r, k * VW:(k + 1) * VW], pr[:, (step - 1) % 2, k, r], vbd[:, k, n, :],
                                            start=True, stop=True)
                    ins.then_inc(s_at, 1)
                if step >= 2:
                    pe.wait_ge(s_atc, step - 1)
                    for k in range(KD):
                        ins = pe.matmul(ps_proj[:, 0:D], attT[:, k, :], wproj_sb[:, k, :], start=(k == 0), stop=(k == KD - 1))
                    ins.then_inc(s_y, 1)
                router_step(step)
                if step == 7:
                    pe.wait_ge(s_tabc, 1)
                    for c, at in enumerate((TAB0, TAB1)):
                        ins = pe.matmul(ps_cnt[0:1, at:at + NET], tab_col[:, c:c + 1], ident[:, 0:NET], start=True, stop=True)
                    ins.then_inc(s_tabp, 1)

            experts = [pe.alloc_register(f"tensor_expert{i}") for i in range(SLOTS)]

            def expert(slot):
                return pe.snap(experts[slot], min_val=0, max_val=NEXP - 1)

            def load_expert(tile, slot):
                pe.reg_load(experts[slot], tab_exp[0:1, bass.ds(tile, 1)])

            def weights(e, part, k, n):
                return w_sb[:, bass.ds(e, 1), part, k * n:(k + 1) * n].rearrange("p a n -> p (a n)")

            def hidden_transposes(tile, early=False):
                pe.wait_ge(s_hb, tile + 1)
                if not early:
                    pe.wait_ge(s_hl[1], tile)
                for k in range(KH):
                    ins = transpose(ps_hidT[k // 2][:, (k % 2) * P:(k % 2 + 1) * P], hb[:, k * P:(k + 1) * P])
                ins.then_inc(s_ht, 1)

            def row_transposes(tile, early=False):
                pe.wait_ge(s_fn, tile + 1)
                if not early:
                    pe.wait_ge(s_fl, tile)
                for k in range(KD):
                    ins = transpose(ps_rows[:, k * P:(k + 1) * P], fxn[:, k * P:(k + 1) * P])
                ins.then_inc(s_ft, 1)

            def hidden(tile, slot, early=False):
                e = expert(slot)
                pe.wait_ge(s_fl, tile + 1)
                if not early:
                    pe.wait_ge(s_hb, tile)
                for k in range(KD):
                    for a, part in ((fx_hi, HI1), (fx_hi, LO1), (fx_lo, HI1)):
                        ins = pe.matmul(ps_hidden[:, :], a[slot][:, k, :], weights(e, part, k, HID),
                                        start=(k == 0 and a is fx_hi and part == HI1), stop=(k == KD - 1 and a is fx_lo))
                ins.then_inc(s_h, 1)

            def expert_out(tile, slot, early=False):
                e = expert(slot)
                if not early:
                    pe.wait_ge(s_yb, tile)
                for k in range(KH):
                    if k % 2 == 0:
                        pe.wait_ge(s_hl[k // 2], tile + 1)
                    for a, part in ((h_hi, HI2), (h_hi, LO2), (h_lo, HI2)):
                        ins = pe.matmul(ps_out[:, 0:D], a[:, k, :], weights(e, part, k, D),
                                        start=(k == 0 and a is h_hi and part == HI2), stop=(k == KH - 1 and a is h_lo))
                ins.then_inc(s_fy, 1)

            def step(rnd, slot, first_round=False, last_round=False):
                t = rnd * SLOTS + slot
                first, last = first_round and slot == 0, last_round and slot == SLOTS - 1
                early = first_round and slot == 1
                if not first:
                    hidden_transposes(t - 1, early)
                if not last:
                    row_transposes(t + 1)
                hidden(t, slot, early=first)
                if not last:
                    load_expert(t + 1, (slot + 1) % SLOTS)
                if not first:
                    expert_out(t - 1, (slot - 1) % SLOTS, early)

            pe.wait_ge(s_tab, 1)
            pe.wait_ge(s_z, len(TILES))
            row_transposes(0, early=True)
            pe.wait_ge(s_wlo, NPIECE)
            load_expert(0, 0)
            for slot in range(SLOTS):
                step(0, slot, first_round=True)
            for slot in range(SLOTS):
                step(1, slot)
            with pe.Fori(1, ROUNDS // 2) as pair:
                for r in (2 * pair, 2 * pair + 1):
                    for slot in range(SLOTS):
                        step(r, slot)
            for slot in range(SLOTS):
                step(ROUNDS - 1, slot, last_round=True)
            hidden_transposes(NET - 1)
            expert_out(NET - 1, SLOTS - 1)


_INS = ["L0_attn_x", "L0_attn_Wqkv", "L0_attn_bqkv", "L0_attn_Wproj", "L0_attn_bproj", "L0_attn_mapping",
        "L0_ffn_Wr", "L0_ffn_br", "L0_ffn_W1", "L0_ffn_b1", "L0_ffn_W2", "L0_ffn_b2"]


def kernel(**inputs):
    import numpy as _np
    import concourse.bacc as _bacc
    from concourse import mybir as _mybir
    from concourse.bass_utils import run_bass_kernel_spmd as _run

    nc = _bacc.Bacc("TRN2", target_bir_lowering=False, num_devices=1)
    arrays, args = {}, []
    for name in _INS:
        a = _np.ascontiguousarray(inputs[name])
        arrays[f"in_{name}_dram"] = a
        args.append(nc.dram_tensor(f"in_{name}_dram", a.shape, _mybir.dt.from_np(a.dtype), kind="ExternalInput").ap())
    out = nc.dram_tensor("out_0_dram", (1, M, D), F32, kind="ExternalOutput").ap()
    build(nc, *args, out)
    r = _run(nc, [arrays], core_ids=[0])
    return r.results[0]["out_0_dram"]
```
